# Optimizing a Trainium2 kernel written in Bass

```python
import numpy as np
import jax
import jax.numpy as jnp

def _softmax(x, axis=-1):
    return jax.nn.softmax(x, axis=axis)

def _gelu(x):
    return jax.nn.gelu(x, approximate=True)

def _silu(x):
    return jax.nn.silu(x)

def _sigmoid(x):
    return jax.nn.sigmoid(x)

def _layernorm(x, axis=-1, eps=1e-05):
    m = jnp.mean(x, axis=axis, keepdims=True)
    v = jnp.var(x, axis=axis, keepdims=True)
    return (x - m) / jnp.sqrt(v + eps)

def _scatter_add(tgt, idx, src, axis=0):
    return tgt.at[idx].add(src)

def _segment_sum(src, seg, n):
    return jax.ops.segment_sum(src, seg, n)
kernel_name = 'mk_decoder_postln_d2_seqx_r4_c52196'

def setup_inputs(seed: int=0):
    np.random.seed(seed)
    _w = jnp.asarray

    def _rec_inputs():
        import jax
        import jax.numpy as jnp
        _rk = jax.random.key(seed)
        x = 7.22e-05 + 1 * jax.random.normal(jax.random.fold_in(_rk, 1), (16, 128, 512), jnp.float32)
        _lenS = 128 - jax.random.randint(jax.random.fold_in(_rk, 7), (16,), 0, max(1, 128 // 4) + 1, jnp.int32)
        _lenS2 = 128 - jax.random.randint(jax.random.fold_in(_rk, 8), (16,), 0, max(1, 128 // 4) + 1, jnp.int32)
        _ctx_1024P = jax.random.normal(jax.random.fold_in(_rk, 11), (16, 16, 256), jnp.float32)
        _ctx_1024c = jax.random.dirichlet(jax.random.fold_in(_rk, 511), 0.3 * jnp.ones((16,), jnp.float32), (16, 128))
        _ctx_1024t = jnp.einsum('bsk,bkd->bsd', _ctx_1024c, _ctx_1024P)
        _ctx_1024t = _ctx_1024t * jax.lax.rsqrt(jnp.mean(jnp.square(_ctx_1024t)) + 1e-12) * 0.953939
        ctx_1024 = -1.39393e-06 + 0.999914 * (_ctx_1024t + 0.3 * jax.random.normal(jax.random.fold_in(_rk, 611), (16, 128, 256), jnp.float32))
        fside_BxSx2_0 = jax.random.uniform(jax.random.fold_in(_rk, 12), (16, 128, 2), jnp.float32, 0.0, 0.999707)
        return (x, ctx_1024, fside_BxSx2_0)
    x, ctx_1024, fside_BxSx2_0 = _rec_inputs()

    def _L0_attn_setup():
        import jax, jax.numpy as jnp
        import numpy as np
        import math
        N_HEADS, D_MODEL, D_HEAD = (16, 512, 128)
        BATCH, SEQ = (4, 512)
        ROPE_THETA = 10000.0

        def _rope_cos_sin(seq_len, head_dim, dtype=jnp.float32):
            inv_freq = 1.0 / ROPE_THETA ** (jnp.arange(0, head_dim, 2, dtype=jnp.float32) / head_dim)
            m = jnp.arange(seq_len, dtype=jnp.float32)
            freqs = jnp.outer(m, inv_freq)
            return (jnp.cos(freqs).astype(dtype), jnp.sin(freqs).astype(dtype))

        def _apply_rope(x, cos, sin):
            x1 = x[..., 0::2]
            x2 = x[..., 1::2]
            cos = cos[None, :, None, :]
            sin = sin[None, :, None, :]
            r1 = x1 * cos - x2 * sin
            r2 = x1 * sin + x2 * cos
            out = jnp.stack([r1, r2], axis=-1)
            return out.reshape(x.shape)
        key = jax.random.key(seed)
        ks = jax.random.split(key, 9)
        std = 0.02
        return {'normalized_resid_pre': jax.random.normal(ks[0], (BATCH, SEQ, D_MODEL), jnp.float32), 'W_Q': jax.random.normal(ks[1], (N_HEADS, D_MODEL, D_HEAD), jnp.float32) * std, 'b_Q': jnp.zeros((N_HEADS, D_HEAD), jnp.float32), 'W_K': jax.random.normal(ks[2], (N_HEADS, D_MODEL, D_HEAD), jnp.float32) * std, 'b_K': jnp.zeros((N_HEADS, D_HEAD), jnp.float32), 'W_V': jax.random.normal(ks[3], (N_HEADS, D_MODEL, D_HEAD), jnp.float32) * std, 'b_V': jnp.zeros((N_HEADS, D_HEAD), jnp.float32), 'W_O': jax.random.normal(ks[4], (N_HEADS, D_HEAD, D_MODEL), jnp.float32) * std, 'b_O': jnp.zeros((D_MODEL,), jnp.float32)}
    _L0_attn_all = _L0_attn_setup()
    _L0_attn_in = {k: v for k, v in _L0_attn_all.items() if k in ('W_Q', 'b_Q', 'W_K', 'b_K', 'W_V', 'b_V', 'W_O', 'b_O')}
    del _L0_attn_all

    def _L0_xattn_setup():
        import jax, jax.numpy as jnp
        import numpy as np
        DIM = 512
        CTX_DIM = 256
        N_HEADS = 32
        HEAD_DIM = DIM // N_HEADS
        POS_DIM = 2
        B, N, CTXN = (2, 512, 512)
        ROPE_BASE = 10000.0

        def apply_axial_rope(x, pos):
            b, n, h, d = x.shape
            p = pos.shape[-1]
            dpa = d // p
            half = dpa // 2
            freqs = ROPE_BASE ** (-jnp.arange(half, dtype=x.dtype) / half)
            ang = pos[..., :, None] * freqs
            cos = jnp.cos(ang)[:, :, None, :, :]
            sin = jnp.sin(ang)[:, :, None, :, :]
            xr = x.reshape(b, n, h, p, half, 2)
            x1, x2 = (xr[..., 0], xr[..., 1])
            out = jnp.stack([x1 * cos - x2 * sin, x1 * sin + x2 * cos], axis=-1)
            return out.reshape(b, n, h, d)
        key = jax.random.key(seed)
        ks = jax.random.split(key, 8)
        x = jax.random.normal(ks[0], (B, N, DIM), jnp.float32)
        ctx = jax.random.normal(ks[1], (B, CTXN, CTX_DIM), jnp.float32)
        pos_map = jax.random.uniform(ks[2], (B, N, POS_DIM), jnp.float32)
        ctx_pos_map = jax.random.uniform(ks[3], (B, CTXN, POS_DIM), jnp.float32)
        Wq = jax.random.normal(ks[4], (DIM, DIM), jnp.float32) / np.sqrt(DIM)
        Wkv = jax.random.normal(ks[5], (CTX_DIM, 2 * DIM), jnp.float32) / np.sqrt(CTX_DIM)
        Wout = jax.random.normal(ks[6], (DIM, DIM), jnp.float32) / np.sqrt(DIM)
        bout = jnp.zeros((DIM,), jnp.float32)
        return {'x': x, 'ctx': ctx, 'pos_map': pos_map, 'ctx_pos_map': ctx_pos_map, 'Wq': Wq, 'Wkv': Wkv, 'Wout': Wout, 'bout': bout}
    _L0_xattn_all = _L0_xattn_setup()
    _L0_xattn_in = {k: v for k, v in _L0_xattn_all.items() if k in ('Wq', 'Wkv', 'Wout', 'bout')}
    del _L0_xattn_all

    def _L0_ffn_setup():
        import math
        import jax, jax.numpy as jnp
        import numpy as np
        from jax import lax
        D = 512
        I = 256
        E = 32
        K = 4
        NG = 8
        TKG = 3
        NSH = 2
        SCALE = 2.5
        CF = 1.25
        B, S = (2, 512)

        def _router(x, router_w, e_bias):
            scores = jax.nn.sigmoid(x @ router_w.T)
            sc = scores + e_bias[None, :]
            T = x.shape[0]
            gs = sc.reshape(T, NG, E // NG)
            group_scores = lax.top_k(gs, 2)[0].sum(-1)
            _, gidx = lax.top_k(group_scores, TKG)
            gmask = jnp.zeros((T, NG), sc.dtype).at[jnp.arange(T)[:, None], gidx].set(1.0)
            smask = jnp.repeat(gmask, E // NG, axis=1)
            masked = jnp.where(smask > 0, sc, 0.0)
            _, topk_idx = lax.top_k(masked, K)
            topk_w = jnp.take_along_axis(scores, topk_idx, axis=1)
            topk_w = topk_w / (topk_w.sum(-1, keepdims=True) + 1e-20)
            topk_w = topk_w * SCALE
            return (topk_idx.astype(jnp.int32), topk_w)

        def _moe_forward(hidden_states, router_w, e_bias, W_gate, W_up, W_down, shared_gate, shared_up, shared_down):
            b, s, d = hidden_states.shape
            T = b * s
            C = int(math.ceil(CF * T / E))
            EC = E * C
            x = hidden_states.reshape(T, d)
            topk_idx, topk_w = _router(x, router_w, e_bias)
            expert_flat = topk_idx.reshape(-1)
            w_flat = topk_w.reshape(-1)
            tok_flat = jnp.repeat(jnp.arange(T, dtype=jnp.int32), K)
            sort_ix = jnp.argsort(expert_flat)
            e_sorted = expert_flat[sort_ix]
            tok_s = tok_flat[sort_ix]
            w_s = w_flat[sort_ix]
            counts = jnp.zeros(E, jnp.int32).at[e_sorted].add(1)
            group_start = jnp.concatenate([jnp.zeros(1, jnp.int32), jnp.cumsum(counts)[:-1].astype(jnp.int32)])
            pos = jnp.arange(T * K, dtype=jnp.int32) - group_start[e_sorted]
            valid = pos < C
            dest = e_sorted * C + jnp.where(valid, pos, 0)
            slots_token = jnp.zeros(EC, jnp.int32).at[dest].add(jnp.where(valid, tok_s, 0))
            slots_w = jnp.zeros(EC, w_s.dtype).at[dest].add(jnp.where(valid, w_s, 0.0))
            Xp = x[slots_token].reshape(E, C, d)
            G = jnp.einsum('ecd,edi->eci', Xp, W_gate)
            U = jnp.einsum('ecd,edi->eci', Xp, W_up)
            Y = jnp.einsum('eci,eid->ecd', jax.nn.silu(G) * U, W_down)
            Yf = Y.reshape(EC, d) * slots_w[:, None]
            out = jnp.zeros((T, d), x.dtype).at[slots_token].add(Yf)
            shared = jax.nn.silu(x @ shared_gate.T) * (x @ shared_up.T) @ shared_down.T
            return (out + shared).reshape(b, s, d)
        key = jax.random.key(seed)
        ks = jax.random.split(key, 8)

        def rn(k, shape, scale=0.02):
            return jax.random.normal(k, shape, jnp.float32) * scale
        return {'hidden_states': jax.random.normal(ks[0], (B, S, D), jnp.float32), 'router_w': rn(ks[1], (E, D)), 'e_bias': jnp.zeros((E,), jnp.float32), 'W_gate': rn(ks[2], (E, D, I)), 'W_up': rn(ks[3], (E, D, I)), 'W_down': rn(ks[4], (E, I, D)), 'shared_gate': rn(ks[5], (I * NSH, D)), 'shared_up': rn(ks[6], (I * NSH, D)), 'shared_down': rn(ks[7], (D, I * NSH))}
    _L0_ffn_all = _L0_ffn_setup()
    _L0_ffn_in = {k: v for k, v in _L0_ffn_all.items() if k in ('router_w', 'e_bias', 'W_gate', 'W_up', 'W_down', 'shared_gate', 'shared_up', 'shared_down')}
    del _L0_ffn_all

    def _L1_attn_setup():
        import jax, jax.numpy as jnp
        import numpy as np
        L, N, E, H = (512, 2, 512, 16)
        DH = E // H
        SCALE = DH ** (-0.5)
        key = jax.random.key(seed)
        k1, k2, k3 = jax.random.split(key, 3)
        x = jax.random.normal(k1, (L, N, E), dtype=jnp.float32)
        weight_qkv = jax.random.normal(k2, (3 * E, E), dtype=jnp.float32) * 0.02
        weight_out = jax.random.normal(k3, (E, E), dtype=jnp.float32) * 0.02
        return {'x': x, 'weight_qkv': weight_qkv, 'weight_out': weight_out}
    _L1_attn_all = _L1_attn_setup()
    _L1_attn_in = {k: v for k, v in _L1_attn_all.items() if k in ('weight_qkv', 'weight_out')}
    del _L1_attn_all

    def _L1_xattn_setup():
        import jax, jax.numpy as jnp
        import numpy as np
        EPS = 1e-05

        def rmsnorm(x, g, eps=EPS):
            var = jnp.mean(jnp.square(x), axis=-1, keepdims=True)
            return x * jax.lax.rsqrt(var + eps) * g
        key = jax.random.key(seed)
        ks = jax.random.split(key, 8)
        B, Sq, Skv = (2, 1024, 128)
        dim, cdim, H, D = (512, 256, 16, 128)
        inner = H * D
        s = lambda f: 1.0 / np.sqrt(f)
        return {'hidden_states': jax.random.normal(ks[0], (B, Sq, dim), jnp.float32), 'encoder_hidden_states': jax.random.normal(ks[1], (B, Skv, cdim), jnp.float32), 'Wq': jax.random.normal(ks[2], (dim, inner), jnp.float32) * s(dim), 'Wk': jax.random.normal(ks[3], (cdim, inner), jnp.float32) * s(cdim), 'Wv': jax.random.normal(ks[4], (cdim, inner), jnp.float32) * s(cdim), 'Wo': jax.random.normal(ks[5], (inner, dim), jnp.float32) * s(inner), 'gq': jnp.ones((D,), jnp.float32), 'gk': jnp.ones((D,), jnp.float32)}
    _L1_xattn_all = _L1_xattn_setup()
    _L1_xattn_in = {k: v for k, v in _L1_xattn_all.items() if k in ('Wq', 'Wk', 'Wv', 'Wo', 'gq', 'gk')}
    del _L1_xattn_all

    def _L1_ffn_setup():
        import jax, jax.numpy as jnp
        import numpy as np
        B, T, D = (1, 256, 512)
        F_DIM = 352
        E = 8
        TOPK = 2
        key = jax.random.key(seed)
        ks = jax.random.split(key, 5)
        x = jax.random.normal(ks[0], (B, T, D), dtype=jnp.float32)
        gate_w = jax.random.normal(ks[1], (E, D), dtype=jnp.float32) * 0.02
        gate_proj = jax.random.normal(ks[2], (E, F_DIM, D), dtype=jnp.float32) * 0.02
        up_proj = jax.random.normal(ks[3], (E, F_DIM, D), dtype=jnp.float32) * 0.02
        down_proj = jax.random.normal(ks[4], (E, D, F_DIM), dtype=jnp.float32) * 0.02
        return {'x': x, 'gate_w': gate_w, 'gate_proj': gate_proj, 'up_proj': up_proj, 'down_proj': down_proj}
    _L1_ffn_all = _L1_ffn_setup()
    _L1_ffn_in = {k: v for k, v in _L1_ffn_all.items() if k in ('gate_w', 'gate_proj', 'up_proj', 'down_proj')}
    del _L1_ffn_all
    return {'x': x, 'ctx_1024': ctx_1024, 'fside_BxSx2_0': fside_BxSx2_0, 'L0_attn_W_Q': _L0_attn_in['W_Q'], 'L0_attn_b_Q': _L0_attn_in['b_Q'], 'L0_attn_W_K': _L0_attn_in['W_K'], 'L0_attn_b_K': _L0_attn_in['b_K'], 'L0_attn_W_V': _L0_attn_in['W_V'], 'L0_attn_b_V': _L0_attn_in['b_V'], 'L0_attn_W_O': _L0_attn_in['W_O'], 'L0_attn_b_O': _L0_attn_in['b_O'], 'L0_xattn_Wq': _L0_xattn_in['Wq'], 'L0_xattn_Wkv': _L0_xattn_in['Wkv'], 'L0_xattn_Wout': _L0_xattn_in['Wout'], 'L0_xattn_bout': _L0_xattn_in['bout'], 'L0_ffn_router_w': _L0_ffn_in['router_w'], 'L0_ffn_e_bias': _L0_ffn_in['e_bias'], 'L0_ffn_W_gate': _L0_ffn_in['W_gate'], 'L0_ffn_W_up': _L0_ffn_in['W_up'], 'L0_ffn_W_down': _L0_ffn_in['W_down'], 'L0_ffn_shared_gate': _L0_ffn_in['shared_gate'], 'L0_ffn_shared_up': _L0_ffn_in['shared_up'], 'L0_ffn_shared_down': _L0_ffn_in['shared_down'], 'L1_attn_weight_qkv': _L1_attn_in['weight_qkv'], 'L1_attn_weight_out': _L1_attn_in['weight_out'], 'L1_xattn_Wq': _L1_xattn_in['Wq'], 'L1_xattn_Wk': _L1_xattn_in['Wk'], 'L1_xattn_Wv': _L1_xattn_in['Wv'], 'L1_xattn_Wo': _L1_xattn_in['Wo'], 'L1_xattn_gq': _L1_xattn_in['gq'], 'L1_xattn_gk': _L1_xattn_in['gk'], 'L1_ffn_gate_w': _L1_ffn_in['gate_w'], 'L1_ffn_gate_proj': _L1_ffn_in['gate_proj'], 'L1_ffn_up_proj': _L1_ffn_in['up_proj'], 'L1_ffn_down_proj': _L1_ffn_in['down_proj']}

def reference(x, ctx_1024, fside_BxSx2_0, L0_attn_W_Q, L0_attn_b_Q, L0_attn_W_K, L0_attn_b_K, L0_attn_W_V, L0_attn_b_V, L0_attn_W_O, L0_attn_b_O, L0_xattn_Wq, L0_xattn_Wkv, L0_xattn_Wout, L0_xattn_bout, L0_ffn_router_w, L0_ffn_e_bias, L0_ffn_W_gate, L0_ffn_W_up, L0_ffn_W_down, L0_ffn_shared_gate, L0_ffn_shared_up, L0_ffn_shared_down, L1_attn_weight_qkv, L1_attn_weight_out, L1_xattn_Wq, L1_xattn_Wk, L1_xattn_Wv, L1_xattn_Wo, L1_xattn_gq, L1_xattn_gk, L1_ffn_gate_w, L1_ffn_gate_proj, L1_ffn_up_proj, L1_ffn_down_proj):
    import jax
    import jax.numpy as jnp

    def _L0_attn_ref(normalized_resid_pre, W_Q, b_Q, W_K, b_K, W_V, b_V, W_O, b_O):
        import jax, jax.numpy as jnp
        import numpy as np
        import math
        N_HEADS, D_MODEL, D_HEAD = (16, 512, 128)
        BATCH, SEQ = (4, 512)
        ROPE_THETA = 10000.0

        def _rope_cos_sin(seq_len, head_dim, dtype=jnp.float32):
            inv_freq = 1.0 / ROPE_THETA ** (jnp.arange(0, head_dim, 2, dtype=jnp.float32) / head_dim)
            m = jnp.arange(seq_len, dtype=jnp.float32)
            freqs = jnp.outer(m, inv_freq)
            return (jnp.cos(freqs).astype(dtype), jnp.sin(freqs).astype(dtype))

        def _apply_rope(x, cos, sin):
            x1 = x[..., 0::2]
            x2 = x[..., 1::2]
            cos = cos[None, :, None, :]
            sin = sin[None, :, None, :]
            r1 = x1 * cos - x2 * sin
            r2 = x1 * sin + x2 * cos
            out = jnp.stack([r1, r2], axis=-1)
            return out.reshape(x.shape)
        x = normalized_resid_pre
        T = x.shape[1]
        d_head = W_Q.shape[-1]
        Q = jnp.einsum('btc,ncd->btnd', x, W_Q) + b_Q
        K = jnp.einsum('btc,ncd->btnd', x, W_K) + b_K
        V = jnp.einsum('btc,ncd->btnd', x, W_V) + b_V
        cos, sin = _rope_cos_sin(T, d_head, x.dtype)
        Q = _apply_rope(Q, cos, sin)
        K = _apply_rope(K, cos, sin)
        scores = jnp.einsum('bqnd,bknd->bnqk', Q, K) / math.sqrt(d_head)
        causal = jnp.tril(jnp.ones((T, T), dtype=bool))
        scores = jnp.where(causal[None, None], scores, -jnp.inf)
        probs = jax.nn.softmax(scores, axis=-1)
        z = jnp.einsum('bnqk,bknd->bqnd', probs, V)
        out = jnp.einsum('bqnd,ndm->bqm', z, W_O) + b_O
        return out

    def _L0_xattn_ref(x, ctx, pos_map, ctx_pos_map, Wq, Wkv, Wout, bout):
        import jax, jax.numpy as jnp
        import numpy as np
        DIM = 512
        CTX_DIM = 256
        N_HEADS = 32
        HEAD_DIM = DIM // N_HEADS
        POS_DIM = 2
        B, N, CTXN = (2, 512, 512)
        ROPE_BASE = 10000.0

        def apply_axial_rope(x, pos):
            b, n, h, d = x.shape
            p = pos.shape[-1]
            dpa = d // p
            half = dpa // 2
            freqs = ROPE_BASE ** (-jnp.arange(half, dtype=x.dtype) / half)
            ang = pos[..., :, None] * freqs
            cos = jnp.cos(ang)[:, :, None, :, :]
            sin = jnp.sin(ang)[:, :, None, :, :]
            xr = x.reshape(b, n, h, p, half, 2)
            x1, x2 = (xr[..., 0], xr[..., 1])
            out = jnp.stack([x1 * cos - x2 * sin, x1 * sin + x2 * cos], axis=-1)
            return out.reshape(b, n, h, d)
        b, n, _ = x.shape
        ctx_n = ctx.shape[1]
        q = (x @ Wq).reshape(b, n, N_HEADS, HEAD_DIM)
        k, v = jnp.split(ctx @ Wkv, 2, axis=-1)
        k = k.reshape(b, ctx_n, N_HEADS, HEAD_DIM)
        v = v.reshape(b, ctx_n, N_HEADS, HEAD_DIM)
        q = apply_axial_rope(q, pos_map)
        k = apply_axial_rope(k, ctx_pos_map)
        scale = 1.0 / np.sqrt(HEAD_DIM).astype(np.float32)
        logits = jnp.einsum('bqhd,bkhd->bhqk', q, k) * scale
        w = jax.nn.softmax(logits, axis=-1)
        attn = jnp.einsum('bhqk,bkhd->bqhd', w, v)
        attn = attn.reshape(b, n, N_HEADS * HEAD_DIM)
        return attn @ Wout + bout

    def _L0_ffn_ref(hidden_states, router_w, e_bias, W_gate, W_up, W_down, shared_gate, shared_up, shared_down):
        import math
        import jax, jax.numpy as jnp
        import numpy as np
        from jax import lax
        D = 512
        I = 256
        E = 32
        K = 4
        NG = 8
        TKG = 3
        NSH = 2
        SCALE = 2.5
        CF = 1.25
        B, S = (2, 512)

        def _router(x, router_w, e_bias):
            scores = jax.nn.sigmoid(x @ router_w.T)
            sc = scores + e_bias[None, :]
            T = x.shape[0]
            gs = sc.reshape(T, NG, E // NG)
            group_scores = lax.top_k(gs, 2)[0].sum(-1)
            _, gidx = lax.top_k(group_scores, TKG)
            gmask = jnp.zeros((T, NG), sc.dtype).at[jnp.arange(T)[:, None], gidx].set(1.0)
            smask = jnp.repeat(gmask, E // NG, axis=1)
            masked = jnp.where(smask > 0, sc, 0.0)
            _, topk_idx = lax.top_k(masked, K)
            topk_w = jnp.take_along_axis(scores, topk_idx, axis=1)
            topk_w = topk_w / (topk_w.sum(-1, keepdims=True) + 1e-20)
            topk_w = topk_w * SCALE
            return (topk_idx.astype(jnp.int32), topk_w)

        def _moe_forward(hidden_states, router_w, e_bias, W_gate, W_up, W_down, shared_gate, shared_up, shared_down):
            b, s, d = hidden_states.shape
            T = b * s
            C = int(math.ceil(CF * T / E))
            EC = E * C
            x = hidden_states.reshape(T, d)
            topk_idx, topk_w = _router(x, router_w, e_bias)
            expert_flat = topk_idx.reshape(-1)
            w_flat = topk_w.reshape(-1)
            tok_flat = jnp.repeat(jnp.arange(T, dtype=jnp.int32), K)
            sort_ix = jnp.argsort(expert_flat)
            e_sorted = expert_flat[sort_ix]
            tok_s = tok_flat[sort_ix]
            w_s = w_flat[sort_ix]
            counts = jnp.zeros(E, jnp.int32).at[e_sorted].add(1)
            group_start = jnp.concatenate([jnp.zeros(1, jnp.int32), jnp.cumsum(counts)[:-1].astype(jnp.int32)])
            pos = jnp.arange(T * K, dtype=jnp.int32) - group_start[e_sorted]
            valid = pos < C
            dest = e_sorted * C + jnp.where(valid, pos, 0)
            slots_token = jnp.zeros(EC, jnp.int32).at[dest].add(jnp.where(valid, tok_s, 0))
            slots_w = jnp.zeros(EC, w_s.dtype).at[dest].add(jnp.where(valid, w_s, 0.0))
            Xp = x[slots_token].reshape(E, C, d)
            G = jnp.einsum('ecd,edi->eci', Xp, W_gate)
            U = jnp.einsum('ecd,edi->eci', Xp, W_up)
            Y = jnp.einsum('eci,eid->ecd', jax.nn.silu(G) * U, W_down)
            Yf = Y.reshape(EC, d) * slots_w[:, None]
            out = jnp.zeros((T, d), x.dtype).at[slots_token].add(Yf)
            shared = jax.nn.silu(x @ shared_gate.T) * (x @ shared_up.T) @ shared_down.T
            return (out + shared).reshape(b, s, d)
        return _moe_forward(hidden_states, router_w, e_bias, W_gate, W_up, W_down, shared_gate, shared_up, shared_down)

    def _L1_attn_ref(x, weight_qkv, weight_out):
        import jax, jax.numpy as jnp
        import numpy as np
        L, N, E, H = (512, 2, 512, 16)
        DH = E // H
        SCALE = DH ** (-0.5)
        l, n, e = x.shape
        h, dh = (H, DH)
        qkv = jnp.einsum('lne,fe->lnf', x, weight_qkv)
        q, k, v = jnp.split(qkv, 3, axis=-1)
        q = q.reshape(l, n, h, dh) * jnp.asarray(SCALE, x.dtype)
        k = k.reshape(l, n, h, dh)
        v = v.reshape(l, n, h, dh)
        attn = jnp.einsum('lnhd,mnhd->nhlm', q, k)
        causal = jnp.tril(jnp.ones((l, l), dtype=bool))
        attn = jnp.where(causal, attn, jnp.asarray(-jnp.inf, attn.dtype))
        attn = jax.nn.softmax(attn, axis=-1)
        out = jnp.einsum('nhlm,mnhd->lnhd', attn, v).reshape(l, n, e)
        return jnp.einsum('lne,fe->lnf', out, weight_out)

    def _L1_xattn_ref(hidden_states, encoder_hidden_states, Wq, Wk, Wv, Wo, gq, gk):
        import jax, jax.numpy as jnp
        import numpy as np
        EPS = 1e-05

        def rmsnorm(x, g, eps=EPS):
            var = jnp.mean(jnp.square(x), axis=-1, keepdims=True)
            return x * jax.lax.rsqrt(var + eps) * g
        B, Sq, _ = hidden_states.shape
        Skv = encoder_hidden_states.shape[1]
        D = gq.shape[0]
        H = Wq.shape[1] // D
        scale = 1.0 / np.sqrt(D)
        q = (hidden_states @ Wq).reshape(B, Sq, H, D)
        k = (encoder_hidden_states @ Wk).reshape(B, Skv, H, D)
        v = (encoder_hidden_states @ Wv).reshape(B, Skv, H, D)
        q = rmsnorm(q, gq)
        k = rmsnorm(k, gk)
        scores = jnp.einsum('bqhd,bkhd->bhqk', q, k) * scale
        attn = jax.nn.softmax(scores, axis=-1)
        out = jnp.einsum('bhqk,bkhd->bqhd', attn, v)
        out = out.reshape(B, Sq, H * D)
        return out @ Wo

    def _L1_ffn_ref(x, gate_w, gate_proj, up_proj, down_proj):
        import jax, jax.numpy as jnp
        import numpy as np
        B, T, D = (1, 256, 512)
        F_DIM = 352
        E = 8
        TOPK = 2
        b, t, d = x.shape
        x_flat = x.reshape(-1, d)
        n = x_flat.shape[0]
        router_logits = x_flat @ gate_w.T
        top_w, sel = jax.lax.top_k(router_logits, TOPK)
        top_w = jax.nn.softmax(top_w, axis=-1)
        tok_ids = jnp.arange(n)[:, None]
        tw = jnp.zeros((n, E), dtype=x.dtype).at[tok_ids, sel].add(top_w)
        g = jnp.einsum('nd,efd->enf', x_flat, gate_proj)
        u = jnp.einsum('nd,efd->enf', x_flat, up_proj)
        h = jax.nn.silu(g) * u
        eo = jnp.einsum('enf,edf->end', h, down_proj)
        out = jnp.einsum('end,ne->nd', eo, tw)
        return out.reshape(b, t, d)
    x = _layernorm(x + _L0_attn_ref(x, L0_attn_W_Q, L0_attn_b_Q, L0_attn_W_K, L0_attn_b_K, L0_attn_W_V, L0_attn_b_V, L0_attn_W_O, L0_attn_b_O), axis=-1)
    x = _layernorm(x + _L0_xattn_ref(x, ctx_1024, fside_BxSx2_0, fside_BxSx2_0, L0_xattn_Wq, L0_xattn_Wkv, L0_xattn_Wout, L0_xattn_bout), axis=-1)
    x = _layernorm(x + _L0_ffn_ref(x, L0_ffn_router_w, L0_ffn_e_bias, L0_ffn_W_gate, L0_ffn_W_up, L0_ffn_W_down, L0_ffn_shared_gate, L0_ffn_shared_up, L0_ffn_shared_down), axis=-1)
    x = _layernorm(x + _L1_attn_ref(x, L1_attn_weight_qkv, L1_attn_weight_out), axis=-1)
    x = _layernorm(x + _L1_xattn_ref(x, ctx_1024, L1_xattn_Wq, L1_xattn_Wk, L1_xattn_Wv, L1_xattn_Wo, L1_xattn_gq, L1_xattn_gk), axis=-1)
    x = _layernorm(x + _L1_ffn_ref(x, L1_ffn_gate_w, L1_ffn_gate_proj, L1_ffn_up_proj, L1_ffn_down_proj), axis=-1)
    return x

_drawn_inputs = setup_inputs


def setup_inputs(seed=0):
    import zlib

    import numpy as np

    out = dict(_drawn_inputs(seed))
    spreads = {'L0_attn_b_Q': (0.0, 0.8),
     'L0_attn_b_K': (0.0, 0.8),
     'L0_attn_b_V': (0.0, 0.1),
     'L0_attn_b_O': (0.0, 0.1),
     'L0_xattn_bout': (0.0, 0.1),
     'L0_ffn_e_bias': (0.0, 0.36),
     'L1_xattn_gq': (1.0, 0.2),
     'L1_xattn_gk': (1.0, 0.2)}
    factors = {'L0_attn_W_Q': 4.535,
     'L0_attn_W_K': 4.438,
     'L0_ffn_router_w': 3.212,
     'L0_ffn_W_gate': 3.078,
     'L0_ffn_W_up': 3.024,
     'L0_ffn_W_down': 3.019}
    for name, (base, spread) in spreads.items():
        noise = np.random.default_rng([zlib.crc32(name.encode()), seed]).standard_normal(out[name].shape)
        drawn = base * np.exp(spread * noise) if base else spread * noise
        out[name] = jnp.asarray(drawn.astype(out[name].dtype))
    for name, factor in factors.items():
        out[name] = (out[name] * factor).astype(out[name].dtype)
    return out
```

```python
from contextlib import ExitStack

import numpy as np

import concourse.bass as bass
from concourse import mybir
from concourse.alu_op_type import AluOpType

F32 = mybir.dt.float32
I32 = mybir.dt.int32
U32 = mybir.dt.uint32
ALU = mybir.AluOpType
ACT = mybir.ActivationFunctionType
AX = mybir.AxisListType

P = 128
D = 512
C = D // P
B = 16
EPS = 1e-5
LEAD = 4
NEG = -1e30


def done(n):
    return n + 1 + LEAD


def landed(n):
    return 16 * (n + 1)


class Stage:

    def __init__(self, nc, ctx, name):
        self.nc, self.ctx, self.name, self.used = nc, ctx, name, []
        ctx.callback(self.clear)

    def clear(self):
        if self.used:
            self.nc.clear_and_free_semaphores(self.used)
            self.nc.all_engine_barrier()

    def sbuf(self, name, shape, dt=F32):
        return self.ctx.enter_context(self.nc.sbuf_tensor(f"{self.name}_{name}", shape, dt))

    def sem(self, name):
        self.used.append(self.nc.alloc_semaphore(f"{self.name}_{name}"))
        return self.used[-1]

    def sems(self, *names):
        return [self.sem(n) for n in names]


def head_start(engine, *sems):
    for s in sems:
        engine.sem_inc(s, LEAD)


def carry_wait(engine, still):
    engine.memset(still[:], 0.0)


def heads(ap, n):
    return ap.rearrange("p (h d) -> p h d", h=n)


def wide_attention(nc, name, psum, ident, x_src, x_dst, w_dram, rope=None, rms=None):
    G, H = 4, 4
    KC = C if rope else w_dram["ctxT"].shape[2]
    with ExitStack() as ctx:
        st = Stage(nc, ctx, name)
        pQ, pK, pV, pA, pB, pS, pP, pO = psum

        wq = st.sbuf("wq", [P, C, G * D])
        wk = st.sbuf("wk", [P, KC, G * D])
        wv = st.sbuf("wv", [P, KC, G * D])
        wo = st.sbuf("wo", [P, G * H, D])
        xin = st.sbuf("xin", [P, D])
        xres = st.sbuf("xres", [P, D])
        xT = st.sbuf("xT", [P, C, P])
        tq = st.sbuf("tq", [P, D])
        tk = st.sbuf("tk", [P, D])
        sq = st.sbuf("sq", [P, D])
        sk = st.sbuf("sk", [P, D])
        kr = st.sbuf("kr", [P, D])
        qT = st.sbuf("qT", [P, H, P])
        kT = st.sbuf("kT", [P, H, P])
        v = st.sbuf("v", [P, 2, D])
        prob = st.sbuf("prob", [P, H, P])
        probT = st.sbuf("probT", [P, H, P])
        zn = st.sbuf("zn", [P, D])
        zT = st.sbuf("zT", [P, H, P])
        y = st.sbuf("y", [P, D])
        yn = st.sbuf("yn", [P, D])
        stats = st.sbuf("stats", [P, 6])
        mv = st.sbuf("mv", [P, 2])
        rstd = st.sbuf("rstd", [P, 1])
        mhalf = st.sbuf("mhalf", [P, H])
        eps = st.sbuf("eps", [P, 1])
        still = st.sbuf("still", [P, 1])
        nmax = st.sbuf("nmax", [P, H])
        rsum = st.sbuf("rsum", [P, H])
        rinv = st.sbuf("rinv", [P, H])
        if rope:
            qr = st.sbuf("qr", [P, D])
            sm = st.sbuf("sm", [P, H, P])
            bias = {n: st.sbuf("b" + n, [P, G * D]) for n in "qkv"}
            bo = st.sbuf("bo", [P, D])
            tab = {n: st.sbuf(n, [P, P]) for n in ("cosq", "sinq", "cosk", "sink", "mask")}
            srcT = xT
        else:
            qr = tq
            srcT = st.sbuf("ctxT", [P, KC, P])
            g2 = st.sbuf("g2", [P, 2, P])
            gg = st.sbuf("gg", [P, P])
            ssq = st.sbuf("ssq", [P, H])
            ssk = st.sbuf("ssk", [P, H])
            rq = st.sbuf("rq", [P, 2, H])
            rk = st.sbuf("rk", [P, H])
            nb = st.sbuf("nb", [P, H])
            epsn = st.sbuf("epsn", [P, H])

        c_in, x_in, r_in, ctx_in, out_st = st.sems("c_in", "x_in", "r_in", "ctx_in", "out_st")
        w_in, wo_in = ([st.sem(f"{n}{g}") for g in range(G)] for n in ("w_in", "wo_in"))
        pe_x, pe_q, pe_k, pe_v = st.sems("pe_x", "pe_q", "pe_k", "pe_v")
        pe_qt, pe_kt, pe_s, pe_pt, pe_z, pe_zt, pe_o = st.sems("pe_qt", "pe_kt", "pe_s", "pe_pt", "pe_z", "pe_zt", "pe_o")
        act_x, act_qt, act_kt, act_e, act_zt, act_pt = st.sems("act_x", "act_qt", "act_kt", "act_e", "act_zt", "act_pt")
        v_tq, v_tk, v_q, v_k, v_v = st.sems("v_tq", "v_tk", "v_q", "v_k", "v_v")
        v_aq, v_ak, v_sm, v_nm, v_nb, v_ri, v_z = st.sems("v_aq", "v_ak", "v_sm", "v_nm", "v_nb", "v_ri", "v_z")
        v_y, v_st, v_mv, v_yn = st.sems("v_y", "v_st", "v_mv", "v_yn")
        g_q, g_k, g_mq, g_mk, g_rq, g_rk, g_x, g_c, g_ve, g_rs = st.sems(
            "g_q", "g_k", "g_mq", "g_mk", "g_rq", "g_rk", "g_x", "g_c", "g_ve", "g_rs")

        n_const = 9 if rope else 2
        block = ctx.enter_context(nc.Block())

        @block.sync
        def _(sp):
            sp.sem_inc(out_st, 16)
            sp.dma_start(xin[:], x_src[0]).then_inc(x_in, 16)
            if rms:
                sp.dma_start(srcT[:], w_dram["ctxT"][:, 0]).then_inc(ctx_in, 16)
            for g in range(G):
                cols = slice(D * g, D * g + D)
                for t, n in ((wq, "wq"), (wk, "wk"), (wv, "wv")):
                    sp.dma_start(t[:, :, cols], w_dram[n][:, :, cols]).then_inc(w_in[g], 16)
                sp.dma_start(wo[:, H * g:H * g + H], w_dram["wo"][:, H * g:H * g + H]).then_inc(wo_in[g], 16)
                if g == 0:
                    sp.dma_start(xres[:], x_src[0]).then_inc(r_in, 16)

            def next_tiles(b):
                sp.wait_ge(pe_x, done(b))
                sp.dma_start(xin[:], x_src[b + 1]).then_inc(x_in, 16)
                if rms:
                    sp.wait_ge(pe_v, done(4 * b + 3))
                    sp.dma_start(srcT[:], w_dram["ctxT"][:, b + 1]).then_inc(ctx_in, 16)
                sp.wait_ge(v_y, done(b))
                sp.dma_start(xres[:], x_src[b + 1]).then_inc(r_in, 16)

            def store(b):
                sp.wait_ge(v_yn, done(b))
                sp.dma_start(x_dst[b], yn[:]).then_inc(out_st, 16)

            with sp.Fori(0, B - 1) as b:
                next_tiles(b)
                store(b)
            store(B - 1)
            sp.wait_ge(out_st, landed(B))

        @block.scalar
        def _(act):
            head_start(act, act_x, act_qt, act_kt, act_e, act_zt, act_pt)
            if rope:
                for n in "qkv":
                    act.dma_start(bias[n][:], w_dram["b" + n].partition_broadcast(P)).then_inc(c_in, 16)
                act.dma_start(bo[:], w_dram["bo"].partition_broadcast(P)).then_inc(c_in, 16)
                for n in tab:
                    act.dma_start(tab[n][:], w_dram[n]).then_inc(c_in, 16)
            else:
                act.dma_start(g2[:, 0, :], w_dram["gq"].partition_broadcast(P)).then_inc(c_in, 16)
                act.dma_start(g2[:, 1, :], w_dram["gk"].partition_broadcast(P)).then_inc(c_in, 16)

            def take_x(b):
                act.wait_ge(pe_x, done(b))
                nc.scalar.copy(xT[:], pP[:, :]).then_inc(act_x, 1)

            def take_prob_z(u):
                act.wait_ge(pe_zt, done(u))
                nc.scalar.copy(zT[:], pB[:, :]).then_inc(act_zt, 1)

            def slot(b, g, project=True, back=True):
                u = 4 * b + g
                act.wait_ge(pe_qt, done(u))
                nc.scalar.copy(qT[:], pA[:, :]).then_inc(act_qt, 1)
                act.wait_ge(pe_kt, done(u))
                nc.scalar.copy(kT[:], pB[:, :]).then_inc(act_kt, 1)
                if project and g == G - 1:
                    take_x(b + 1)
                if rope:
                    act.wait_ge(v_nm, done(u))
                    for j in range(H):
                        last = nc.scalar.activation(prob[:, j, :], sm[:, j, :], ACT.Exp, bias=nmax[:, j:j + 1],
                                                    accum_out=rsum[:, j:j + 1])
                else:
                    act.wait_ge(v_nb, done(u))
                    for j in range(H):
                        last = nc.scalar.activation(prob[:, j, :], pS[:, P * j:P * j + P], ACT.Exp,
                                                    bias=nb[:, j:j + 1], scale=rq[:, g % 2, j:j + 1],
                                                    accum_out=rsum[:, j:j + 1])
                last.then_inc(act_e, 1)
                if back:
                    take_prob_z(u - 1)
                act.wait_ge(pe_pt, done(u))
                nc.scalar.copy(probT[:], pP[:, :]).then_inc(act_pt, 1)

            take_x(0)
            slot(0, 0, back=False)
            with act.Fori(0, B - 1) as b:
                for g in range(1, G):
                    slot(b, g)
                slot(b + 1, 0)
            for g in range(1, G):
                slot(B - 1, g, project=g < G - 1)
            take_prob_z(G * B - 1)

        @block.gpsimd
        def _(pool):
            head_start(pool, g_q, g_k, g_mq, g_mk, g_rq, g_rk, g_x, g_ve, g_rs)
            nc.gpsimd.memset(mhalf[:], -0.5).then_inc(g_c, 1)
            nc.gpsimd.memset(eps[:], EPS).then_inc(g_c, 1)
            pool.wait_ge(g_c, 2)
            pool.wait_ge(c_in, 16 * n_const)
            if rms:
                nc.gpsimd.memset(epsn[:], EPS * P).then_inc(g_c, 1)
                nc.gpsimd.tensor_tensor(gg[:], g2[:, 0, :], g2[:, 1, :], ALU.mult).then_inc(g_c, 1)
                pool.wait_ge(g_c, 4)
                nc.gpsimd.tensor_scalar(gg[:], gg[:], float(np.sqrt(P)), 0.0, ALU.mult, ALU.add).then_inc(g_c, 1)

            def turned(out, t, sin):
                for half in range(2):
                    o = heads(out[:], H)[:, :, 64 * half:64 * half + 64]
                    i = heads(t[:], H)[:, :, 64 - 64 * half:128 - 64 * half]
                    s = tab[sin][:, 64 * half:64 * half + 64].unsqueeze(1).to_broadcast([P, H, 64])
                    last = nc.gpsimd.tensor_tensor(o, i, s, ALU.mult)
                return last

            def project(u, par):
                pool.wait_ge(v_tq, done(u))
                if rope:
                    pool.wait_ge(v_q, done(u - 1))
                    turned(sq, tq, "sinq").then_inc(g_q, 1)
                    pool.wait_ge(v_tk, done(u))
                    pool.wait_ge(v_k, done(u - 1))
                    turned(sk, tk, "sink").then_inc(g_k, 1)
                    return
                nc.gpsimd.tensor_tensor(sq[:], tq[:], tq[:], ALU.mult).then_inc(g_q, 1)
                pool.wait_ge(v_tk, done(u))
                nc.gpsimd.tensor_tensor(sk[:], tk[:], tk[:], ALU.mult).then_inc(g_k, 1)
                pool.wait_ge(v_aq, done(u))
                nc.gpsimd.tensor_tensor(rq[:, par, :], ssq[:], epsn[:], ALU.add).then_inc(g_mq, 1)
                pool.wait_ge(g_mq, done(u))
                nc.gpsimd.tensor_tensor(rq[:, par, :], rq[:, par, :], mhalf[:], ALU.pow).then_inc(g_rq, 1)
                pool.wait_ge(v_ak, done(u))
                nc.gpsimd.tensor_tensor(rk[:], ssk[:], epsn[:], ALU.add).then_inc(g_mk, 1)
                pool.wait_ge(g_mk, done(u))
                nc.gpsimd.tensor_tensor(rk[:], rk[:], mhalf[:], ALU.pow).then_inc(g_rk, 1)

            def residual(b):
                if rope:
                    pool.wait_ge(r_in, landed(b))
                    nc.gpsimd.tensor_tensor(xres[:], xres[:], bo[:], ALU.add).then_inc(g_x, 1)

            def norm(b):
                pool.wait_ge(v_mv, done(b))
                nc.gpsimd.tensor_tensor(rstd[:], mv[:, 1:2], eps[:], ALU.add).then_inc(g_ve, 1)
                pool.wait_ge(g_ve, done(b))
                nc.gpsimd.tensor_tensor(rstd[:], rstd[:], mhalf[:, 0:1], ALU.pow).then_inc(g_rs, 1)

            project(0, 0)
            residual(0)
            project(1, 1)
            with pool.Fori(0, B - 1) as b:
                for n in range(2, 6):
                    project(4 * b + n, n % 2)
                norm(b)
                residual(b + 1)
            project(4 * B - 2, 0)
            project(4 * B - 1, 1)
            norm(B - 1)

        @block.vector
        def _(dve):
            head_start(dve, v_tq, v_tk, v_q, v_k, v_v, v_aq, v_ak, v_sm, v_nm, v_nb, v_ri, v_z, v_y, v_st, v_mv, v_yn)
            dve.wait_ge(c_in, 16 * n_const)
            if rms:
                dve.wait_ge(g_c, 5)

            def rotate(u, ps, t, a, out, bcol, cos, t_sem, a_sem, g_sem, o_sem):
                nc.vector.tensor_tensor(t[:], ps[:, :], bcol, ALU.add).then_inc(t_sem, 1)
                dve.wait_ge(t_sem, done(u))
                c = tab[cos][:].unsqueeze(1).to_broadcast([P, H, P])
                nc.vector.tensor_tensor(heads(a[:], H), heads(t[:], H), c, ALU.mult).then_inc(a_sem, 1)
                dve.wait_ge(a_sem, done(u))
                return a

            def project(u, g):
                par = g % 2
                cols = slice(D * g, D * g + D)
                dve.wait_ge(pe_q, done(u))
                if rope:
                    rotate(u, pQ, tq, qr, qr, bias["q"][:, cols], "cosq", v_tq, v_aq, g_q, v_q)
                    dve.wait_ge(g_q, done(u))
                    nc.vector.tensor_tensor(qr[:], qr[:], sq[:], ALU.add).then_inc(v_q, 1)
                    dve.wait_ge(pe_k, done(u))
                    rotate(u, pK, tk, kr, kr, bias["k"][:, cols], "cosk", v_tk, v_ak, g_k, v_k)
                    dve.wait_ge(g_k, done(u))
                    nc.vector.tensor_tensor(kr[:], kr[:], sk[:], ALU.add).then_inc(v_k, 1)
                    dve.wait_ge(pe_v, done(u))
                    nc.vector.tensor_tensor(v[:, par, :], pV[:, :], bias["v"][:, cols], ALU.add).then_inc(v_v, 1)
                    return
                nc.vector.tensor_copy(tq[:], pQ[:, :]).then_inc(v_tq, 1)
                dve.wait_ge(pe_k, done(u))
                nc.vector.tensor_copy(tk[:], pK[:, :]).then_inc(v_tk, 1)
                dve.wait_ge(g_q, done(u))
                nc.vector.tensor_reduce(ssq[:], heads(sq[:], H), AX.X, ALU.add).then_inc(v_aq, 1)
                dve.wait_ge(g_k, done(u))
                nc.vector.tensor_reduce(ssk[:], heads(sk[:], H), AX.X, ALU.add).then_inc(v_ak, 1)
                dve.wait_ge(pe_v, done(u))
                nc.vector.tensor_copy(v[:, par, :], pV[:, :]).then_inc(v_v, 1)
                dve.wait_ge(g_rk, done(u))
                for j in range(H):
                    last = nc.vector.scalar_tensor_tensor(
                        out=kr[:, P * j:P * j + P], in0=tk[:, P * j:P * j + P], scalar=rk[:, j:j + 1], in1=gg[:],
                        op0=ALU.mult, op1=ALU.mult)
                last.then_inc(v_k, 1)

            def take_z(u):
                dve.wait_ge(pe_z, done(u))
                nc.vector.reciprocal(rinv[:], rsum[:]).then_inc(v_ri, 1)
                dve.wait_ge(v_ri, done(u))
                nc.vector.tensor_tensor(heads(zn[:], H), heads(pA[:, :], H), rinv[:].unsqueeze(2).to_broadcast([P, H, P]),
                                        ALU.mult).then_inc(v_z, 1)

            def norm(b):
                dve.wait_ge(pe_o, done(4 * b + 3))
                if rope:
                    dve.wait_ge(g_x, done(b))
                else:
                    dve.wait_ge(r_in, landed(b))
                nc.vector.tensor_tensor(y[:], pO[:, :], xres[:], ALU.add).then_inc(v_y, 1)
                dve.wait_ge(v_y, done(b))
                nc.vector.bn_stats(stats[:], y[:]).then_inc(v_st, 1)
                dve.wait_ge(v_st, done(b))
                carry_wait(nc.vector, still)
                nc.vector.bn_aggr(mv[:], stats[:]).then_inc(v_mv, 1)

            def normed(b):
                dve.wait_ge(g_rs, done(b))
                dve.wait_ge(out_st, landed(b))
                nc.vector.tensor_scalar(yn[:], y[:], mv[:, 0:1], rstd[:], ALU.subtract, ALU.mult).then_inc(v_yn, 1)

            def slot(b, g, project_next=True, back=True, finish=False):
                u = 4 * b + g
                if finish:
                    norm(b - 1)
                if back:
                    take_z(u - 1)
                dve.wait_ge(pe_s, done(u))
                if rope:
                    nc.vector.tensor_tensor(sm[:], heads(pS[:, :], H), tab["mask"][:].unsqueeze(1).to_broadcast([P, H, P]),
                                            ALU.add).then_inc(v_sm, 1)
                    dve.wait_ge(v_sm, done(u))
                    nc.vector.tensor_reduce(nmax[:], sm[:], AX.X, ALU.max, negate=True).then_inc(v_nm, 1)
                else:
                    nc.vector.tensor_reduce(nmax[:], heads(pS[:, :], H), AX.X, ALU.max, negate=True).then_inc(v_nm, 1)
                    dve.wait_ge(v_nm, done(u))
                    dve.wait_ge(g_rq, done(u))
                    nc.vector.tensor_tensor(nb[:], nmax[:], rq[:, g % 2, :], ALU.mult).then_inc(v_nb, 1)
                if project_next:
                    project(u + 1, (g + 1) % G)
                if finish:
                    normed(b - 1)

            project(0, 0)
            slot(0, 0, back=False)
            slot(0, 1)
            with dve.Fori(0, B - 1) as b:
                slot(b, 2)
                slot(b, 3)
                slot(b + 1, 0)
                slot(b + 1, 1, finish=True)
            slot(B - 1, 2)
            slot(B - 1, 3, project_next=False)
            take_z(G * B - 1)
            norm(B - 1)
            normed(B - 1)

        @block.tensor
        def _(pe):
            head_start(pe, pe_x, pe_q, pe_k, pe_v, pe_qt, pe_kt, pe_s, pe_pt, pe_z, pe_zt, pe_o)

            def turn_x(b):
                pe.wait_ge(x_in, landed(b))
                for c in range(C):
                    last = nc.tensor.transpose(pP[:, P * c:P * c + P], xin[:, P * c:P * c + P], ident[:])
                last.then_inc(pe_x, 1)

            def project(ps, w, lhs, n, g, sem):
                for c in range(n):
                    last = nc.tensor.matmul(ps[:, :], lhs[:, c, :], w[:, c, D * g:D * g + D], start=c == 0, stop=c == n - 1)
                last.then_inc(sem, 1)

            def turn_q(u):
                pe.wait_ge(v_q if rope else v_tq, done(u))
                for j in range(H):
                    last = nc.tensor.transpose(pA[:, P * j:P * j + P], qr[:, P * j:P * j + P], ident[:])
                last.then_inc(pe_qt, 1)
                pe.wait_ge(v_k, done(u))
                for j in range(H):
                    last = nc.tensor.transpose(pB[:, P * j:P * j + P], kr[:, P * j:P * j + P], ident[:])
                last.then_inc(pe_kt, 1)

            def probs_v(u, g):
                pe.wait_ge(act_pt, done(u))
                pe.wait_ge(v_v, done(u))
                for j in range(H):
                    last = nc.tensor.matmul(pA[:, P * j:P * j + P], probT[:, j, :], v[:, g % 2, P * j:P * j + P],
                                            start=True, stop=True)
                last.then_inc(pe_z, 1)

            def turn_z(u):
                pe.wait_ge(v_z, done(u))
                for j in range(H):
                    last = nc.tensor.transpose(pB[:, P * j:P * j + P], zn[:, P * j:P * j + P], ident[:])
                last.then_inc(pe_zt, 1)

            def output(u, b, g):
                pe.wait_ge(act_zt, done(u))
                pe.wait_ge(wo_in[g], 16)
                if g == 0:
                    pe.wait_ge(v_y, done(b - 1))
                for j in range(H):
                    last = nc.tensor.matmul(pO[:, :], zT[:, j, :], wo[:, H * g + j, :], start=g == 0 and j == 0,
                                            stop=g == G - 1 and j == H - 1)
                last.then_inc(pe_o, 1)

            def slot(b, g, project_next=True, back=True):
                u = 4 * b + g
                turn_q(u)
                if project_next and g == G - 1:
                    pe.wait_ge(act_pt, done(u - 1))
                    turn_x(b + 1)
                pe.wait_ge(act_qt, done(u))
                if back:
                    probs_v(u - 1, (g - 1) % G)
                pe.wait_ge(act_kt, done(u))
                for j in range(H):
                    last = nc.tensor.matmul(pS[:, P * j:P * j + P], qT[:, j, :], kT[:, j, :], start=True, stop=True)
                last.then_inc(pe_s, 1)
                if project_next:
                    pe.wait_ge(w_in[(g + 1) % G], 48)
                    if g == G - 1:
                        pe.wait_ge(act_x, done(b + 1))
                        if rms:
                            pe.wait_ge(ctx_in, landed(b + 1))
                    project(pQ, wq, xT, C, (g + 1) % G, pe_q)
                    project(pK, wk, srcT, KC, (g + 1) % G, pe_k)
                if back:
                    turn_z(u - 1)
                if project_next:
                    pe.wait_ge(v_v, done(u))
                    project(pV, wv, srcT, KC, (g + 1) % G, pe_v)
                pe.wait_ge(act_e, done(u))
                for j in range(H):
                    last = nc.tensor.transpose(pP[:, P * j:P * j + P], prob[:, j, :], ident[:])
                last.then_inc(pe_pt, 1)
                if back:
                    output(u - 1, b - 1 if g == 0 else b, (g - 1) % G)

            turn_x(0)
            pe.wait_ge(act_x, done(0))
            if rms:
                pe.wait_ge(ctx_in, landed(0))
            pe.wait_ge(w_in[0], 48)
            project(pQ, wq, xT, C, 0, pe_q)
            project(pK, wk, srcT, KC, 0, pe_k)
            project(pV, wv, srcT, KC, 0, pe_v)
            slot(0, 0, back=False)
            with pe.Fori(0, B - 1) as b:
                for g in range(1, G):
                    slot(b, g)
                slot(b + 1, 0)
            for g in range(1, G):
                slot(B - 1, g, project_next=g < G - 1)
            u = G * B - 1
            probs_v(u, G - 1)
            turn_z(u)
            output(u, B - 1, G - 1)


def narrow_attention(nc, name, psum, ident, x_src, x_dst, w_dram, NH, events, rope=False, causal=False):
    DH = D // NH
    H = 4
    UN = NH // H
    W = 32
    NBLK = NH * W // P
    ROUNDS = NBLK // 4
    HB = NH // 2
    KC = C if causal else w_dram["ctxT"].shape[2]
    SCALE = float(1.0 / np.sqrt(float(DH)))
    with ExitStack() as ctx:
        st = Stage(nc, ctx, name)
        pJ, pT, pS0, pS1, pP, pO, pZ0, pZ1 = psum
        pS, pZ = (pS0, pS1), (pZ0, pZ1)

        wq = st.sbuf("wq", [P, C, D])
        wk = st.sbuf("wk", [P, KC, D])
        wv = st.sbuf("wv", [P, KC, D])
        wo = st.sbuf("wo", [P, C, D])
        xin = st.sbuf("xin", [P, D])
        xres = st.sbuf("xres", [P, D])
        xT = st.sbuf("xT", [P, C, P])
        qs = st.sbuf("qs", [P, NH, W])
        ks = st.sbuf("ks", [P, NH, W])
        qT = st.sbuf("qT", [P, 2, NBLK, P])
        kT = st.sbuf("kT", [P, 2, NBLK, P])
        va = st.sbuf("va", [P, 2, NH, DH + 1])
        nmax = st.sbuf("nmax", [P, 2, H])
        low = st.sbuf("low", [P, 2, H, P])
        prob = st.sbuf("prob", [P, 2, H, P])
        probT = st.sbuf("probT", [P, 2, H, P])
        zn = st.sbuf("zn", [P, D])
        zT = st.sbuf("zT", [P, C, P])
        rinv = st.sbuf("rinv", [P, 2, HB])
        y = st.sbuf("y", [P, D])
        yn = st.sbuf("yn", [P, D])
        stats = st.sbuf("stats", [P, 6])
        mv = st.sbuf("mv", [P, 2])
        rstd = st.sbuf("rstd", [P, 1])
        mhalf = st.sbuf("mhalf", [P, 1])
        eps = st.sbuf("eps", [P, 1])
        still = st.sbuf("still", [P, 1])
        if causal:
            sm = st.sbuf("sm", [P, 2, H, P])
            mask = st.sbuf("mask", [P, P])
        if rope:
            srcT = st.sbuf("ctxT", [P, KC, P])
            bo = st.sbuf("bo", [P, D])
            pos = st.sbuf("pos", [P, 2 * B])
            freq = st.sbuf("freq", [P, 4])
            ang = st.sbuf("ang", [P, 2, 8 * B])
            turns = st.sbuf("turns", [P, 2, 8 * B])
            tab = st.sbuf("tab", [P, 3, B, 8])
            tc = {n: st.sbuf("tc" + n, [P, D]) for n in "qk"}
            ts = {n: st.sbuf("ts" + n, [P, D]) for n in "qk"}
        else:
            srcT = xT

        c_in, x_in, r_in, ctx_in, out_st = st.sems("c_in", "x_in", "r_in", "ctx_in", "out_st")
        w_in = st.sems("wq_in", "wk_in", "wv_in", "wo_in")
        pe_x, pe_q, pe_k, pe_v, pe_t, pe_s, pe_pt, pe_z, pe_zt, pe_o = st.sems(
            "pe_x", "pe_q", "pe_k", "pe_v", "pe_t", "pe_s", "pe_pt", "pe_z", "pe_zt", "pe_o")
        act_x, act_v, act_t, act_e, act_pt, act_zt, act_tab = st.sems("act_x", "act_v", "act_t", "act_e", "act_pt", "act_zt", "act_tab")
        v_q, v_k, v_sm, v_nm, v_low, v_ri, v_z, v_y, v_st, v_mv, v_yn, v_tab = st.sems(
            "v_q", "v_k", "v_sm", "v_nm", "v_low", "v_ri", "v_z", "v_y", "v_st", "v_mv", "v_yn", "v_tab")
        g_c, g_q, g_k, g_low, g_x, g_ve, g_rs = st.sems("g_c", "g_q", "g_k", "g_low", "g_x", "g_ve", "g_rs")
        q_ready, k_ready = (g_q, g_k) if rope else (v_q, v_k)
        low_ready = g_low if causal else v_low

        n_const = 16 * (3 if rope else 1)
        block = ctx.enter_context(nc.Block())

        def each_batch(engine, slot):
            for s in range(UN):
                slot(0, s, 0, back=False)
            with engine.Fori(0, B // 2 - 1) as i:
                for par in (1, 0):
                    for s in range(UN):
                        slot(2 * i + 2 - par, s, par)
            for s in range(UN):
                slot(B - 1, s, 1, ahead=False)

        @block.sync
        def _(sp):
            sp.sem_inc(out_st, 16)
            sp.dma_start(xin[:], x_src(0)).then_inc(x_in, 16)
            if rope:
                sp.dma_start(srcT[:], w_dram["ctxT"][:, 0]).then_inc(ctx_in, 16)
            for n, t, s in zip("qkvo", (wq, wk, wv, wo), w_in):
                sp.dma_start(t[:], w_dram["w" + n]).then_inc(s, 16)
            sp.dma_start(xres[:], x_src(0)).then_inc(r_in, 16)

            def next_tiles(b):
                sp.wait_ge(pe_x, done(b))
                sp.dma_start(xin[:], x_src(b + 1)).then_inc(x_in, 16)
                if rope:
                    sp.wait_ge(pe_v, done(b))
                    sp.dma_start(srcT[:], w_dram["ctxT"][:, b + 1]).then_inc(ctx_in, 16)

            def store(b):
                sp.wait_ge(v_yn, done(b))
                sp.dma_start(x_dst(b), yn[:]).then_inc(out_st, 16)

            def next_residual(b):
                sp.wait_ge(v_y, done(b))
                sp.dma_start(xres[:], x_src(b + 1)).then_inc(r_in, 16)

            next_tiles(0)
            with sp.Fori(0, B - 2) as b:
                next_tiles(b + 1)
                next_residual(b)
                store(b)
            next_residual(B - 2)
            store(B - 2)
            store(B - 1)
            sp.wait_ge(out_st, landed(B))

        @block.scalar
        def _(act):
            head_start(act, act_x, act_v, act_t, act_e, act_pt, act_zt)
            if rope:
                act.dma_start(pos[:], w_dram["pos"]).then_inc(c_in, 16)
                act.dma_start(freq[:], w_dram["freq"]).then_inc(c_in, 16)
                act.dma_start(bo[:], w_dram["bo"].partition_broadcast(P)).then_inc(c_in, 16)
                act.wait_ge(v_tab, 8)
                nc.scalar.activation(tab[:, 1].rearrange("p b f -> p (b f)"), ang[:, 0], ACT.Sin).then_inc(act_tab, 1)
                nc.scalar.activation(tab[:, 0].rearrange("p b f -> p (b f)"), ang[:, 1], ACT.Sin).then_inc(act_tab, 1)
            else:
                act.dma_start(mask[:], w_dram["mask"]).then_inc(c_in, 16)

            def take_x(b):
                act.wait_ge(pe_x, done(b))
                nc.scalar.copy(xT[:], pJ[:, :]).then_inc(act_x, 1)

            def take_v(b, par):
                act.wait_ge(pe_v, done(b))
                nc.scalar.copy(va[:, par, :, 0:DH], heads(pJ[:, :], NH)).then_inc(act_v, 1)

            def take_t(b, par, n):
                act.wait_ge(pe_t, done(2 * ROUNDS * b + n))
                t, r = (qT, n) if n < ROUNDS else (kT, n - ROUNDS)
                nc.scalar.copy(t[:, par, 4 * r:4 * r + 4, :], pT[:, :]).then_inc(act_t, 1)

            def take_prob(u, s):
                act.wait_ge(pe_pt, done(u))
                nc.scalar.copy(probT[:, s % 2], pP[:, :]).then_inc(act_pt, 1)

            def slot(b, s, par, back=True, ahead=True):
                u = UN * b + s
                if back or s >= 2:
                    take_prob(u - 2, s)
                act.wait_ge(low_ready, done(u))
                nc.scalar.activation(prob[:, s % 2], low[:, s % 2], ACT.Exp, scale=SCALE).then_inc(act_e, 1)
                for e in events[s]:
                    if e == "x" and ahead:
                        take_x(b + 1)
                    if e == "v" and ahead:
                        take_v(b + 1, 1 - par)
                    if e == "zt" and back:
                        act.wait_ge(pe_zt, done(b - 1))
                        nc.scalar.copy(zT[:], pT[:, :]).then_inc(act_zt, 1)
                    if isinstance(e, int) and ahead:
                        take_t(b + 1, 1 - par, e)

            take_x(0)
            take_v(0, 0)
            for n in range(2 * ROUNDS):
                take_t(0, 0, n)
            each_batch(act, slot)
            take_prob(UN * B - 2, 0)
            take_prob(UN * B - 1, 1)
            act.wait_ge(pe_zt, done(B - 1))
            nc.scalar.copy(zT[:], pT[:, :]).then_inc(act_zt, 1)

        @block.gpsimd
        def _(pool):
            head_start(pool, g_q, g_k, g_low, g_x, g_ve, g_rs)
            nc.gpsimd.memset(mhalf[:], -0.5).then_inc(g_c, 1)
            nc.gpsimd.memset(va[:], 1.0).then_inc(g_c, 1)
            nc.gpsimd.memset(eps[:], EPS).then_inc(g_c, 1)
            if rope:
                nc.gpsimd.memset(qs[:], 0.0).then_inc(g_c, 1)
                nc.gpsimd.memset(ks[:], 0.0).then_inc(g_c, 1)
            pool.wait_ge(g_c, 5 if rope else 3)
            pool.wait_ge(c_in, n_const)

            def rotated(b):
                for t, o, v_sem, g_sem in (("q", qs, v_q, g_q), ("k", ks, v_k, g_k)):
                    pool.wait_ge(v_sem, done(b))
                    nc.gpsimd.tensor_tensor(o[:, :, 0:DH], heads(tc[t][:], NH), heads(ts[t][:], NH), ALU.add).then_inc(g_sem, 1)

            def residual(b):
                if rope:
                    pool.wait_ge(r_in, landed(b))
                    nc.gpsimd.tensor_tensor(xres[:], xres[:], bo[:], ALU.add).then_inc(g_x, 1)

            def norm(b):
                pool.wait_ge(v_mv, done(b))
                nc.gpsimd.tensor_tensor(rstd[:], mv[:, 1:2], eps[:], ALU.add).then_inc(g_ve, 1)
                pool.wait_ge(g_ve, done(b))
                nc.gpsimd.tensor_tensor(rstd[:], rstd[:], mhalf[:], ALU.pow).then_inc(g_rs, 1)

            def slot(b, s, par, back=True, ahead=True):
                u = UN * b + s
                if causal:
                    pool.wait_ge(v_nm, done(u))
                    pool.wait_ge(act_e, done(u - 2))
                    nc.gpsimd.tensor_tensor(low[:, s % 2], sm[:, s % 2], nmax[:, s % 2].unsqueeze(2).to_broadcast([P, H, P]),
                                            ALU.add).then_inc(g_low, 1)
                for e in events[s]:
                    if e == "k" and ahead and rope:
                        rotated(b + 1)
                    if e == "o" and back:
                        norm(b - 1)
                        residual(b)

            if rope:
                rotated(0)
            residual(0)
            each_batch(pool, slot)
            norm(B - 1)

        @block.vector
        def _(dve):
            head_start(dve, v_q, v_k, v_sm, v_nm, v_low, v_ri, v_z, v_y, v_st, v_mv, v_yn)
            dve.wait_ge(c_in, n_const)
            if rope:
                two_pi = 2 * np.pi
                hi = float(np.float32(6.28125))
                lo = float(np.float32(two_pi - hi))
                magic = 12582912.0
                nc.vector.tensor_tensor(ang[:, 0].rearrange("p (n f) -> p n f", f=4), pos[:].unsqueeze(2).to_broadcast([P, 2 * B, 4]),
                                        freq[:].unsqueeze(1).to_broadcast([P, 2 * B, 4]), ALU.mult).then_inc(v_tab, 1)
                dve.wait_ge(v_tab, 1)
                nc.vector.tensor_scalar(ang[:, 1], ang[:, 0], float(np.pi / 2), None, ALU.add).then_inc(v_tab, 1)
                dve.wait_ge(v_tab, 2)
                nc.vector.tensor_scalar(turns[:], ang[:], float(1 / two_pi), magic, ALU.mult, ALU.add).then_inc(v_tab, 1)
                dve.wait_ge(v_tab, 3)
                nc.vector.tensor_scalar(turns[:], turns[:], -magic, None, ALU.add).then_inc(v_tab, 1)
                dve.wait_ge(v_tab, 4)
                nc.vector.scalar_tensor_tensor(out=ang[:], in0=turns[:], scalar=-hi, in1=ang[:], op0=ALU.mult, op1=ALU.add).then_inc(v_tab, 1)
                dve.wait_ge(v_tab, 5)
                nc.vector.scalar_tensor_tensor(out=ang[:], in0=turns[:], scalar=-lo, in1=ang[:], op0=ALU.mult, op1=ALU.add).then_inc(v_tab, 1)
                dve.wait_ge(v_tab, 6)
                nc.vector.tensor_scalar(ang[:], ang[:], 3.1415925, -3.1415925, ALU.min, ALU.max).then_inc(v_tab, 2)
                dve.wait_ge(act_tab, 2)
                nc.vector.tensor_scalar(tab[:, 2], tab[:, 1], -1.0, None, ALU.mult).then_inc(v_tab, 1)
                dve.wait_ge(v_tab, 9)

            def take(b, ps, t, out, pe_sem, v_sem):
                dve.wait_ge(pe_sem, done(b))
                if not rope:
                    nc.vector.tensor_copy(out[:].rearrange("p h w -> p (h w)"), ps[:, :]).then_inc(v_sem, 1)
                    return
                nc.vector.tensor_tensor(tc[t][:].rearrange("p (n f) -> p n f", f=8), ps[:, :].rearrange("p (n f) -> p n f", f=8),
                                        tab[:, 0, b].unsqueeze(1).to_broadcast([P, 2 * NH, 8]), ALU.mult)
                for half in range(2):
                    o = heads(ts[t][:], NH)[:, :, 8 * half:8 * half + 8]
                    i = heads(ps[:, :], NH)[:, :, 8 - 8 * half:16 - 8 * half]
                    last = nc.vector.tensor_tensor(o, i, tab[:, 2 - half, b].unsqueeze(1).to_broadcast([P, NH, 8]), ALU.mult)
                last.then_inc(v_sem, 1)

            def take_z(b):
                dve.wait_ge(pe_z, done(UN * b + UN - 1))
                for n in range(2):
                    z = pZ[n][:, 0:HB * (DH + 1)].rearrange("p (h d) -> p h d", h=HB)
                    last = nc.vector.reciprocal(rinv[:, n], z[:, :, DH])
                last.then_inc(v_ri, 1)
                dve.wait_ge(v_ri, done(b))
                for n in range(2):
                    z = pZ[n][:, 0:HB * (DH + 1)].rearrange("p (h d) -> p h d", h=HB)
                    last = nc.vector.tensor_tensor(heads(zn[:, n * D // 2:(n + 1) * D // 2], HB), z[:, :, 0:DH],
                                                   rinv[:, n].unsqueeze(2).to_broadcast([P, HB, DH]), ALU.mult)
                last.then_inc(v_z, 1)

            def norm(b):
                dve.wait_ge(pe_o, done(b))
                if rope:
                    dve.wait_ge(g_x, done(b))
                else:
                    dve.wait_ge(r_in, landed(b))
                nc.vector.tensor_tensor(y[:], pO[:, :], xres[:], ALU.add).then_inc(v_y, 1)
                dve.wait_ge(v_y, done(b))
                nc.vector.bn_stats(stats[:], y[:]).then_inc(v_st, 1)
                dve.wait_ge(v_st, done(b))
                carry_wait(nc.vector, still)
                nc.vector.bn_aggr(mv[:], stats[:]).then_inc(v_mv, 1)
                dve.wait_ge(g_rs, done(b))
                dve.wait_ge(out_st, landed(b))
                nc.vector.tensor_scalar(yn[:], y[:], mv[:, 0:1], rstd[:], ALU.subtract, ALU.mult).then_inc(v_yn, 1)

            def slot(b, s, par, back=True, ahead=True):
                u = UN * b + s
                dve.wait_ge(pe_s, done(u))
                nb = nmax[:, s % 2].unsqueeze(2).to_broadcast([P, H, P])
                if causal:
                    dve.wait_ge(g_low, done(u - 2))
                    nc.vector.tensor_tensor(sm[:, s % 2], heads(pS[s % 2][:, :], H), mask[:].unsqueeze(1).to_broadcast([P, H, P]),
                                            ALU.add).then_inc(v_sm, 1)
                    dve.wait_ge(v_sm, done(u))
                    nc.vector.tensor_reduce(nmax[:, s % 2], sm[:, s % 2], AX.X, ALU.max, negate=True).then_inc(v_nm, 1)
                else:
                    nc.vector.tensor_reduce(nmax[:, s % 2], heads(pS[s % 2][:, :], H), AX.X, ALU.max, negate=True).then_inc(v_nm, 1)
                    dve.wait_ge(v_nm, done(u))
                    dve.wait_ge(act_e, done(u - 2))
                    nc.vector.tensor_tensor(low[:, s % 2], heads(pS[s % 2][:, :], H), nb, ALU.add).then_inc(v_low, 1)
                if s == 2 and back:
                    take_z(b - 1)
                for e in events[s]:
                    if e == "q" and ahead:
                        take(b + 1, pJ, "q", qs, pe_q, v_q)
                    if e == "k" and ahead:
                        take(b + 1, pJ, "k", ks, pe_k, v_k)
                    if e == "o" and back:
                        norm(b - 1)

            if rope:
                dve.wait_ge(g_c, 5)
            take(0, pJ, "q", qs, pe_q, v_q)
            take(0, pJ, "k", ks, pe_k, v_k)
            each_batch(dve, slot)
            take_z(B - 1)
            norm(B - 1)

        @block.tensor
        def _(pe):
            head_start(pe, pe_x, pe_q, pe_k, pe_v, pe_t, pe_s, pe_pt, pe_z, pe_zt, pe_o)

            def turn_x(b):
                pe.wait_ge(x_in, landed(b))
                pe.wait_ge(act_v, done(b - 1))
                for c in range(C):
                    last = nc.tensor.transpose(pJ[:, P * c:P * c + P], xin[:, P * c:P * c + P], ident[:])
                last.then_inc(pe_x, 1)

            def project(w, lhs, n, sem):
                for c in range(n):
                    last = nc.tensor.matmul(pJ[:, :], lhs[:, c, :], w[:, c, :], start=c == 0, stop=c == n - 1)
                last.then_inc(sem, 1)

            def project_q(b):
                pe.wait_ge(act_x, done(b))
                project(wq, xT, C, pe_q)

            def project_k(b):
                if rope:
                    pe.wait_ge(ctx_in, landed(b))
                pe.wait_ge(v_q, done(b))
                project(wk, srcT, KC, pe_k)

            def project_v(b):
                pe.wait_ge(v_k, done(b))
                project(wv, srcT, KC, pe_v)

            def turn(b, n):
                src, r = (qs, n) if n < ROUNDS else (ks, n - ROUNDS)
                pe.wait_ge(q_ready if n < ROUNDS else k_ready, done(b))
                pe.wait_ge(act_t, done(2 * ROUNDS * b + n - 1))
                pe.wait_ge(act_zt, done(b - 2))
                flat = src[:].rearrange("p h w -> p (h w)")
                for j in range(4):
                    last = nc.tensor.transpose(pT[:, P * j:P * j + P], flat[:, P * (4 * r + j):P * (4 * r + j + 1)], ident[:])
                last.then_inc(pe_t, 1)

            def place(s, j):
                r, block_ = s % 4, 4 * (s // 4) + j
                return 4 * block_ + r, slice(W * r, W * r + W), block_

            def turn_prob(u, s):
                pe.wait_ge(act_e, done(u))
                pe.wait_ge(act_pt, done(u - 1))
                for j in range(H):
                    last = nc.tensor.transpose(pP[:, P * j:P * j + P], prob[:, s % 2, j, :], ident[:])
                last.then_inc(pe_pt, 1)

            def probs_v(u, b, s, par):
                pe.wait_ge(act_pt, done(u))
                if s == 0:
                    pe.wait_ge(act_v, done(b))
                    pe.wait_ge(v_z, done(b - 1))
                for j in range(H):
                    h = place(s, j)[0]
                    col = (h % HB) * (DH + 1)
                    last = nc.tensor.matmul(pZ[h // HB][:, col:col + DH + 1], probT[:, s % 2, j, :], va[:, par, h, :],
                                            start=True, stop=True)
                last.then_inc(pe_z, 1)

            def turn_z(b):
                pe.wait_ge(v_z, done(b))
                pe.wait_ge(act_t, done(2 * ROUNDS * (b + 1) + 2 * ROUNDS - 1))
                for c in range(C):
                    last = nc.tensor.transpose(pT[:, P * c:P * c + P], zn[:, P * c:P * c + P], ident[:])
                last.then_inc(pe_zt, 1)

            def output(b):
                pe.wait_ge(act_zt, done(b))
                pe.wait_ge(v_y, done(b - 1))
                for c in range(C):
                    last = nc.tensor.matmul(pO[:, :], zT[:, c, :], wo[:, c, :], start=c == 0, stop=c == C - 1)
                last.then_inc(pe_o, 1)

            def slot(b, s, par, back=True, ahead=True):
                u = UN * b + s
                if s == 0:
                    pe.wait_ge(act_t, done(2 * ROUNDS * b + 2 * ROUNDS - 1))
                pe.wait_ge(v_sm if causal else v_low, done(u - 2))
                for j in range(H):
                    _, rows, blk = place(s, j)
                    last = nc.tensor.matmul(pS[s % 2][:, P * j:P * j + P], qT[rows, par, blk, :], kT[rows, par, blk, :],
                                            start=True, stop=True)
                last.then_inc(pe_s, 1)
                if back or s >= 2:
                    turn_prob(u - 2, s)
                if back or s >= 3:
                    s3 = (s - 3) % UN
                    here = s >= 3
                    probs_v(u - 3, b if here else b - 1, s3, par if here else 1 - par)
                for e in events[s]:
                    if ahead:
                        if e == "x":
                            turn_x(b + 1)
                        if e == "q":
                            project_q(b + 1)
                        if e == "k":
                            project_k(b + 1)
                        if e == "v":
                            project_v(b + 1)
                        if isinstance(e, int):
                            turn(b + 1, e)
                    if back:
                        if e == "zt":
                            turn_z(b - 1)
                        if e == "o":
                            output(b - 1)

            turn_x(0)
            pe.wait_ge(w_in[0], 16)
            project_q(0)
            pe.wait_ge(w_in[1], 16)
            project_k(0)
            pe.wait_ge(w_in[2], 16)
            pe.wait_ge(g_c, 3)
            project_v(0)
            for n in range(2 * ROUNDS):
                turn(0, n)
            pe.wait_ge(w_in[3], 16)
            each_batch(pe, slot)
            last_u = UN * B - 1
            turn_prob(last_u - 1, 0)
            probs_v(last_u - 2, B - 1, UN - 3, 1)
            turn_prob(last_u, 1)
            probs_v(last_u - 1, B - 1, UN - 2, 1)
            probs_v(last_u, B - 1, UN - 1, 1)
            pe.wait_ge(v_z, done(B - 1))
            for c in range(C):
                last = nc.tensor.transpose(pT[:, P * c:P * c + P], zn[:, P * c:P * c + P], ident[:])
            last.then_inc(pe_zt, 1)
            output(B - 1)


EVENTS_8 = [["x"], ["q"], ["k"], ["zt", "v"], ["o", 0], [1], [2], [3]]
EVENTS_4 = [["x"], ["q"], ["k"], ["zt", 0, "o", "v", 1]]


class Chain:

    def __init__(self, engine, sem):
        self.engine, self.sem, self.n = engine, sem, 0

    def __call__(self, ins):
        self.n += 1
        ins.then_inc(self.sem, 1)
        self.engine.wait_ge(self.sem, self.n)


def in_turns(engine, slot, rounds, ring):
    slot(0, 0, back=False)
    with engine.Fori(0, rounds - 1) as i:
        for n in range(1, ring):
            slot(i, n)
        slot(i + 1, 0)
    for n in range(1, ring):
        slot(rounds - 1, n, ahead=n < ring - 1)


def following(i, n, ring):
    return (i, n + 1) if n < ring - 1 else (i + 1, 0)


def preceding(i, n, ring):
    return (i, n - 1) if n else (i - 1, ring - 1)


def shared_expert(nc, psum, ident, x_src, w_dram, base, logits, NE):
    R = 4
    with ExitStack() as ctx:
        st = Stage(nc, ctx, "c")
        pX, pG, pU, pL, pO = psum[0:5]
        wg, wu, wd = (st.sbuf(n, [P, C, D]) for n in ("wg", "wu", "wd"))
        rw = st.sbuf("rw", [P, C, NE])
        xin = st.sbuf("xin", [P, R, D])
        xT = st.sbuf("xT", [P, 2, C, P])
        gate = st.sbuf("gate", [P, C, P])
        h = st.sbuf("h", [P, C, P])
        x_in = [st.sem(f"x_in{n}") for n in range(R)]
        w_in, wd_in, pe_x, pe_l, pe_g, pe_u, pe_o = st.sems("w_in", "wd_in", "pe_x", "pe_l", "pe_g", "pe_u", "pe_o")
        act_x, act_g, act_l, v_h, v_b = st.sems("act_x", "act_g", "act_l", "v_h", "v_b")
        block = ctx.enter_context(nc.Block())

        @block.sync
        def _(sp):
            def load(i, n):
                sp.dma_start(xin[:, n, :], x_src[R * i + n]).then_inc(x_in[n], 16)

            load(0, 0)
            sp.dma_start(rw[:], w_dram["rw"]).then_inc(w_in, 16)
            sp.dma_start(wg[:], w_dram["sg"]).then_inc(w_in, 16)
            sp.dma_start(wu[:], w_dram["su"]).then_inc(w_in, 16)
            sp.dma_start(wd[:], w_dram["sd"]).then_inc(wd_in, 16)
            for n in range(1, R):
                load(0, n)
            with sp.Fori(0, B // R - 1) as i:
                for n in range(R):
                    sp.wait_ge(v_b, done(R * i + n))
                    load(i + 1, n)

        @block.scalar
        def _(act):
            head_start(act, act_x, act_g, act_l)

            def take_x(i, n):
                act.wait_ge(pe_x, done(R * i + n))
                nc.scalar.copy(xT[:, n % 2], pX[:, :]).then_inc(act_x, 1)

            def slot(i, n, back=True, ahead=True):
                b = R * i + n
                act.wait_ge(pe_l, done(b))
                nc.scalar.copy(logits[:, b, :], pL[:, 0:NE]).then_inc(act_l, 1)
                act.wait_ge(pe_g, done(b))
                act.wait_ge(v_h, done(b - 1))
                nc.scalar.activation(gate[:], pG[:, :], ACT.Silu).then_inc(act_g, 1)
                if ahead:
                    take_x(*following(i, n, R))

            take_x(0, 0)
            in_turns(act, slot, B // R, R)

        @block.vector
        def _(dve):
            head_start(dve, v_h, v_b)

            def shared(i, n):
                b = R * i + n
                dve.wait_ge(pe_o, done(b))
                nc.vector.tensor_tensor(base[:, b, :], pO[:, :], xin[:, n, :], ALU.add).then_inc(v_b, 1)

            def slot(i, n, back=True, ahead=True):
                b = R * i + n
                if back:
                    shared(*preceding(i, n, R))
                dve.wait_ge(act_g, done(b))
                dve.wait_ge(pe_u, done(b))
                nc.vector.tensor_tensor(h[:], gate[:], pU[:, :].rearrange("p (c t) -> p c t", c=C), ALU.mult).then_inc(v_h, 1)

            in_turns(dve, slot, B // R, R)
            shared(B // R - 1, R - 1)

        @block.tensor
        def _(pe):
            head_start(pe, pe_x, pe_l, pe_g, pe_u, pe_o)

            def turn_x(i, n):
                pe.wait_ge(x_in[n], landed(i))
                for c in range(C):
                    last = nc.tensor.transpose(pX[:, P * c:P * c + P], xin[:, n, P * c:P * c + P], ident[:])
                last.then_inc(pe_x, 1)

            def up(ps, w, n, sem):
                for i in range(C):
                    for c in range(C):
                        last = nc.tensor.matmul(ps[:, P * i:P * i + P], w[:, c, P * i:P * i + P], xT[:, n % 2, c, :],
                                                start=c == 0, stop=c == C - 1)
                last.then_inc(sem, 1)

            def down(b):
                pe.wait_ge(v_h, done(b))
                pe.wait_ge(v_b, done(b - 1))
                for c in range(C):
                    last = nc.tensor.matmul(pO[:, :], h[:, c, :], wd[:, c, :], start=c == 0, stop=c == C - 1)
                last.then_inc(pe_o, 1)

            def slot(i, n, back=True, ahead=True):
                b = R * i + n
                pe.wait_ge(act_x, done(b))
                pe.wait_ge(act_l, done(b - 1))
                for c in range(C):
                    last = nc.tensor.matmul(pL[:, 0:NE], xT[:, n % 2, c, :], rw[:, c, :], start=c == 0, stop=c == C - 1)
                last.then_inc(pe_l, 1)
                if ahead:
                    turn_x(*following(i, n, R))
                pe.wait_ge(act_g, done(b - 1))
                up(pG, wg, n, pe_g)
                if back:
                    down(b - 1)
                pe.wait_ge(v_h, done(b - 1))
                up(pU, wu, n, pe_u)

            turn_x(0, 0)
            pe.wait_ge(w_in, 48)
            pe.wait_ge(wd_in, 16)
            in_turns(pe, slot, B // R, R)
            down(B - 1)


def route(nc, name, psum, tri, ones, logits, w_dram, NE, K, weight, slot_in, slot_out, grouped):
    NG, CAP, DROPPED = 8, 80, 80 * 32
    with ExitStack() as ctx:
        st = Stage(nc, ctx, name)
        pPos, pTot = psum[0], psum[1]
        iota = st.sbuf("iota", [P, 128])
        top = st.sbuf("top", [P, B, 8])
        topi = st.sbuf("topi", [P, B, 8], U32)
        topf = st.sbuf("topf", [P, B, 8])
        hot = st.sbuf("hot", [P, K, B, NE])
        sel = st.sbuf("sel", [P, B, NE])
        pos = st.sbuf("pos", [P, B, NE])
        carry = st.sbuf("carry", [P, B + 1, NE])
        prod = st.sbuf("prod", [P, B, NE])
        rowf = st.sbuf("rowf", [P, B, K])
        wsum = st.sbuf("wsum", [P, B])
        wt = st.sbuf("wt", [P, B, K])
        if grouped:
            bias = st.sbuf("bias", [P, NE])
            score = st.sbuf("score", [P, B, NE])
            biased = st.sbuf("biased", [P, B, NE])
            masked = st.sbuf("masked", [P, B, NE])
            pair = st.sbuf("pair", [P, B * NG])
            gscore = st.sbuf("gscore", [P, B, NG])
            gtop = st.sbuf("gtop", [P, B, 8])
            gtopi = st.sbuf("gtopi", [P, B, 8], U32)
            gtopf = st.sbuf("gtopf", [P, B, 8])
            gmask = st.sbuf("gmask", [P, B, NG])
            geq = st.sbuf("geq", [P, B, NG])
            over = st.sbuf("over", [P, B, NE])
        else:
            NT = slot_out["tiles"]
            expd = st.sbuf("expd", [P, B])
            cmp = st.sbuf("cmp", [P, NE, B])
            ntile = st.sbuf("ntile", [P, NE])
            first = st.sbuf("first", [P, NE + 1])
            tcmp = st.sbuf("tcmp", [P, NT, NE])
            texp = st.sbuf("texp", [P, NT])
        c_in, v, act_s, pe_c = st.sems("c_in", "v", "act_s", "pe_c")
        block = ctx.enter_context(nc.Block())
        n_sel = []

        def flat(t):
            return t[:].rearrange("p b e -> p (b e)")

        @block.sync
        def _(sp):
            sp.dma_start(iota[:], w_dram["iota"]).then_inc(c_in, 16)
            if grouped:
                sp.dma_start(bias[:], w_dram["bias"].partition_broadcast(P)).then_inc(c_in, 16)

        @block.vector
        def _(dve):
            step = Chain(dve, v)
            vec = nc.vector
            iota_e = iota[:, 0:NE].unsqueeze(1).to_broadcast([P, B, NE])
            dve.wait_ge(c_in, 32 if grouped else 16)
            ranked = logits
            if grouped:
                dve.wait_ge(act_s, 1)
                step(vec.tensor_tensor(biased[:], score[:], bias[:].unsqueeze(1).to_broadcast([P, B, NE]), ALU.add))
                q = flat(biased).rearrange("p (g m) -> p g m", m=4)
                gs = flat(gscore)
                for n, (i, j) in enumerate([(0, 1), (0, 2), (0, 3), (1, 2), (1, 3), (2, 3)]):
                    step(vec.tensor_tensor(pair[:] if n else gs, q[:, :, i], q[:, :, j], ALU.add))
                    if n:
                        step(vec.tensor_tensor(gs, gs, pair[:], ALU.max))
                for b in range(B):
                    last = vec.max(gtop[:, b], gscore[:, b])
                step(last)
                for b in range(B):
                    last = vec.max_index(gtopi[:, b], gtop[:, b], gscore[:, b])
                step(last)
                step(vec.tensor_copy(gtopf[:], gtopi[:]))
                iota_g = iota[:, 0:NG].unsqueeze(1).to_broadcast([P, B, NG])
                for k in range(3):
                    step(vec.tensor_tensor(geq[:] if k else gmask[:], iota_g, gtopf[:, :, k:k + 1].to_broadcast([P, B, NG]), ALU.is_equal))
                    if k:
                        step(vec.tensor_tensor(gmask[:], gmask[:], geq[:], ALU.add))
                step(vec.tensor_tensor(flat(masked).rearrange("p (g m) -> p g m", m=4), q,
                                       flat(gmask).unsqueeze(2).to_broadcast([P, B * NG, 4]), ALU.mult))
                ranked = masked
            for b in range(B):
                last = vec.max(top[:, b], ranked[:, b])
            step(last)
            for b in range(B):
                last = vec.max_index(topi[:, b], top[:, b], ranked[:, b])
            step(last)
            step(vec.tensor_copy(topf[:], topi[:]))
            for k in range(K):
                step(vec.tensor_tensor(hot[:, k], iota_e, topf[:, :, k:k + 1].to_broadcast([P, B, NE]), ALU.is_equal))
                if k:
                    step(vec.tensor_tensor(sel[:], hot[:, k] if k > 1 else hot[:, 1], sel[:] if k > 1 else hot[:, 0], ALU.add))
            n_sel.append(step.n)

            if grouped:
                for k in range(K):
                    step(vec.tensor_tensor(prod[:], hot[:, k], score[:], ALU.mult))
                    step(vec.tensor_reduce(wt[:, :, k], prod[:], AX.X, ALU.add))
                step(vec.tensor_reduce(wsum[:], wt[:], AX.X, ALU.add))
                step(vec.tensor_scalar(wsum[:], wsum[:], 1e-20, None, ALU.add))
                step(vec.reciprocal(wsum[:], wsum[:]))
                step(vec.tensor_tensor(wt[:], wt[:], wsum[:].unsqueeze(2).to_broadcast([P, B, K]), ALU.mult))
                step(vec.tensor_scalar(weight[:], wt[:], 2.5, None, ALU.mult))
            else:
                step(vec.tensor_tensor(wsum[:], top[:, :, 1], top[:, :, 0], ALU.subtract))
                n_sel.append(step.n)
                dve.wait_ge(act_s, 1)
                step(vec.tensor_scalar(wsum[:], expd[:], 1.0, None, ALU.add))
                step(vec.reciprocal(weight[:, :, 0], wsum[:]))
                step(vec.tensor_tensor(weight[:, :, 1], weight[:, :, 0], expd[:], ALU.mult))

            step(vec.memset(carry[:, 0], 0.0))
            dve.wait_ge(pe_c, 1)
            for b in range(B):
                step(vec.tensor_tensor(carry[:, b + 1], carry[:, b], pTot[:, NE * b:NE * b + NE], ALU.add))
            step(vec.tensor_tensor(pos[:], pPos[:, 0:B * NE].rearrange("p (b e) -> p b e", b=B), carry[:, 0:B], ALU.add))
            if grouped:
                step(vec.tensor_scalar(over[:], pos[:], float(CAP), 2.0 * DROPPED, ALU.is_ge, ALU.mult))
                step(vec.tensor_tensor(pos[:], pos[:], over[:], ALU.add))
                step(vec.tensor_scalar(prod[:], iota_e, float(CAP), None, ALU.mult))
                step(vec.tensor_tensor(pos[:], pos[:], prod[:], ALU.add))
                step(vec.tensor_scalar(pos[:], pos[:], float(DROPPED), None, ALU.min))
            else:
                step(vec.tensor_scalar(cmp[:], iota[:, 0:B].unsqueeze(1).to_broadcast([P, NE, B]), float(P), None, ALU.mult))
                step(vec.tensor_tensor(cmp[:], carry[:, B].unsqueeze(2).to_broadcast([P, NE, B]), cmp[:], ALU.is_gt))
                step(vec.tensor_reduce(ntile[:], cmp[:], AX.X, ALU.add))
                step(vec.memset(first[:, 0:1], 0.0))
                for e in range(NE):
                    step(vec.tensor_tensor(first[:, e + 1:e + 2], first[:, e:e + 1], ntile[:, e:e + 1], ALU.add))
                step(vec.tensor_scalar(ntile[:], first[:, 0:NE], float(P), None, ALU.mult))
                step(vec.tensor_tensor(pos[:], pos[:], ntile[:].unsqueeze(1).to_broadcast([P, B, NE]), ALU.add))
                step(vec.tensor_tensor(tcmp[:], iota[:, 0:NT].unsqueeze(2).to_broadcast([P, NT, NE]),
                                       first[:, 1:NE + 1].unsqueeze(1).to_broadcast([P, NT, NE]), ALU.is_ge))
                step(vec.tensor_reduce(texp[:], tcmp[:], AX.X, ALU.add))
                step(vec.tensor_scalar(slot_out["expert"][:], texp[:], float(NE - 1), None, ALU.min))
            for k in range(K):
                step(vec.tensor_tensor(prod[:], hot[:, k], pos[:], ALU.mult))
                step(vec.tensor_reduce(rowf[:, :, k], prod[:], AX.X, ALU.add))
            step(vec.tensor_copy(slot_in[:], rowf[:]))

        @block.scalar
        def _(act):
            if grouped:
                nc.scalar.activation(score[:], logits[:], ACT.Sigmoid).then_inc(act_s, 1)
            else:
                act.wait_ge(v, n_sel[1])
                nc.scalar.activation(expd[:], wsum[:], ACT.Exp).then_inc(act_s, 1)

        @block.tensor
        def _(pe):
            pe.wait_ge(v, n_sel[0])
            nc.tensor.matmul(pPos[:, 0:B * NE], tri[:], flat(sel), start=True, stop=True)
            nc.tensor.matmul(pTot[:, 0:B * NE], ones[:], flat(sel), start=True, stop=True).then_inc(pe_c, 1)


def dispatch(nc, name, x_src, rows, packed, K, bound, ready):
    R = 4
    with ExitStack() as ctx:
        st = Stage(nc, ctx, name)
        xs = st.sbuf("xs", [P, R, D])
        idx = st.sbuf("idx", [P, R, K], U32)
        one = st.sbuf("one", [P, 1])
        still = st.sbuf("still", [P, R, 2])
        x_in = [st.sem(f"x_in{n}") for n in range(R)]
        sent = [st.sem(f"sent{n}") for n in range(R)]
        g_i, g_one = st.sems("g_i", "g_one")
        block = ctx.enter_context(nc.Block())

        @block.sync
        def _(sp):
            for n in range(R):
                sp.dma_start(xs[:, n, :], x_src[n]).then_inc(x_in[n], 16)
            with sp.Fori(0, B // R - 1) as i:
                for n in range(R):
                    sp.wait_ge(sent[n], 16 * K * (i + 1))
                    sp.dma_start(xs[:, n, :], x_src[R * i + R + n]).then_inc(x_in[n], 16)

        @block.gpsimd
        def _(pool):
            nc.gpsimd.memset(one[:], 1.0).then_inc(g_one, 1)
            pool.wait_ge(g_one, 1)
            for s, value in ready:
                pool.wait_ge(s, value)

            def tile(i, n):
                nc.gpsimd.tensor_copy(idx[:, n], rows[:, R * i + n]).then_inc(g_i, 1)
                pool.wait_ge(x_in[n], landed(i))
                nc.gpsimd.tensor_tensor(still[:, n, 0:1], one[:], one[:], ALU.add)
                pool.wait_ge(g_i, R * i + n + 1)
                nc.gpsimd.tensor_tensor(still[:, n, 1:2], one[:], one[:], ALU.add)
                for k in range(K):
                    nc.gpsimd.indirect_dma_start(packed, bass.IndirectOffsetOnAxis(ap=idx[:, n, k:k + 1], axis=0),
                                                 xs[:, n, :], None, bounds_check=bound, oob_is_err=False).then_inc(sent[n], 16)

            for n in range(R):
                tile(0, n)
            with pool.Fori(1, B // R) as i:
                for n in range(R):
                    pool.wait_ge(sent[n], 16 * K * i)
                    tile(i, n)
            for n in range(R):
                pool.wait_ge(sent[n], 16 * K * (B // R))


def capped_experts(nc, psum, ident, packed, result, zero, w_dram):
    NE, CAP, F, R = 32, 80, 256, 4
    FC = F // P
    with ExitStack() as ctx:
        st = Stage(nc, ctx, "m")
        pX, pG, pU, pO = psum[0:2], psum[2:4], psum[4:6], psum[6:8]
        xe = st.sbuf("xe", [CAP, R, D])
        wg = st.sbuf("wg", [P, R, C, F])
        wu = st.sbuf("wu", [P, R, C, F])
        wd = st.sbuf("wd", [P, R, FC, D])
        xT = st.sbuf("xT", [P, 2, C, CAP])
        gate = st.sbuf("gate", [P, 2, FC, CAP])
        h = st.sbuf("h", [P, 2, FC, CAP])
        ye = st.sbuf("ye", [CAP, 2, D])
        x_in = [st.sem(f"x_in{n}") for n in range(R)]
        w_in = [st.sem(f"w_in{n}") for n in range(R)]
        y_out = [st.sem(f"y_out{n}") for n in range(2)]
        z_out, pe_x, pe_g, pe_u, pe_o, act_g, act_y, v_x, v_h = st.sems(
            "z_out", "pe_x", "pe_g", "pe_u", "pe_o", "act_g", "act_y", "v_x", "v_h")
        block = ctx.enter_context(nc.Block())

        @block.sync
        def _(sp):
            def load(i, n):
                e = R * i + n
                sp.dma_start(xe[:, n, :], packed[e]).then_inc(x_in[n], 16)
                sp.dma_start(wg[:, n], w_dram["wg"][e]).then_inc(w_in[n], 16)
                sp.dma_start(wu[:, n], w_dram["wu"][e]).then_inc(w_in[n], 16)
                sp.dma_start(wd[:, n], w_dram["wd"][e]).then_inc(w_in[n], 16)

            def store(i, n):
                sp.wait_ge(act_y, done(R * i + n))
                sp.dma_start(result[0:NE * CAP].rearrange("(e r) d -> e r d", r=CAP)[R * i + n], ye[:, n % 2, :]).then_inc(y_out[n % 2], 16)

            for n in range(2):
                sp.sem_inc(y_out[n], 16)
            for n in range(R):
                load(0, n)
            sp.dma_start(result[NE * CAP:NE * CAP + 1, :], zero[0:1, :]).then_inc(z_out, 16)
            with sp.Fori(0, NE // R - 1) as i:
                for n in range(R):
                    sp.wait_ge(pe_o, done(R * i + n))
                    load(i + 1, n)
                    store(i, n)
            for n in range(R):
                store(NE // R - 1, n)
            sp.wait_ge(z_out, 16)
            for n in range(2):
                sp.wait_ge(y_out[n], landed(NE // 2))

        @block.scalar
        def _(act):
            head_start(act, act_g, act_y)

            def take_y(i, n):
                e = R * i + n
                act.wait_ge(pe_o, done(e))
                act.wait_ge(y_out[n % 2], landed(R // 2 * i + n // 2))
                nc.scalar.copy(ye[:, n % 2, :], pO[n % 2][0:CAP, :]).then_inc(act_y, 1)

            def slot(i, n, back=True, ahead=True):
                e = R * i + n
                act.wait_ge(pe_g, done(e))
                act.wait_ge(v_h, done(e - 2))
                nc.scalar.activation(gate[:, n % 2], pG[n % 2][:, 0:FC * CAP].rearrange("p (c t) -> p c t", c=FC),
                                     ACT.Silu).then_inc(act_g, 1)
                if back:
                    take_y(*preceding(i, n, R))

            in_turns(act, slot, NE // R, R)
            take_y(NE // R - 1, R - 1)

        @block.vector
        def _(dve):
            head_start(dve, v_x, v_h)

            def take_x(i, n):
                dve.wait_ge(pe_x, done(R * i + n))
                nc.vector.tensor_copy(xT[:, n % 2], pX[n % 2][:, 0:C * CAP].rearrange("p (c t) -> p c t", c=C)).then_inc(v_x, 1)

            def slot(i, n, back=True, ahead=True):
                e = R * i + n
                if ahead:
                    take_x(*following(i, n, R))
                dve.wait_ge(act_g, done(e))
                dve.wait_ge(pe_u, done(e))
                nc.vector.tensor_tensor(h[:, n % 2], gate[:, n % 2], pU[n % 2][:, 0:FC * CAP].rearrange("p (c t) -> p c t", c=FC),
                                        ALU.mult).then_inc(v_h, 1)

            take_x(0, 0)
            in_turns(dve, slot, NE // R, R)

        @block.tensor
        def _(pe):
            head_start(pe, pe_x, pe_g, pe_u, pe_o)

            def turn_x(i, n):
                pe.wait_ge(x_in[n], landed(i))
                for c in range(C):
                    last = nc.tensor.transpose(pX[n % 2][:, CAP * c:CAP * c + CAP], xe[:, n, P * c:P * c + P], ident[0:CAP, 0:CAP])
                last.then_inc(pe_x, 1)

            def up(ps, w, n, sem):
                for f in range(FC):
                    for c in range(C):
                        last = nc.tensor.matmul(ps[n % 2][:, CAP * f:CAP * f + CAP], w[:, n, c, P * f:P * f + P],
                                                xT[:, n % 2, c, :], start=c == 0, stop=c == C - 1)
                last.then_inc(sem, 1)

            def down(i, n):
                e = R * i + n
                pe.wait_ge(v_h, done(e))
                pe.wait_ge(act_y, done(e - 2))
                for f in range(FC):
                    last = nc.tensor.matmul(pO[n % 2][0:CAP, :], h[:, n % 2, f, :], wd[:, n, f, :], start=f == 0, stop=f == FC - 1)
                last.then_inc(pe_o, 1)

            def slot(i, n, back=True, ahead=True):
                e = R * i + n
                if ahead:
                    turn_x(*following(i, n, R))
                pe.wait_ge(w_in[n], 48 * (i + 1))
                pe.wait_ge(v_x, done(e))
                pe.wait_ge(act_g, done(e - 2))
                up(pG, wg, n, pe_g)
                pe.wait_ge(v_h, done(e - 2))
                up(pU, wu, n, pe_u)
                if back:
                    down(*preceding(i, n, R))

            turn_x(0, 0)
            in_turns(pe, slot, NE // R, R)
            down(NE // R - 1, R - 1)


def routed_experts(nc, psum, ident, packed, result, expert, w_dram, NT):
    NE, F, R = 8, 352, 4
    FC = 3
    rows = [P, P, F - 2 * P]
    with ExitStack() as ctx:
        st = Stage(nc, ctx, "n")
        pX, pH, pG, pU, pO = psum[0], psum[1], psum[2:4], psum[4:6], psum[6:8]
        xe = st.sbuf("xe", [P, R, D])
        wg = st.sbuf("wg", [P, R, C, F])
        wu = st.sbuf("wu", [P, R, C, F])
        wd = st.sbuf("wd", [P, R, FC, D])
        xT = st.sbuf("xT", [P, 2, C, P])
        gate = st.sbuf("gate", [P, 2, F])
        h = st.sbuf("h", [P, 2, F])
        hT = st.sbuf("hT", [P, 2, FC, P])
        ye = st.sbuf("ye", [P, R, D])
        x_in, w_in, d_in, y_out = ([st.sem(f"{s}{n}") for n in range(R)] for s in ("x_in", "w_in", "d_in", "y_out"))
        pe_x, pe_g, pe_u, pe_h, pe_o, act_x, act_g, act_h, v_y, v_h = st.sems(
            "pe_x", "pe_g", "pe_u", "pe_h", "pe_o", "act_x", "act_g", "act_h", "v_y", "v_h")
        block = ctx.enter_context(nc.Block())

        @block.sync
        def _(sp):
            def load(i, n, fresh):
                t = R * i + n
                e = sp.value_load(expert[0:1, bass.ds(t, 1)], min_val=0, max_val=NE - 1)
                sp.dma_start(xe[:, n, :], packed[t]).then_inc(x_in[n], 16)
                if not fresh:
                    sp.wait_ge(pe_u, done(t - R))
                sp.dma_start(wg[:, n], w_dram["wg"][e]).then_inc(w_in[n], 16)
                sp.dma_start(wu[:, n], w_dram["wu"][e]).then_inc(w_in[n], 16)
                if not fresh:
                    sp.wait_ge(pe_o, done(t - R))
                sp.dma_start(wd[:, n, 0:2], w_dram["wd01"][e]).then_inc(d_in[n], 16)
                sp.dma_start(wd[0:rows[2], n, 2], w_dram["wd2"][e]).then_inc(d_in[n], 16)

            def store(i, n):
                sp.wait_ge(v_y, done(R * i + n))
                sp.dma_start(result.rearrange("(t r) d -> t r d", r=P)[R * i + n], ye[:, n, :]).then_inc(y_out[n], 16)

            for n in range(R):
                sp.sem_inc(y_out[n], 16)
                load(0, n, True)
            with sp.Fori(0, NT // R - 1) as i:
                for n in range(R):
                    sp.wait_ge(pe_x, done(R * i + n))
                    load(i + 1, n, False)
                    store(i, n)
            for n in range(R):
                store(NT // R - 1, n)
            for n in range(R):
                sp.wait_ge(y_out[n], landed(NT // R))

        @block.scalar
        def _(act):
            head_start(act, act_x, act_g, act_h)

            def take_x(i, n):
                act.wait_ge(pe_x, done(R * i + n))
                nc.scalar.copy(xT[:, n % 2], pX[:, :]).then_inc(act_x, 1)

            def take_h(i, n):
                act.wait_ge(pe_h, done(R * i + n))
                nc.scalar.copy(hT[:, n % 2, 0:2], pH[:, 0:2 * P])
                nc.scalar.copy(hT[0:rows[2], n % 2, 2], pH[0:rows[2], 2 * P:3 * P]).then_inc(act_h, 1)

            def slot(i, n, back=True, ahead=True):
                t = R * i + n
                if ahead:
                    take_x(*following(i, n, R))
                act.wait_ge(pe_g, done(t))
                act.wait_ge(v_h, done(t - 2))
                nc.scalar.activation(gate[:, n % 2], pG[n % 2][:, 0:F], ACT.Silu).then_inc(act_g, 1)
                if back:
                    take_h(*preceding(i, n, R))

            take_x(0, 0)
            in_turns(act, slot, NT // R, R)
            take_h(NT // R - 1, R - 1)

        @block.vector
        def _(dve):
            head_start(dve, v_y, v_h)

            def take_y(i, n):
                dve.wait_ge(pe_o, done(R * i + n))
                dve.wait_ge(y_out[n], landed(i))
                nc.vector.tensor_copy(ye[:, n, :], pO[n % 2][:, :]).then_inc(v_y, 1)

            def slot(i, n, back=True, ahead=True):
                t = R * i + n
                dve.wait_ge(act_g, done(t))
                dve.wait_ge(pe_u, done(t))
                nc.vector.tensor_tensor(h[:, n % 2], gate[:, n % 2], pU[n % 2][:, 0:F], ALU.mult).then_inc(v_h, 1)
                if back:
                    take_y(*preceding(i, n, R))

            in_turns(dve, slot, NT // R, R)
            take_y(NT // R - 1, R - 1)

        @block.tensor
        def _(pe):
            head_start(pe, pe_x, pe_g, pe_u, pe_h, pe_o)

            def turn_x(i, n):
                pe.wait_ge(x_in[n], landed(i))
                pe.wait_ge(act_x, done(R * i + n - 1))
                for c in range(C):
                    last = nc.tensor.transpose(pX[:, P * c:P * c + P], xe[:, n, P * c:P * c + P], ident[:])
                last.then_inc(pe_x, 1)

            def turn_h(i, n):
                pe.wait_ge(v_h, done(R * i + n))
                pe.wait_ge(act_h, done(R * i + n - 1))
                for f in range(FC):
                    last = nc.tensor.transpose(pH[0:rows[f], P * f:P * f + P], h[:, n % 2, P * f:P * f + rows[f]], ident[:])
                last.then_inc(pe_h, 1)

            def up(ps, w, n, sem):
                for c in range(C):
                    last = nc.tensor.matmul(ps[n % 2][:, 0:F], xT[:, n % 2, c, :], w[:, n, c, :], start=c == 0, stop=c == C - 1)
                last.then_inc(sem, 1)

            def down(i, n):
                t = R * i + n
                pe.wait_ge(act_h, done(t))
                pe.wait_ge(d_in[n], 32 * (i + 1))
                pe.wait_ge(v_y, done(t - 2))
                for f in range(FC):
                    last = nc.tensor.matmul(pO[n % 2][:, :], hT[0:rows[f], n % 2, f, :], wd[0:rows[f], n, f, :], start=f == 0, stop=f == FC - 1)
                last.then_inc(pe_o, 1)

            def slot(i, n, back=True, ahead=True):
                t = R * i + n
                if ahead:
                    turn_x(*following(i, n, R))
                pe.wait_ge(w_in[n], 32 * (i + 1))
                pe.wait_ge(act_x, done(t))
                pe.wait_ge(act_g, done(t - 2))
                up(pG, wg, n, pe_g)
                if back:
                    turn_h(*preceding(i, n, R))
                pe.wait_ge(v_h, done(t - 2))
                up(pU, wu, n, pe_u)
                if back:
                    down(*preceding(i, n, R))

            turn_x(0, 0)
            in_turns(pe, slot, NT // R, R)
            turn_h(NT // R - 1, R - 1)
            down(NT // R - 1, R - 1)


def combine(nc, name, base, x_src, result, rows, weight, x_dst, K):
    R = 4
    with ExitStack() as ctx:
        st = Stage(nc, ctx, name)
        got = st.sbuf("got", [P, R, K, D])
        idx = st.sbuf("idx", [P, R, K], U32)
        acc = st.sbuf("acc", [P, R, D])
        yn = st.sbuf("yn", [P, R, D])
        xin = st.sbuf("xin", [P, R, D]) if base is None else None
        stats = st.sbuf("stats", [P, R, 6])
        mv = st.sbuf("mv", [P, R, 2])
        rstd = st.sbuf("rstd", [P, R])
        mhalf = st.sbuf("mhalf", [P, 1])
        eps = st.sbuf("eps", [P, 1])
        still, gstill = st.sbuf("still", [P, 1]), st.sbuf("gstill", [P, R])
        x_in, g_in, y_out = ([st.sem(f"{s}{n}") for n in range(R)] for s in ("x_in", "g_in", "y_out"))
        g_c, g_i, g_ve, g_rs, v_k, v_acc, v_st, v_mv, v_yn = st.sems("g_c", "g_i", "g_ve", "g_rs", "v_k", "v_acc", "v_st", "v_mv", "v_yn")
        block = ctx.enter_context(nc.Block())

        @block.sync
        def _(sp):
            for n in range(R):
                sp.sem_inc(y_out[n], 16)
                if base is None:
                    sp.dma_start(xin[:, n, :], x_src[n]).then_inc(x_in[n], 16)

            def store(i, n):
                sp.wait_ge(v_yn, done(R * i + n))
                sp.dma_start(x_dst[R * i + n], yn[:, n, :]).then_inc(y_out[n], 16)

            with sp.Fori(0, B // R - 1) as i:
                for n in range(R):
                    store(i, n)
                    if base is None:
                        sp.dma_start(xin[:, n, :], x_src[R * i + R + n]).then_inc(x_in[n], 16)
            for n in range(R):
                store(B // R - 1, n)
            for n in range(R):
                sp.wait_ge(y_out[n], landed(B // R))

        @block.gpsimd
        def _(pool):
            head_start(pool, g_i, g_ve, g_rs)
            nc.gpsimd.memset(mhalf[:], -0.5).then_inc(g_c, 1)
            nc.gpsimd.memset(eps[:], EPS).then_inc(g_c, 1)
            pool.wait_ge(g_c, 2)

            def gather(i, n):
                b = R * i + n
                pool.wait_ge(v_acc, done(b - R))
                nc.gpsimd.tensor_copy(idx[:, n], rows[:, b]).then_inc(g_i, 1)
                pool.wait_ge(g_i, done(b))
                nc.gpsimd.tensor_tensor(gstill[:, n:n + 1], mhalf[:], mhalf[:], ALU.add)
                for k in range(K):
                    nc.gpsimd.indirect_dma_start(got[:, n, k, :], None, result,
                                                 bass.IndirectOffsetOnAxis(ap=idx[:, n, k:k + 1], axis=0)).then_inc(g_in[n], 16)

            def norm(i, n):
                b = R * i + n
                pool.wait_ge(v_mv, done(b))
                nc.gpsimd.tensor_tensor(rstd[:, n:n + 1], mv[:, n, 1:2], eps[:], ALU.add).then_inc(g_ve, 1)
                pool.wait_ge(g_ve, done(b))
                nc.gpsimd.tensor_tensor(rstd[:, n:n + 1], rstd[:, n:n + 1], mhalf[:], ALU.pow).then_inc(g_rs, 1)

            for n in range(R):
                gather(0, n)
            with pool.Fori(0, B // R - 1) as i:
                for n in range(R):
                    norm(i, n)
                    gather(i + 1, n)
            for n in range(R):
                norm(B // R - 1, n)

        @block.vector
        def _(dve):
            head_start(dve, v_k, v_acc, v_st, v_mv, v_yn)

            def tile(i, n):
                b = R * i + n
                dve.wait_ge(g_in[n], 16 * K * (i + 1))
                dve.wait_ge(v_yn, done(b - R))
                if base is None:
                    dve.wait_ge(x_in[n], landed(i))
                for k in range(K):
                    if k:
                        dve.wait_ge(v_k, done((K - 1) * b + k - 1))
                    prev = acc[:, n] if k else (xin[:, n] if base is None else base[:, b])
                    ins = nc.vector.scalar_tensor_tensor(out=acc[:, n], in0=got[:, n, k, :], scalar=weight[:, b, k:k + 1], in1=prev,
                                                         op0=ALU.mult, op1=ALU.add)
                    ins.then_inc(v_k if k < K - 1 else v_acc, 1)
                dve.wait_ge(v_acc, done(b))
                nc.vector.bn_stats(stats[:, n], acc[:, n]).then_inc(v_st, 1)
                dve.wait_ge(v_st, done(b))
                carry_wait(nc.vector, still)
                nc.vector.bn_aggr(mv[:, n], stats[:, n]).then_inc(v_mv, 1)

            def normed(i, n):
                dve.wait_ge(g_rs, done(R * i + n))
                dve.wait_ge(y_out[n], landed(i))
                nc.vector.tensor_scalar(yn[:, n], acc[:, n], mv[:, n, 0:1], rstd[:, n:n + 1], ALU.subtract, ALU.mult).then_inc(v_yn, 1)

            tile(0, 0)
            with dve.Fori(0, B // R - 1) as i:
                for n in range(1, R):
                    tile(i, n)
                    normed(i, n - 1)
                tile(i + 1, 0)
                normed(i, R - 1)
            for n in range(1, R):
                tile(B // R - 1, n)
                normed(B // R - 1, n - 1)
            normed(B // R - 1, R - 1)


def logits_only(nc, psum, ident, x_src, w_dram, logits, NE):
    R = 4
    with ExitStack() as ctx:
        st = Stage(nc, ctx, "r")
        pX, pL = psum[0:2], psum[2:4]
        xin = st.sbuf("xin", [P, R, D])
        xT = st.sbuf("xT", [P, 2, C, P])
        rw = st.sbuf("rw", [P, C, NE])
        x_in = [st.sem(f"x_in{n}") for n in range(R)]
        w_in, pe_x, pe_l, act_x, v_l = st.sems("w_in", "pe_x", "pe_l", "act_x", "v_l")
        block = ctx.enter_context(nc.Block())

        @block.sync
        def _(sp):
            sp.dma_start(rw[:], w_dram["rw"]).then_inc(w_in, 16)
            for n in range(R):
                sp.dma_start(xin[:, n, :], x_src[n]).then_inc(x_in[n], 16)
            with sp.Fori(0, B // R - 1) as i:
                for n in range(R):
                    sp.wait_ge(pe_x, done(R * i + n))
                    sp.dma_start(xin[:, n, :], x_src[R * i + R + n]).then_inc(x_in[n], 16)

        @block.scalar
        def _(act):
            head_start(act, act_x)
            with act.Fori(0, B // 2) as i:
                for n in range(2):
                    act.wait_ge(pe_x, done(2 * i + n))
                    act.wait_ge(pe_l, done(2 * i + n - 2))
                    nc.scalar.copy(xT[:, n], pX[n][:, :]).then_inc(act_x, 1)

        @block.vector
        def _(dve):
            head_start(dve, v_l)
            with dve.Fori(0, B // 2) as i:
                for n in range(2):
                    dve.wait_ge(pe_l, done(2 * i + n))
                    nc.vector.tensor_copy(logits[:, 2 * i + n, :], pL[n][:, 0:NE]).then_inc(v_l, 1)

        @block.tensor
        def _(pe):
            head_start(pe, pe_x, pe_l)

            def turn_x(i, n):
                pe.wait_ge(x_in[n], landed(i))
                pe.wait_ge(act_x, done(R * i + n - 2))
                for c in range(C):
                    last = nc.tensor.transpose(pX[n % 2][:, P * c:P * c + P], xin[:, n, P * c:P * c + P], ident[:])
                last.then_inc(pe_x, 1)

            def slot(i, n, back=True, ahead=True):
                b = R * i + n
                if ahead:
                    turn_x(*following(i, n, R))
                pe.wait_ge(act_x, done(b))
                pe.wait_ge(v_l, done(b - 2))
                for c in range(C):
                    last = nc.tensor.matmul(pL[n % 2][:, 0:NE], xT[:, n % 2, c, :], rw[:, c, :], start=c == 0, stop=c == C - 1)
                last.then_inc(pe_l, 1)

            pe.wait_ge(w_in, 16)
            turn_x(0, 0)
            in_turns(pe, slot, B // R, R)


NT2 = (2 * B * P + 7 * (P - 1)) // P + 1
NT2 += -NT2 % 4


def decoder(nc, x, ctxT, c, out):
    def scratch(name, rows):
        return nc.dram_tensor(name, [rows, D], F32, kind="Internal").ap()

    xs = [scratch(f"x{n}", B * P).rearrange("(b p) d -> b p d", p=P) for n in range(1, 6)]
    packed1, result1 = scratch("packed1", 32 * 80), scratch("result1", 32 * 80 + 1)
    packed2, result2 = scratch("packed2", NT2 * P), scratch("result2", NT2 * P)

    def of(prefix):
        return {n[2:]: a for n, a in c.items() if n.startswith(prefix)}

    with ExitStack() as ctx:
        st = Stage(nc, ctx, "all")
        psum = [ctx.enter_context(nc.psum_tensor(f"bank{n}", [P, 512], F32)) for n in range(8)]
        ident, tri, ones = (st.sbuf(n, [P, P]) for n in ("ident", "tri", "ones"))
        zero = st.sbuf("zero", [P, D])
        c_in, zeroed, packed_out, g_z = st.sems("c_in", "zeroed", "packed_out", "g_z")
        with nc.Block() as block:
            @block.sync
            def _(sp):
                sp.dma_start(ident[:], c["ident"]).then_inc(c_in, 16)
                sp.dma_start(tri[:], c["tri"]).then_inc(c_in, 16)
                sp.dma_start(ones[:], c["ones"]).then_inc(c_in, 16)
                sp.wait_ge(g_z, 1)
                for packed in (packed1, packed2):
                    n = packed.shape[0] // P
                    sp.dma_start(packed.rearrange("(p n) d -> p n d", p=P), zero[:].unsqueeze(1).to_broadcast([P, n, D])).then_inc(packed_out, 16)
                sp.wait_ge(c_in, 48)

            @block.gpsimd
            def _(pool):
                nc.gpsimd.memset(zero[:], 0.0).then_inc(g_z, 1)

        zeroed_rows = [(packed_out, 32)]
        wide_attention(nc, "a", psum, ident, x, xs[0], of("a_"), rope=True)
        narrow_attention(nc, "b", psum, ident, lambda b: xs[0][b], lambda b: xs[1][b], {**of("b_"), "ctxT": ctxT}, 32,
                         EVENTS_8, rope=True)
        with ExitStack() as moe:
            sc = Stage(nc, moe, "moe1")
            base, logits = sc.sbuf("base", [P, B, D]), sc.sbuf("logits", [P, B, 32])
            weight, rows = sc.sbuf("weight", [P, B, 4]), sc.sbuf("rows", [P, B, 4], U32)
            w = of("c_")
            shared_expert(nc, psum, ident, xs[1], w, base, logits, 32)
            route(nc, "cr", psum, tri, ones, logits, w, 32, 4, weight, rows, None, True)
            dispatch(nc, "cd", xs[1], rows, packed1, 4, 32 * 80 - 1, zeroed_rows)
            capped_experts(nc, psum, ident, packed1.rearrange("(e r) d -> e r d", r=80), result1, zero, w)
            combine(nc, "cc", base, None, result1, rows, weight, xs[2], 4)
        steps = [t.rearrange("l (j n) d -> j l n d", n=8) for t in (xs[2], xs[3])]
        narrow_attention(nc, "d", psum, ident, lambda b: steps[0][b], lambda b: steps[1][b], of("d_"), 16, EVENTS_4, causal=True)
        wide_attention(nc, "e", psum, ident, xs[3], xs[4], {**of("e_"), "ctxT": ctxT}, rms=True)
        with ExitStack() as moe:
            sc = Stage(nc, moe, "moe2")
            logits = sc.sbuf("logits", [P, B, 8])
            weight, rows = sc.sbuf("weight", [P, B, 2]), sc.sbuf("rows", [P, B, 2], U32)
            expert = sc.sbuf("expert", [P, NT2], I32)
            w = of("f_")
            logits_only(nc, psum, ident, xs[4], w, logits, 8)
            route(nc, "fr", psum, tri, ones, logits, w, 8, 2, weight, rows, {"tiles": NT2, "expert": expert}, False)
            dispatch(nc, "fd", xs[4], rows, packed2, 2, NT2 * P - 1, [])
            routed_experts(nc, psum, ident, packed2.rearrange("(t r) d -> t r d", r=P), result2, expert, w, NT2)
            combine(nc, "fc", None, xs[4], result2, rows, weight, out, 2)


def rope_tables():
    inv = (np.float32(1.0) / np.power(np.float32(10000.0), np.arange(0, 128, 2, dtype=np.float32) / np.float32(128))).astype(np.float32)
    ang = np.outer(np.arange(P, dtype=np.float32), inv).astype(np.float32)
    c, s = np.cos(ang), np.sin(ang)
    cos, sin = np.concatenate([c, c], 1), np.concatenate([-s, s], 1)
    scale = np.float32(1.0 / np.sqrt(128.0))
    return {"cosq": cos * scale, "sinq": sin * scale, "cosk": cos, "sink": sin}


def causal_mask():
    i = np.arange(P)
    return np.where(i[None, :] <= i[:, None], 0.0, NEG).astype(np.float32)


def by_chunk(w):
    return np.ascontiguousarray(w.reshape(-1, P, w.shape[1]).transpose(1, 0, 2))


def pairs_apart(w, groups):
    r, c = w.shape
    return w.reshape(r, groups, -1, 2).transpose(0, 1, 3, 2).reshape(r, c)


def layout_l0_attn(i):
    flat = {n: i[f"L0_attn_W_{n}"].transpose(1, 0, 2).reshape(D, -1) for n in "QKV"}
    out = {
        "a_wq": by_chunk(pairs_apart(flat["Q"], 16)), "a_wk": by_chunk(pairs_apart(flat["K"], 16)),
        "a_wv": by_chunk(flat["V"]), "a_wo": np.ascontiguousarray(i["L0_attn_W_O"].transpose(1, 0, 2)),
        "a_bq": pairs_apart(i["L0_attn_b_Q"].reshape(1, -1), 16)[0], "a_bk": pairs_apart(i["L0_attn_b_K"].reshape(1, -1), 16)[0],
        "a_bv": i["L0_attn_b_V"].reshape(-1), "a_bo": i["L0_attn_b_O"], "a_mask": causal_mask(),
    }
    out.update({"a_" + n: t.astype(np.float32) for n, t in rope_tables().items()})
    return out


def layout_l1_xattn(i):
    return {
        "e_wq": by_chunk(i["L1_xattn_Wq"]), "e_wk": by_chunk(i["L1_xattn_Wk"]), "e_wv": by_chunk(i["L1_xattn_Wv"]),
        "e_wo": by_chunk(i["L1_xattn_Wo"]), "e_gq": i["L1_xattn_gq"], "e_gk": i["L1_xattn_gk"],
    }


def layout_shared(i):
    return {"x": i["x"], "ctxT": np.ascontiguousarray(i["ctx_1024"].reshape(B, P, 2, P).transpose(3, 0, 2, 1)),
            "ident": np.eye(P, dtype=np.float32)}


def layout_l0_xattn(i):
    wk, wv = i["L0_xattn_Wkv"][:, :D], i["L0_xattn_Wkv"][:, D:]
    freq = np.power(np.float32(10000.0), -np.arange(4, dtype=np.float32) / np.float32(4)).astype(np.float32)
    return {
        "b_wq": by_chunk(pairs_apart(i["L0_xattn_Wq"], 32)), "b_wk": by_chunk(pairs_apart(wk, 32)), "b_wv": by_chunk(wv),
        "b_wo": by_chunk(i["L0_xattn_Wout"]), "b_bo": i["L0_xattn_bout"],
        "b_pos": np.ascontiguousarray(i["fside_BxSx2_0"].transpose(1, 0, 2).reshape(P, 2 * B)),
        "b_freq": np.ascontiguousarray(np.broadcast_to(freq, (P, 4))),
    }


def layout_l1_attn(i):
    w = i["L1_attn_weight_qkv"]
    r = np.arange(P)
    seen = (r[None, :] % 8 == r[:, None] % 8) & (r[None, :] // 8 <= r[:, None] // 8)
    return {
        "d_wq": by_chunk(w[:D].T), "d_wk": by_chunk(w[D:2 * D].T), "d_wv": by_chunk(w[2 * D:].T),
        "d_wo": by_chunk(i["L1_attn_weight_out"].T), "d_mask": np.where(seen, 0.0, NEG).astype(np.float32),
    }


def layout_moe(i):
    def by_expert(w):
        return np.ascontiguousarray(w.reshape(w.shape[0], -1, P, w.shape[2]).transpose(0, 2, 1, 3))

    down = i["L1_ffn_down_proj"].transpose(0, 2, 1)
    iota = np.ascontiguousarray(np.broadcast_to(np.arange(P, dtype=np.float32), (P, P)))
    return {
        "c_rw": by_chunk(i["L0_ffn_router_w"].T), "c_sg": by_chunk(i["L0_ffn_shared_gate"].T),
        "c_su": by_chunk(i["L0_ffn_shared_up"].T), "c_sd": by_chunk(i["L0_ffn_shared_down"].T),
        "c_bias": i["L0_ffn_e_bias"], "c_iota": iota, "c_wg": by_expert(i["L0_ffn_W_gate"]), "c_wu": by_expert(i["L0_ffn_W_up"]),
        "c_wd": by_expert(i["L0_ffn_W_down"]),
        "f_rw": by_chunk(i["L1_ffn_gate_w"].T), "f_iota": iota, "f_wg": by_expert(i["L1_ffn_gate_proj"].transpose(0, 2, 1)),
        "f_wu": by_expert(i["L1_ffn_up_proj"].transpose(0, 2, 1)), "f_wd01": by_expert(down[:, :2 * P]),
        "f_wd2": np.ascontiguousarray(down[:, 2 * P:]),
        "tri": np.triu(np.ones((P, P), np.float32), 1), "ones": np.ones((P, P), np.float32),
    }


def kernel(**inputs):
    import concourse.bacc as bacc
    from concourse.bass_utils import run_bass_kernel_spmd

    i = {n: np.asarray(a) for n, a in inputs.items()}
    arrays = layout_shared(i)
    for part in (layout_l0_attn, layout_l0_xattn, layout_moe, layout_l1_attn, layout_l1_xattn):
        arrays.update(part(i))
    nc = bacc.Bacc("TRN2", target_bir_lowering=False, num_devices=1)
    arrays = {"in_" + n: np.ascontiguousarray(a) for n, a in arrays.items()}
    aps = {n[3:]: nc.dram_tensor(n, a.shape, mybir.dt.from_np(a.dtype), kind="ExternalInput").ap() for n, a in arrays.items()}
    out = nc.dram_tensor("out", (B, P, D), F32, kind="ExternalOutput").ap()
    decoder(nc, aps["x"], aps["ctxT"], aps, out)
    return run_bass_kernel_spmd(nc, [arrays], core_ids=[0]).results[0]["out"]
```

```python
from contextlib import ExitStack

import numpy as np

import concourse.bass as bass
from concourse import mybir
from concourse.alu_op_type import AluOpType

F32 = mybir.dt.float32
F32R = mybir.dt.float32r
I32 = mybir.dt.int32
U32 = mybir.dt.uint32
ALU = mybir.AluOpType
ACT = mybir.ActivationFunctionType
AX = mybir.AxisListType

P = 128
D = 512
C = D // P
B = 16
EPS = 1e-5
LEAD = 4
NEG = -1e30


def done(n):
    return n + 1 + LEAD


def landed(n):
    return 16 * (n + 1)


class Stage:

    def __init__(self, nc, ctx, name):
        self.nc, self.ctx, self.name, self.used = nc, ctx, name, []
        ctx.callback(self.clear)

    def clear(self):
        if self.used:
            self.nc.clear_and_free_semaphores(self.used)
            self.nc.all_engine_barrier()

    def sbuf(self, name, shape, dt=F32):
        return self.ctx.enter_context(self.nc.sbuf_tensor(f"{self.name}_{name}", shape, dt))

    def sem(self, name):
        self.used.append(self.nc.alloc_semaphore(f"{self.name}_{name}"))
        return self.used[-1]

    def sems(self, *names):
        return [self.sem(n) for n in names]


def head_start(engine, *sems):
    for s in sems:
        engine.sem_inc(s, LEAD)


def carry_wait(engine, still):
    engine.memset(still[:], 0.0)


def heads(ap, n):
    return ap.rearrange("p (h d) -> p h d", h=n)


def split_product(nc, ps, a_hi, a_lo, b_hi, b_lo, start=True, stop=True):
    nc.tensor.matmul(ps, a_lo, b_hi, start=start, stop=False)
    nc.tensor.matmul(ps, a_hi, b_lo, start=False, stop=False)
    return nc.tensor.matmul(ps, a_hi, b_hi, start=False, stop=stop)


def wide_attention(nc, name, psum, ident, x_src, x_dst, w_dram, rope=None, rms=None):
    G, H = 4, 4
    KC = C if rope else w_dram["ctxT"].shape[2]
    KINDS = "qkvo"
    with ExitStack() as ctx:
        st = Stage(nc, ctx, name)
        pQ, pK, pV, pA, pB, pS, pP, pO = psum

        rows_of = {"q": C, "k": KC, "v": KC, "o": H}
        raw = st.sbuf("raw", [P, 3, C, D])
        RAW = {"q": 0, "k": 1, "v": 2, "o": 0}
        hi = {n: st.sbuf(f"w{n}_hi", [P, rows_of[n], D], F32R) for n in KINDS}
        lo = {n: st.sbuf(f"w{n}_lo", [P, rows_of[n], D], F32R) for n in KINDS}
        xin = st.sbuf("xin", [P, D])
        xall = st.sbuf("xall", [P, B, D])
        x_hi = st.sbuf("x_hi", [P, 2, C, P], F32R)
        x_lo = st.sbuf("x_lo", [P, 2, C, P], F32R)
        yall = st.sbuf("yall", [P, B, D])
        tq = st.sbuf("tq", [P, D])
        tk = st.sbuf("tk", [P, D])
        sq = st.sbuf("sq", [P, D])
        sk = st.sbuf("sk", [P, D])
        kr = st.sbuf("kr", [P, D])
        qT = st.sbuf("qT", [P, H, P])
        kT = st.sbuf("kT", [P, H, P])
        v = st.sbuf("v", [P, 2, D])
        probT = st.sbuf("probT", [P, H, P])
        zn = st.sbuf("zn", [P, D])
        z_hi = st.sbuf("z_hi", [P, H, P], F32R)
        z_lo = st.sbuf("z_lo", [P, H, P], F32R)
        stats = st.sbuf("stats", [P, 6])
        mv = st.sbuf("mv", [P, 2])
        rstd = st.sbuf("rstd", [P, 1])
        mhalf = st.sbuf("mhalf", [P, H])
        eps = st.sbuf("eps", [P, 1])
        still, idle = st.sbuf("still", [P, 1]), st.sbuf("idle", [P, 1])
        nmax = st.sbuf("nmax", [P, H])
        rsum = st.sbuf("rsum", [P, H])
        rinv = st.sbuf("rinv", [P, H])
        if rope:
            qr = st.sbuf("qr", [P, D])
            prob = sm = st.sbuf("sm", [P, H, P])
            bias = {n: st.sbuf("b" + n, [P, D]) for n in "qkv"}
            bo = st.sbuf("bo", [P, D])
            tab = {n: st.sbuf(n, [P, P]) for n in ("cosq", "sinq", "cosk", "sink", "mask")}
            s_hi, s_lo = x_hi, x_lo
        else:
            prob = st.sbuf("prob", [P, H, P])
            qr = tq
            src = st.sbuf("ctxT", [P, KC, P])
            s_hi = st.sbuf("s_hi", [P, 2, KC, P], F32R)
            s_lo = st.sbuf("s_lo", [P, 2, KC, P], F32R)
            g2 = st.sbuf("g2", [P, 2, P])
            gg = st.sbuf("gg", [P, P])
            ssq = st.sbuf("ssq", [P, H])
            ssk = st.sbuf("ssk", [P, H])
            rq = st.sbuf("rq", [P, 2, H])
            rk = st.sbuf("rk", [P, H])
            nb = st.sbuf("nb", [P, H])
            epsn = st.sbuf("epsn", [P, H])

        c_in, x_in, y_in, ctx_in, b_in, out_st = st.sems("c_in", "x_in", "y_in", "ctx_in", "b_in", "out_st")
        raw_in = st.sems("raw_in0", "raw_in1", "raw_in2")
        w_hi = {n: st.sem(f"hi_{n}") for n in KINDS}
        w_lo = {n: st.sem(f"lo_{n}") for n in KINDS}
        pe_x, pe_q, pe_k, pe_v = st.sems("pe_x", "pe_q", "pe_k", "pe_v")
        pe_qt, pe_kt, pe_s, pe_pt, pe_z, pe_zt, pe_o = st.sems("pe_qt", "pe_kt", "pe_s", "pe_pt", "pe_z", "pe_zt", "pe_o")
        pe_used = {"q": pe_q, "k": pe_k, "v": pe_v, "o": pe_o}
        act_x, act_qt, act_kt, act_e, act_zt, act_pt, act_hi = st.sems(
            "act_x", "act_qt", "act_kt", "act_e", "act_zt", "act_pt", "act_hi")
        v_tq, v_tk, v_q, v_k, v_v = st.sems("v_tq", "v_tk", "v_q", "v_k", "v_v")
        v_aq, v_ak, v_sm, v_nm, v_nb, v_ri, v_z, v_zl = st.sems("v_aq", "v_ak", "v_sm", "v_nm", "v_nb", "v_ri", "v_z", "v_zl")
        v_y, v_st, v_mv, v_yn = st.sems("v_y", "v_st", "v_mv", "v_yn")
        g_q, g_k, g_mq, g_mk, g_rq, g_rk, g_x, g_c, g_ve, g_rs, g_lo = st.sems(
            "g_q", "g_k", "g_mq", "g_mk", "g_rq", "g_rk", "g_x", "g_c", "g_ve", "g_rs", "g_lo")

        n_const = 6 if rope else 2
        block = ctx.enter_context(nc.Block())

        def each_unit(engine, slot, finish=None):
            for g in range(G):
                slot(g, 0, 0, first=g == 0)
                slot(g, 1, 1)
                with engine.Fori(0, B // 2 - 2) as i:
                    for n in range(2):
                        slot(g, 2 * i + 2 + n, n)
                slot(g, B - 2, 0)
                slot(g, B - 1, 1, last=g == G - 1)

        def ends(b):
            return isinstance(b, int) and b == B - 1

        def before_last(b):
            return not (isinstance(b, int) and b >= B - 2)

        def split_hi(engine, copy, n, g):
            if g > 0:
                engine.wait_ge(pe_used[n], done(B * g - 1))
            engine.wait_ge(raw_in[RAW[n]], landed({"q": 2 * g, "o": 2 * g + 1}.get(n, g)))
            copy(hi[n][:], raw[:, RAW[n], 0:rows_of[n], :]).then_inc(w_hi[n], 1)

        def split_lo(engine, tensor_tensor, n, g):
            engine.wait_ge(w_hi[n], g + 1)
            tensor_tensor(lo[n][:], raw[:, RAW[n], 0:rows_of[n], :], hi[n][:].bitcast(F32), ALU.subtract).then_inc(w_lo[n], 1)

        def is_batch(b, n):
            return isinstance(b, int) and b == n

        @block.sync
        def _(sp):
            def weights(n, g):
                if g or n == "o":
                    sp.wait_ge(w_lo[{"q": "o", "o": "q"}.get(n, n)], g + 1 if n == "o" else g)
                w = w_dram["w" + n]
                part = w[:, H * g:H * g + H] if n == "o" else w[:, :, D * g:D * g + D]
                sp.dma_start(raw[:, RAW[n], 0:rows_of[n], :], part).then_inc(raw_in[RAW[n]], 16)

            def context(u, b):
                if rms:
                    sp.wait_ge(g_lo, done(u - 1))
                    sp.dma_start(src[:], w_dram["ctxT"][:, b]).then_inc(ctx_in, 16)

            def biases(g):
                if rope:
                    for n in "qkv":
                        sp.dma_start(bias[n][:], w_dram["b" + n][D * g:D * g + D].partition_broadcast(P)).then_inc(b_in, 16)

            def slot(g, b, par, first=False, last=False):
                u = B * g + b
                if g == 0 and before_last(b):
                    sp.wait_ge(pe_x, done(b + 1))
                    sp.dma_start(xin[:], x_src[b + 2]).then_inc(x_in, 16)
                if first:
                    weights("o", 0)
                    sp.dma_start(yall[:], x_src.rearrange("b p d -> p b d")).then_inc(y_in, 16)
                if before_last(b):
                    context(u + 2, b + 2)
                elif g < G - 1:
                    context(u + 2, b + 2 - B)
                if is_batch(b, 1) and g < G - 1:
                    for n in "qkv":
                        weights(n, g + 1)
                if ends(b) and g < G - 1:
                    if rope:
                        sp.wait_ge(v_v, done(u))
                    biases(g + 1)
                    weights("o", g + 1)
                if g == G - 1 and not is_batch(b, 0) and not is_batch(b, 1):
                    store(b - 2)

            def store(b):
                sp.wait_ge(v_yn, done(b))
                sp.dma_start(x_dst[b], yall[:, b, :]).then_inc(out_st, 16)

            sp.dma_start(xin[:], x_src[0]).then_inc(x_in, 16)
            context(0, 0)
            weights("q", 0)
            biases(0)
            sp.wait_ge(pe_x, done(0))
            sp.dma_start(xin[:], x_src[1]).then_inc(x_in, 16)
            weights("k", 0)
            context(1, 1)
            weights("v", 0)
            each_unit(sp, slot)
            store(B - 2)
            store(B - 1)
            sp.wait_ge(out_st, 16 * B)

        @block.scalar
        def _(act):
            head_start(act, act_x, act_qt, act_kt, act_e, act_zt, act_pt, act_hi)
            if rope:
                for n in tab:
                    act.dma_start(tab[n][:], w_dram[n]).then_inc(c_in, 16)
                act.dma_start(bo[:], w_dram["bo"].partition_broadcast(P)).then_inc(c_in, 16)
            else:
                act.dma_start(g2[:, 0, :], w_dram["gq"].partition_broadcast(P)).then_inc(c_in, 16)
                act.dma_start(g2[:, 1, :], w_dram["gk"].partition_broadcast(P)).then_inc(c_in, 16)

            def take_x(b):
                act.wait_ge(pe_x, done(b))
                nc.scalar.copy(xall[:, b, :], pP[:, :]).then_inc(act_x, 1)

            def source(g, b, par):
                u = B * g + b
                act.wait_ge(act_x, done(b) if g == 0 else done(B - 1))
                act.wait_ge(pe_v, done(u - 2))
                nc.scalar.copy(idle[:], ident[:, 0:1])
                copy = nc.scalar.copy(x_hi[:, par], xall[:, b, :])
                if rms:
                    act.wait_ge(ctx_in, landed(u))
                    copy = nc.scalar.copy(s_hi[:, par], src[:])
                copy.then_inc(act_hi, 1)

            def take_prob_z(u):
                act.wait_ge(pe_zt, done(u))
                act.wait_ge(pe_o, done(u - 1))
                nc.scalar.copy(z_hi[:], pB[:, :]).then_inc(act_zt, 1)

            def slot(g, b, par, first=False, last=False):
                u = B * g + b
                if is_batch(b, 1) and g > 0:
                    split_hi(act, nc.scalar.copy, "o", g)
                if not last:
                    source(g + 1 if ends(b) else g, 0 if ends(b) else b + 1, 1 - par)
                act.wait_ge(pe_qt, done(u))
                nc.scalar.copy(qT[:], pA[:, :]).then_inc(act_qt, 1)
                act.wait_ge(pe_kt, done(u))
                nc.scalar.copy(kT[:], pB[:, :]).then_inc(act_kt, 1)
                if ends(b) and not last:
                    split_hi(act, nc.scalar.copy, "v", g + 1)
                if g == 0 and before_last(b):
                    take_x(b + 2)
                if rope:
                    act.wait_ge(v_nm, done(u))
                    for j in range(H):
                        step = nc.scalar.activation(prob[:, j, :], sm[:, j, :], ACT.Exp, bias=nmax[:, j:j + 1],
                                                    accum_out=rsum[:, j:j + 1])
                else:
                    act.wait_ge(v_nb, done(u))
                    for j in range(H):
                        step = nc.scalar.activation(prob[:, j, :], pS[:, P * j:P * j + P], ACT.Exp,
                                                    bias=nb[:, j:j + 1], scale=rq[:, par, j:j + 1],
                                                    accum_out=rsum[:, j:j + 1])
                step.then_inc(act_e, 1)
                if not first:
                    take_prob_z(u - 1)
                act.wait_ge(pe_pt, done(u))
                nc.scalar.copy(probT[:], pP[:, :]).then_inc(act_pt, 1)
                if is_batch(b, B - 2) and g < G - 1:
                    split_hi(act, nc.scalar.copy, "q", g + 1)

            take_x(0)
            source(0, 0, 0)
            take_x(1)
            for n in "qvo":
                split_hi(act, nc.scalar.copy, n, 0)
            each_unit(act, slot)
            take_prob_z(G * B - 1)

        @block.gpsimd
        def _(pool):
            head_start(pool, g_q, g_k, g_mq, g_mk, g_rq, g_rk, g_x, g_ve, g_rs, g_lo)
            nc.gpsimd.memset(mhalf[:], -0.5).then_inc(g_c, 1)
            nc.gpsimd.memset(eps[:], EPS).then_inc(g_c, 1)
            pool.wait_ge(g_c, 2)

            def source(g, b, par):
                pool.wait_ge(act_hi, done(B * g + b))
                sub = nc.gpsimd.tensor_tensor(x_lo[:, par].rearrange("p c t -> p (c t)"), xall[:, b, :],
                                              x_hi[:, par].rearrange("p c t -> p (c t)").bitcast(F32), ALU.subtract)
                if rms:
                    sub = nc.gpsimd.tensor_tensor(s_lo[:, par], src[:], s_hi[:, par].bitcast(F32), ALU.subtract)
                sub.then_inc(g_lo, 1)

            def turned(out, t, sin):
                for half in range(2):
                    o = heads(out[:], H)[:, :, 64 * half:64 * half + 64]
                    i = heads(t[:], H)[:, :, 64 - 64 * half:128 - 64 * half]
                    s = tab[sin][:, 64 * half:64 * half + 64].unsqueeze(1).to_broadcast([P, H, 64])
                    step = nc.gpsimd.tensor_tensor(o, i, s, ALU.mult)
                return step

            def project(u, par):
                if rope:
                    pool.wait_ge(v_tq, done(u))
                    pool.wait_ge(v_q, done(u - 1))
                    turned(sq, tq, "sinq").then_inc(g_q, 1)
                    pool.wait_ge(v_tk, done(u))
                    pool.wait_ge(v_k, done(u - 1))
                    turned(sk, tk, "sink").then_inc(g_k, 1)
                    return
                pool.wait_ge(v_tk, done(u))
                nc.gpsimd.tensor_tensor(sk[:], tk[:], tk[:], ALU.mult).then_inc(g_k, 1)
                pool.wait_ge(v_tq, done(u))
                nc.gpsimd.tensor_tensor(sq[:], tq[:], tq[:], ALU.mult).then_inc(g_q, 1)
                pool.wait_ge(v_ak, done(u))
                nc.gpsimd.tensor_tensor(rk[:], ssk[:], epsn[:], ALU.add).then_inc(g_mk, 1)
                pool.wait_ge(g_mk, done(u))
                nc.gpsimd.tensor_tensor(rk[:], rk[:], mhalf[:], ALU.pow).then_inc(g_rk, 1)
                pool.wait_ge(v_aq, done(u))
                nc.gpsimd.tensor_tensor(rq[:, par, :], ssq[:], epsn[:], ALU.add).then_inc(g_mq, 1)
                pool.wait_ge(g_mq, done(u))
                nc.gpsimd.tensor_tensor(rq[:, par, :], rq[:, par, :], mhalf[:], ALU.pow).then_inc(g_rq, 1)

            def residual(b):
                if rope:
                    nc.gpsimd.tensor_tensor(yall[:, b, :], yall[:, b, :], bo[:], ALU.add).then_inc(g_x, 1)

            def norm(b):
                pool.wait_ge(v_mv, done(b))
                nc.gpsimd.tensor_tensor(rstd[:], mv[:, 1:2], eps[:], ALU.add).then_inc(g_ve, 1)
                pool.wait_ge(g_ve, done(b))
                nc.gpsimd.tensor_tensor(rstd[:], rstd[:], mhalf[:, 0:1], ALU.pow).then_inc(g_rs, 1)

            def slot(g, b, par, first=False, last=False):
                u = B * g + b
                if not last:
                    source(g + 1 if ends(b) else g, 0 if ends(b) else b + 1, 1 - par)
                if g == G - 1 and not is_batch(b, 0) and not is_batch(b, 1):
                    norm(b - 2)
                if is_batch(b, 1) and g > 0:
                    split_lo(pool, nc.gpsimd.tensor_tensor, "o", g)
                if ends(b) and not last:
                    split_lo(pool, nc.gpsimd.tensor_tensor, "v", g + 1)
                if not last:
                    project(u + 1, 1 - par)
                if first:
                    pool.wait_ge(y_in, 16)
                if g == 0:
                    residual(b)

            source(0, 0, 0)
            split_lo(pool, nc.gpsimd.tensor_tensor, "v", 0)
            pool.wait_ge(c_in, 16 * n_const)
            if rms:
                nc.gpsimd.memset(epsn[:], EPS * P).then_inc(g_c, 1)
                nc.gpsimd.tensor_tensor(gg[:], g2[:, 0, :], g2[:, 1, :], ALU.mult).then_inc(g_c, 1)
                pool.wait_ge(g_c, 4)
                nc.gpsimd.tensor_scalar(gg[:], gg[:], float(np.sqrt(P)), 0.0, ALU.mult, ALU.add).then_inc(g_c, 1)
            project(0, 0)
            split_lo(pool, nc.gpsimd.tensor_tensor, "o", 0)
            each_unit(pool, slot)
            norm(B - 2)
            norm(B - 1)

        @block.vector
        def _(dve):
            head_start(dve, v_tq, v_tk, v_q, v_k, v_v, v_aq, v_ak, v_sm, v_nm, v_nb, v_ri, v_z, v_zl, v_y, v_st, v_mv, v_yn)

            def rotate(u, ps, t, a, out, bcol, cos, t_sem, a_sem, g_sem, o_sem):
                nc.vector.tensor_tensor(t[:], ps[:, :], bcol, ALU.add).then_inc(t_sem, 1)
                dve.wait_ge(t_sem, done(u))
                c = tab[cos][:].unsqueeze(1).to_broadcast([P, H, P])
                nc.vector.tensor_tensor(heads(a[:], H), heads(t[:], H), c, ALU.mult).then_inc(a_sem, 1)
                dve.wait_ge(a_sem, done(u))
                return a

            def project(g, b, par, u_z=None):
                u = B * g + b
                if rope:
                    dve.wait_ge(pe_q, done(u))
                    if is_batch(b, 0):
                        dve.wait_ge(b_in, 48 * (g + 1))
                    rotate(u, pQ, tq, qr, qr, bias["q"][:], "cosq", v_tq, v_aq, g_q, v_q)
                    dve.wait_ge(g_q, done(u))
                    nc.vector.tensor_tensor(qr[:], qr[:], sq[:], ALU.add).then_inc(v_q, 1)
                    dve.wait_ge(pe_k, done(u))
                    rotate(u, pK, tk, kr, kr, bias["k"][:], "cosk", v_tk, v_ak, g_k, v_k)
                    dve.wait_ge(g_k, done(u))
                    nc.vector.tensor_tensor(kr[:], kr[:], sk[:], ALU.add).then_inc(v_k, 1)
                    if u_z is not None:
                        take_z_lo(u_z)
                    dve.wait_ge(pe_v, done(u))
                    nc.vector.tensor_tensor(v[:, par, :], pV[:, :], bias["v"][:], ALU.add).then_inc(v_v, 1)
                    return
                dve.wait_ge(pe_k, done(u))
                nc.vector.tensor_copy(tk[:], pK[:, :]).then_inc(v_tk, 1)
                dve.wait_ge(pe_q, done(u))
                nc.vector.tensor_copy(tq[:], pQ[:, :]).then_inc(v_tq, 1)
                dve.wait_ge(g_k, done(u))
                nc.vector.tensor_reduce(ssk[:], heads(sk[:], H), AX.X, ALU.add).then_inc(v_ak, 1)
                if u_z is not None:
                    take_z_lo(u_z)
                dve.wait_ge(g_q, done(u))
                nc.vector.tensor_reduce(ssq[:], heads(sq[:], H), AX.X, ALU.add).then_inc(v_aq, 1)
                dve.wait_ge(pe_v, done(u))
                nc.vector.tensor_copy(v[:, par, :], pV[:, :]).then_inc(v_v, 1)
                dve.wait_ge(g_rk, done(u))
                for j in range(H):
                    step = nc.vector.scalar_tensor_tensor(
                        out=kr[:, P * j:P * j + P], in0=tk[:, P * j:P * j + P], scalar=rk[:, j:j + 1], in1=gg[:],
                        op0=ALU.mult, op1=ALU.mult)
                step.then_inc(v_k, 1)

            def take_z(u):
                dve.wait_ge(pe_z, done(u))
                nc.vector.reciprocal(rinv[:], rsum[:]).then_inc(v_ri, 1)
                dve.wait_ge(v_ri, done(u))
                nc.vector.tensor_tensor(heads(zn[:], H), heads(pA[:, :], H), rinv[:].unsqueeze(2).to_broadcast([P, H, P]),
                                        ALU.mult).then_inc(v_z, 1)

            def take_z_lo(u):
                dve.wait_ge(act_zt, done(u))
                dve.wait_ge(pe_o, done(u - 1))
                nc.vector.tensor_tensor(z_lo[:], heads(pB[:, :], H), z_hi[:].bitcast(F32), ALU.subtract).then_inc(v_zl, 1)

            def add_output(g, b):
                u = B * g + b
                dve.wait_ge(pe_o, done(u))
                if g == 0:
                    if rope:
                        dve.wait_ge(g_x, done(b))
                    elif is_batch(b, 0):
                        dve.wait_ge(y_in, 16)
                nc.vector.tensor_tensor(yall[:, b, :], pO[:, :], yall[:, b, :], ALU.add).then_inc(v_y, 1)
                if g == G - 1:
                    dve.wait_ge(v_y, done(u))
                    carry_wait(nc.vector, still)
                    nc.vector.bn_stats(stats[:], yall[:, b, :]).then_inc(v_st, 1)
                    dve.wait_ge(v_st, done(b))
                    carry_wait(nc.vector, still)
                    nc.vector.bn_aggr(mv[:], stats[:]).then_inc(v_mv, 1)

            def normed(b):
                dve.wait_ge(g_rs, done(b))
                nc.vector.tensor_scalar(yall[:, b, :], yall[:, b, :], mv[:, 0:1], rstd[:], ALU.subtract, ALU.mult).then_inc(v_yn, 1)

            def slot(g, b, par, first=False, last=False):
                u = B * g + b
                inner = not is_batch(b, 0)
                if not first:
                    take_z(u - 1)
                dve.wait_ge(pe_s, done(u))
                if rope:
                    nc.vector.tensor_tensor(sm[:], heads(pS[:, :], H), tab["mask"][:].unsqueeze(1).to_broadcast([P, H, P]),
                                            ALU.add).then_inc(v_sm, 1)
                    dve.wait_ge(v_sm, done(u))
                    nc.vector.tensor_reduce(nmax[:], sm[:], AX.X, ALU.max, negate=True).then_inc(v_nm, 1)
                else:
                    nc.vector.tensor_reduce(nmax[:], heads(pS[:, :], H), AX.X, ALU.max, negate=True).then_inc(v_nm, 1)
                    dve.wait_ge(v_nm, done(u))
                    dve.wait_ge(g_rq, done(u))
                    nc.vector.tensor_tensor(nb[:], nmax[:], rq[:, par, :], ALU.mult).then_inc(v_nb, 1)
                if g == G - 1 and not is_batch(b, 0) and not is_batch(b, 1):
                    normed(b - 2)
                if not last:
                    project(g + 1 if ends(b) else g, 0 if ends(b) else b + 1, 1 - par, None if first else u - 1)
                if not first:
                    if last:
                        take_z_lo(u - 1)
                    add_output(g if inner else g - 1, b - 1 if inner else B - 1)
                if is_batch(b, B - 2) and g < G - 1:
                    split_lo(dve, nc.vector.tensor_tensor, "q", g + 1)
                    split_hi(dve, nc.vector.tensor_copy, "k", g + 1)
                    split_lo(dve, nc.vector.tensor_tensor, "k", g + 1)

            split_lo(dve, nc.vector.tensor_tensor, "q", 0)
            split_hi(dve, nc.vector.tensor_copy, "k", 0)
            split_lo(dve, nc.vector.tensor_tensor, "k", 0)
            dve.wait_ge(c_in, 16 * n_const)
            if rms:
                dve.wait_ge(g_c, 5)
            project(0, 0, 0)
            each_unit(dve, slot)
            normed(B - 2)
            take_z(G * B - 1)
            take_z_lo(G * B - 1)
            add_output(G - 1, B - 1)
            normed(B - 1)

        @block.tensor
        def _(pe):
            head_start(pe, pe_x, pe_q, pe_k, pe_v, pe_qt, pe_kt, pe_s, pe_pt, pe_z, pe_zt, pe_o)

            def turn_x(b):
                pe.wait_ge(x_in, landed(b))
                for c in range(C):
                    step = nc.tensor.transpose(pP[:, P * c:P * c + P], xin[:, P * c:P * c + P], ident[:])
                step.then_inc(pe_x, 1)

            def ready(n, g, b):
                if is_batch(b, 0):
                    pe.wait_ge(w_lo[n], g + 1)

            def project(n, ps, a_hi, a_lo, g, b, par, sem):
                ready(n, g, b)
                for c in range(rows_of[n]):
                    step = split_product(nc, ps[:, :], a_hi[:, par, c, :], a_lo[:, par, c, :], hi[n][:, c, :], lo[n][:, c, :],
                                         start=c == 0, stop=c == rows_of[n] - 1)
                step.then_inc(sem, 1)

            def project_qk(g, b, par):
                for n in "qk" if rope else "kq":
                    if n == "q":
                        project("q", pQ, x_hi, x_lo, g, b, par, pe_q)
                    else:
                        project("k", pK, s_hi, s_lo, g, b, par, pe_k)

            def turn_q(u):
                pe.wait_ge(v_q if rope else v_tq, done(u))
                pe.wait_ge(v_z, done(u - 2))
                for j in range(H):
                    step = nc.tensor.transpose(pA[:, P * j:P * j + P], qr[:, P * j:P * j + P], ident[:])
                step.then_inc(pe_qt, 1)

            def turn_k(u):
                pe.wait_ge(v_k, done(u))
                pe.wait_ge(v_zl, done(u - 2))
                for j in range(H):
                    step = nc.tensor.transpose(pB[:, P * j:P * j + P], kr[:, P * j:P * j + P], ident[:])
                step.then_inc(pe_kt, 1)

            def probs_v(u, par):
                pe.wait_ge(act_pt, done(u))
                pe.wait_ge(v_v, done(u))
                for j in range(H):
                    step = nc.tensor.matmul(pA[:, P * j:P * j + P], probT[:, j, :], v[:, par, P * j:P * j + P],
                                            start=True, stop=True)
                step.then_inc(pe_z, 1)

            def turn_z(u):
                pe.wait_ge(v_z, done(u))
                for j in range(H):
                    step = nc.tensor.transpose(pB[:, P * j:P * j + P], zn[:, P * j:P * j + P], ident[:])
                step.then_inc(pe_zt, 1)

            def output(g, b):
                u = B * g + b
                pe.wait_ge(v_zl, done(u))
                pe.wait_ge(v_y, done(u - 1))
                ready("o", g, b)
                for j in range(H):
                    step = split_product(nc, pO[:, :], z_hi[:, j, :], z_lo[:, j, :], hi["o"][:, j, :], lo["o"][:, j, :],
                                         start=j == 0, stop=j == H - 1)
                step.then_inc(pe_o, 1)

            def slot(g, b, par, first=False, last=False):
                u = B * g + b
                ng, nb_ = (g + 1, 0) if ends(b) else (g, b + 1)
                if g == 0 and before_last(b):
                    pe.wait_ge(act_pt, done(u - 1))
                    turn_x(b + 2)
                pe.wait_ge(act_qt, done(u))
                if not first:
                    probs_v(u - 1, 1 - par)
                pe.wait_ge(act_kt, done(u))
                for j in range(H):
                    step = nc.tensor.matmul(pS[:, P * j:P * j + P], qT[:, j, :], kT[:, j, :], start=True, stop=True)
                step.then_inc(pe_s, 1)
                if not last:
                    pe.wait_ge(g_lo, done(u + 1))
                    project_qk(ng, nb_, 1 - par)
                if not first:
                    turn_z(u - 1)
                if not last:
                    pe.wait_ge(v_v, done(u))
                    project("v", pV, s_hi, s_lo, ng, nb_, 1 - par, pe_v)
                pe.wait_ge(act_e, done(u))
                for j in range(H):
                    step = nc.tensor.transpose(pP[:, P * j:P * j + P], prob[:, j, :], ident[:])
                step.then_inc(pe_pt, 1)
                if not last:
                    turn_q(u + 1)
                if not last and rope:
                    turn_k(u + 1)
                if not first:
                    inner = not is_batch(b, 0)
                    output(g if inner else g - 1, b - 1 if inner else B - 1)
                if not last and rms:
                    turn_k(u + 1)

            turn_x(0)
            pe.wait_ge(act_x, done(0))
            turn_x(1)
            pe.wait_ge(g_lo, done(0))
            project_qk(0, 0, 0)
            project("v", pV, s_hi, s_lo, 0, 0, 0, pe_v)
            turn_q(0)
            turn_k(0)
            each_unit(pe, slot)
            u = G * B - 1
            probs_v(u, 1)
            turn_z(u)
            output(G - 1, B - 1)


def narrow_attention(nc, name, psum, ident, x_src, x_dst, w_dram, NH, events, rope=False, causal=False):
    DH = D // NH
    H = 4
    UN = NH // H
    W = 32
    NBLK = NH * W // P
    ROUNDS = NBLK // 4
    HB = NH // 2
    KC = C if causal else w_dram["ctxT"].shape[2]
    SCALE = float(1.0 / np.sqrt(float(DH)))
    with ExitStack() as ctx:
        st = Stage(nc, ctx, name)
        pJ, pT, pS0, pS1, pP, pO, pZ0, pZ1 = psum
        pS, pZ = (pS0, pS1), (pZ0, pZ1)

        wq = st.sbuf("wq", [P, C, D])
        wk = st.sbuf("wk", [P, KC, D])
        wv = st.sbuf("wv", [P, KC, D])
        wo = st.sbuf("wo", [P, C, D])
        xin = st.sbuf("xin", [P, D])
        xres = st.sbuf("xres", [P, D])
        xT = st.sbuf("xT", [P, C, P])
        qs = st.sbuf("qs", [P, NH, W])
        ks = st.sbuf("ks", [P, NH, W])
        qT = st.sbuf("qT", [P, 2, NBLK, P])
        kT = st.sbuf("kT", [P, 2, NBLK, P])
        va = st.sbuf("va", [P, 2, NH, DH + 1])
        nmax = st.sbuf("nmax", [P, 2, H])
        low = st.sbuf("low", [P, 2, H, P])
        prob = st.sbuf("prob", [P, 2, H, P])
        probT = st.sbuf("probT", [P, 2, H, P])
        zn = st.sbuf("zn", [P, D])
        zT = st.sbuf("zT", [P, C, P])
        rinv = st.sbuf("rinv", [P, 2, HB])
        y = st.sbuf("y", [P, D])
        yn = st.sbuf("yn", [P, D])
        stats = st.sbuf("stats", [P, 6])
        mv = st.sbuf("mv", [P, 2])
        rstd = st.sbuf("rstd", [P, 1])
        mhalf = st.sbuf("mhalf", [P, 1])
        eps = st.sbuf("eps", [P, 1])
        still = st.sbuf("still", [P, 1])
        if causal:
            sm = st.sbuf("sm", [P, 2, H, P])
            mask = st.sbuf("mask", [P, P])
        if rope:
            srcT = st.sbuf("ctxT", [P, KC, P])
            bo = st.sbuf("bo", [P, D])
            pos = st.sbuf("pos", [P, 2 * B])
            freq = st.sbuf("freq", [P, 4])
            ang = st.sbuf("ang", [P, 2, 8 * B])
            turns = st.sbuf("turns", [P, 2, 8 * B])
            tab = st.sbuf("tab", [P, 3, B, 8])
            tc = {n: st.sbuf("tc" + n, [P, D]) for n in "qk"}
            ts = {n: st.sbuf("ts" + n, [P, D]) for n in "qk"}
        else:
            srcT = xT

        c_in, x_in, r_in, ctx_in, out_st = st.sems("c_in", "x_in", "r_in", "ctx_in", "out_st")
        w_in = st.sems("wq_in", "wk_in", "wv_in", "wo_in")
        pe_x, pe_q, pe_k, pe_v, pe_t, pe_s, pe_pt, pe_z, pe_zt, pe_o = st.sems(
            "pe_x", "pe_q", "pe_k", "pe_v", "pe_t", "pe_s", "pe_pt", "pe_z", "pe_zt", "pe_o")
        act_x, act_v, act_t, act_e, act_pt, act_zt, act_tab = st.sems("act_x", "act_v", "act_t", "act_e", "act_pt", "act_zt", "act_tab")
        v_q, v_k, v_sm, v_nm, v_low, v_ri, v_z, v_y, v_st, v_mv, v_yn, v_tab = st.sems(
            "v_q", "v_k", "v_sm", "v_nm", "v_low", "v_ri", "v_z", "v_y", "v_st", "v_mv", "v_yn", "v_tab")
        g_c, g_q, g_k, g_low, g_x, g_ve, g_rs = st.sems("g_c", "g_q", "g_k", "g_low", "g_x", "g_ve", "g_rs")
        q_ready, k_ready = (g_q, g_k) if rope else (v_q, v_k)
        low_ready = g_low if causal else v_low

        n_const = 16 * (3 if rope else 1)
        block = ctx.enter_context(nc.Block())

        def each_batch(engine, slot):
            for s in range(UN):
                slot(0, s, 0, back=False)
            with engine.Fori(0, B // 2 - 1) as i:
                for par in (1, 0):
                    for s in range(UN):
                        slot(2 * i + 2 - par, s, par)
            for s in range(UN):
                slot(B - 1, s, 1, ahead=False)

        @block.sync
        def _(sp):
            sp.sem_inc(out_st, 16)
            sp.dma_start(xin[:], x_src(0)).then_inc(x_in, 16)
            if rope:
                sp.dma_start(srcT[:], w_dram["ctxT"][:, 0]).then_inc(ctx_in, 16)
            for n, t, s in zip("qkvo", (wq, wk, wv, wo), w_in):
                sp.dma_start(t[:], w_dram["w" + n]).then_inc(s, 16)
            sp.dma_start(xres[:], x_src(0)).then_inc(r_in, 16)

            def next_tiles(b):
                sp.wait_ge(pe_x, done(b))
                sp.dma_start(xin[:], x_src(b + 1)).then_inc(x_in, 16)
                if rope:
                    sp.wait_ge(pe_v, done(b))
                    sp.dma_start(srcT[:], w_dram["ctxT"][:, b + 1]).then_inc(ctx_in, 16)

            def store(b):
                sp.wait_ge(v_yn, done(b))
                sp.dma_start(x_dst(b), yn[:]).then_inc(out_st, 16)

            def next_residual(b):
                sp.wait_ge(v_y, done(b))
                sp.dma_start(xres[:], x_src(b + 1)).then_inc(r_in, 16)

            next_tiles(0)
            with sp.Fori(0, B - 2) as b:
                next_tiles(b + 1)
                next_residual(b)
                store(b)
            next_residual(B - 2)
            store(B - 2)
            store(B - 1)
            sp.wait_ge(out_st, landed(B))

        @block.scalar
        def _(act):
            head_start(act, act_x, act_v, act_t, act_e, act_pt, act_zt)
            if rope:
                act.dma_start(pos[:], w_dram["pos"]).then_inc(c_in, 16)
                act.dma_start(freq[:], w_dram["freq"]).then_inc(c_in, 16)
                act.dma_start(bo[:], w_dram["bo"].partition_broadcast(P)).then_inc(c_in, 16)
                act.wait_ge(v_tab, 8)
                nc.scalar.activation(tab[:, 1].rearrange("p b f -> p (b f)"), ang[:, 0], ACT.Sin).then_inc(act_tab, 1)
                nc.scalar.activation(tab[:, 0].rearrange("p b f -> p (b f)"), ang[:, 1], ACT.Sin).then_inc(act_tab, 1)
            else:
                act.dma_start(mask[:], w_dram["mask"]).then_inc(c_in, 16)

            def take_x(b):
                act.wait_ge(pe_x, done(b))
                nc.scalar.copy(xT[:], pJ[:, :]).then_inc(act_x, 1)

            def take_v(b, par):
                act.wait_ge(pe_v, done(b))
                nc.scalar.copy(va[:, par, :, 0:DH], heads(pJ[:, :], NH)).then_inc(act_v, 1)

            def take_t(b, par, n):
                act.wait_ge(pe_t, done(2 * ROUNDS * b + n))
                t, r = (qT, n) if n < ROUNDS else (kT, n - ROUNDS)
                nc.scalar.copy(t[:, par, 4 * r:4 * r + 4, :], pT[:, :]).then_inc(act_t, 1)

            def take_prob(u, s):
                act.wait_ge(pe_pt, done(u))
                nc.scalar.copy(probT[:, s % 2], pP[:, :]).then_inc(act_pt, 1)

            def slot(b, s, par, back=True, ahead=True):
                u = UN * b + s
                if back or s >= 2:
                    take_prob(u - 2, s)
                act.wait_ge(low_ready, done(u))
                nc.scalar.activation(prob[:, s % 2], low[:, s % 2], ACT.Exp, scale=SCALE).then_inc(act_e, 1)
                for e in events[s]:
                    if e == "x" and ahead:
                        take_x(b + 1)
                    if e == "v" and ahead:
                        take_v(b + 1, 1 - par)
                    if e == "zt" and back:
                        act.wait_ge(pe_zt, done(b - 1))
                        nc.scalar.copy(zT[:], pT[:, :]).then_inc(act_zt, 1)
                    if isinstance(e, int) and ahead:
                        take_t(b + 1, 1 - par, e)

            take_x(0)
            take_v(0, 0)
            for n in range(2 * ROUNDS):
                take_t(0, 0, n)
            each_batch(act, slot)
            take_prob(UN * B - 2, 0)
            take_prob(UN * B - 1, 1)
            act.wait_ge(pe_zt, done(B - 1))
            nc.scalar.copy(zT[:], pT[:, :]).then_inc(act_zt, 1)

        @block.gpsimd
        def _(pool):
            head_start(pool, g_q, g_k, g_low, g_x, g_ve, g_rs)
            nc.gpsimd.memset(mhalf[:], -0.5).then_inc(g_c, 1)
            nc.gpsimd.memset(va[:], 1.0).then_inc(g_c, 1)
            nc.gpsimd.memset(eps[:], EPS).then_inc(g_c, 1)
            if rope:
                nc.gpsimd.memset(qs[:], 0.0).then_inc(g_c, 1)
                nc.gpsimd.memset(ks[:], 0.0).then_inc(g_c, 1)
            pool.wait_ge(g_c, 5 if rope else 3)
            pool.wait_ge(c_in, n_const)

            def rotated(b):
                for t, o, v_sem, g_sem in (("q", qs, v_q, g_q), ("k", ks, v_k, g_k)):
                    pool.wait_ge(v_sem, done(b))
                    nc.gpsimd.tensor_tensor(o[:, :, 0:DH], heads(tc[t][:], NH), heads(ts[t][:], NH), ALU.add).then_inc(g_sem, 1)

            def residual(b):
                if rope:
                    pool.wait_ge(r_in, landed(b))
                    nc.gpsimd.tensor_tensor(xres[:], xres[:], bo[:], ALU.add).then_inc(g_x, 1)

            def norm(b):
                pool.wait_ge(v_mv, done(b))
                nc.gpsimd.tensor_tensor(rstd[:], mv[:, 1:2], eps[:], ALU.add).then_inc(g_ve, 1)
                pool.wait_ge(g_ve, done(b))
                nc.gpsimd.tensor_tensor(rstd[:], rstd[:], mhalf[:], ALU.pow).then_inc(g_rs, 1)

            def slot(b, s, par, back=True, ahead=True):
                u = UN * b + s
                if causal:
                    pool.wait_ge(v_nm, done(u))
                    pool.wait_ge(act_e, done(u - 2))
                    nc.gpsimd.tensor_tensor(low[:, s % 2], sm[:, s % 2], nmax[:, s % 2].unsqueeze(2).to_broadcast([P, H, P]),
                                            ALU.add).then_inc(g_low, 1)
                for e in events[s]:
                    if e == "k" and ahead and rope:
                        rotated(b + 1)
                    if e == "o" and back:
                        norm(b - 1)
                        residual(b)

            if rope:
                rotated(0)
            residual(0)
            each_batch(pool, slot)
            norm(B - 1)

        @block.vector
        def _(dve):
            head_start(dve, v_q, v_k, v_sm, v_nm, v_low, v_ri, v_z, v_y, v_st, v_mv, v_yn)
            dve.wait_ge(c_in, n_const)
            if rope:
                two_pi = 2 * np.pi
                hi = float(np.float32(6.28125))
                lo = float(np.float32(two_pi - hi))
                magic = 12582912.0
                nc.vector.tensor_tensor(ang[:, 0].rearrange("p (n f) -> p n f", f=4), pos[:].unsqueeze(2).to_broadcast([P, 2 * B, 4]),
                                        freq[:].unsqueeze(1).to_broadcast([P, 2 * B, 4]), ALU.mult).then_inc(v_tab, 1)
                dve.wait_ge(v_tab, 1)
                nc.vector.tensor_scalar(ang[:, 1], ang[:, 0], float(np.pi / 2), None, ALU.add).then_inc(v_tab, 1)
                dve.wait_ge(v_tab, 2)
                nc.vector.tensor_scalar(turns[:], ang[:], float(1 / two_pi), magic, ALU.mult, ALU.add).then_inc(v_tab, 1)
                dve.wait_ge(v_tab, 3)
                nc.vector.tensor_scalar(turns[:], turns[:], -magic, None, ALU.add).then_inc(v_tab, 1)
                dve.wait_ge(v_tab, 4)
                nc.vector.scalar_tensor_tensor(out=ang[:], in0=turns[:], scalar=-hi, in1=ang[:], op0=ALU.mult, op1=ALU.add).then_inc(v_tab, 1)
                dve.wait_ge(v_tab, 5)
                nc.vector.scalar_tensor_tensor(out=ang[:], in0=turns[:], scalar=-lo, in1=ang[:], op0=ALU.mult, op1=ALU.add).then_inc(v_tab, 1)
                dve.wait_ge(v_tab, 6)
                nc.vector.tensor_scalar(ang[:], ang[:], 3.1415925, -3.1415925, ALU.min, ALU.max).then_inc(v_tab, 2)
                dve.wait_ge(act_tab, 2)
                nc.vector.tensor_scalar(tab[:, 2], tab[:, 1], -1.0, None, ALU.mult).then_inc(v_tab, 1)
                dve.wait_ge(v_tab, 9)

            def take(b, ps, t, out, pe_sem, v_sem):
                dve.wait_ge(pe_sem, done(b))
                if not rope:
                    nc.vector.tensor_copy(out[:].rearrange("p h w -> p (h w)"), ps[:, :]).then_inc(v_sem, 1)
                    return
                nc.vector.tensor_tensor(tc[t][:].rearrange("p (n f) -> p n f", f=8), ps[:, :].rearrange("p (n f) -> p n f", f=8),
                                        tab[:, 0, b].unsqueeze(1).to_broadcast([P, 2 * NH, 8]), ALU.mult)
                for half in range(2):
                    o = heads(ts[t][:], NH)[:, :, 8 * half:8 * half + 8]
                    i = heads(ps[:, :], NH)[:, :, 8 - 8 * half:16 - 8 * half]
                    last = nc.vector.tensor_tensor(o, i, tab[:, 2 - half, b].unsqueeze(1).to_broadcast([P, NH, 8]), ALU.mult)
                last.then_inc(v_sem, 1)

            def take_z(b):
                dve.wait_ge(pe_z, done(UN * b + UN - 1))
                for n in range(2):
                    z = pZ[n][:, 0:HB * (DH + 1)].rearrange("p (h d) -> p h d", h=HB)
                    last = nc.vector.reciprocal(rinv[:, n], z[:, :, DH])
                last.then_inc(v_ri, 1)
                dve.wait_ge(v_ri, done(b))
                for n in range(2):
                    z = pZ[n][:, 0:HB * (DH + 1)].rearrange("p (h d) -> p h d", h=HB)
                    last = nc.vector.tensor_tensor(heads(zn[:, n * D // 2:(n + 1) * D // 2], HB), z[:, :, 0:DH],
                                                   rinv[:, n].unsqueeze(2).to_broadcast([P, HB, DH]), ALU.mult)
                last.then_inc(v_z, 1)

            def norm(b):
                dve.wait_ge(pe_o, done(b))
                if rope:
                    dve.wait_ge(g_x, done(b))
                else:
                    dve.wait_ge(r_in, landed(b))
                nc.vector.tensor_tensor(y[:], pO[:, :], xres[:], ALU.add).then_inc(v_y, 1)
                dve.wait_ge(v_y, done(b))
                nc.vector.bn_stats(stats[:], y[:]).then_inc(v_st, 1)
                dve.wait_ge(v_st, done(b))
                carry_wait(nc.vector, still)
                nc.vector.bn_aggr(mv[:], stats[:]).then_inc(v_mv, 1)

            def normed(b):
                dve.wait_ge(g_rs, done(b))
                dve.wait_ge(out_st, landed(b))
                nc.vector.tensor_scalar(yn[:], y[:], mv[:, 0:1], rstd[:], ALU.subtract, ALU.mult).then_inc(v_yn, 1)

            def slot(b, s, par, back=True, ahead=True):
                u = UN * b + s
                dve.wait_ge(pe_s, done(u))
                nb = nmax[:, s % 2].unsqueeze(2).to_broadcast([P, H, P])
                if causal:
                    dve.wait_ge(g_low, done(u - 2))
                    nc.vector.tensor_tensor(sm[:, s % 2], heads(pS[s % 2][:, :], H), mask[:].unsqueeze(1).to_broadcast([P, H, P]),
                                            ALU.add).then_inc(v_sm, 1)
                    dve.wait_ge(v_sm, done(u))
                    nc.vector.tensor_reduce(nmax[:, s % 2], sm[:, s % 2], AX.X, ALU.max, negate=True).then_inc(v_nm, 1)
                else:
                    nc.vector.tensor_reduce(nmax[:, s % 2], heads(pS[s % 2][:, :], H), AX.X, ALU.max, negate=True).then_inc(v_nm, 1)
                    dve.wait_ge(v_nm, done(u))
                    dve.wait_ge(act_e, done(u - 2))
                    nc.vector.tensor_tensor(low[:, s % 2], heads(pS[s % 2][:, :], H), nb, ALU.add).then_inc(v_low, 1)
                if s == 2 and back:
                    take_z(b - 1)
                for e in events[s]:
                    if e == "q" and ahead:
                        take(b + 1, pJ, "q", qs, pe_q, v_q)
                    if e == "k" and ahead:
                        take(b + 1, pJ, "k", ks, pe_k, v_k)
                    if e == "o" and back:
                        norm(b - 1)
                    if e == "n" and back:
                        normed(b - 1)

            if rope:
                dve.wait_ge(g_c, 5)
            take(0, pJ, "q", qs, pe_q, v_q)
            take(0, pJ, "k", ks, pe_k, v_k)
            each_batch(dve, slot)
            take_z(B - 1)
            norm(B - 1)
            normed(B - 1)

        @block.tensor
        def _(pe):
            head_start(pe, pe_x, pe_q, pe_k, pe_v, pe_t, pe_s, pe_pt, pe_z, pe_zt, pe_o)

            def turn_x(b):
                pe.wait_ge(x_in, landed(b))
                pe.wait_ge(act_v, done(b - 1))
                for c in range(C):
                    last = nc.tensor.transpose(pJ[:, P * c:P * c + P], xin[:, P * c:P * c + P], ident[:])
                last.then_inc(pe_x, 1)

            def project(w, lhs, n, sem):
                for c in range(n):
                    last = nc.tensor.matmul(pJ[:, :], lhs[:, c, :], w[:, c, :], start=c == 0, stop=c == n - 1)
                last.then_inc(sem, 1)

            def project_q(b):
                pe.wait_ge(act_x, done(b))
                project(wq, xT, C, pe_q)

            def project_k(b):
                if rope:
                    pe.wait_ge(ctx_in, landed(b))
                pe.wait_ge(v_q, done(b))
                project(wk, srcT, KC, pe_k)

            def project_v(b):
                pe.wait_ge(v_k, done(b))
                project(wv, srcT, KC, pe_v)

            def turn(b, n):
                src, r = (qs, n) if n < ROUNDS else (ks, n - ROUNDS)
                pe.wait_ge(q_ready if n < ROUNDS else k_ready, done(b))
                pe.wait_ge(act_t, done(2 * ROUNDS * b + n - 1))
                pe.wait_ge(act_zt, done(b - 2))
                flat = src[:].rearrange("p h w -> p (h w)")
                for j in range(4):
                    last = nc.tensor.transpose(pT[:, P * j:P * j + P], flat[:, P * (4 * r + j):P * (4 * r + j + 1)], ident[:])
                last.then_inc(pe_t, 1)

            def place(s, j):
                r, block_ = s % 4, 4 * (s // 4) + j
                return 4 * block_ + r, slice(W * r, W * r + W), block_

            def turn_prob(u, s):
                pe.wait_ge(act_e, done(u))
                pe.wait_ge(act_pt, done(u - 1))
                for j in range(H):
                    last = nc.tensor.transpose(pP[:, P * j:P * j + P], prob[:, s % 2, j, :], ident[:])
                last.then_inc(pe_pt, 1)

            def probs_v(u, b, s, par):
                pe.wait_ge(act_pt, done(u))
                if s == 0:
                    pe.wait_ge(act_v, done(b))
                    pe.wait_ge(v_z, done(b - 1))
                for j in range(H):
                    h = place(s, j)[0]
                    col = (h % HB) * (DH + 1)
                    last = nc.tensor.matmul(pZ[h // HB][:, col:col + DH + 1], probT[:, s % 2, j, :], va[:, par, h, :],
                                            start=True, stop=True)
                last.then_inc(pe_z, 1)

            def turn_z(b):
                pe.wait_ge(v_z, done(b))
                pe.wait_ge(act_t, done(2 * ROUNDS * (b + 1) + 2 * ROUNDS - 1))
                for c in range(C):
                    last = nc.tensor.transpose(pT[:, P * c:P * c + P], zn[:, P * c:P * c + P], ident[:])
                last.then_inc(pe_zt, 1)

            def output(b):
                pe.wait_ge(act_zt, done(b))
                pe.wait_ge(v_y, done(b - 1))
                for c in range(C):
                    last = nc.tensor.matmul(pO[:, :], zT[:, c, :], wo[:, c, :], start=c == 0, stop=c == C - 1)
                last.then_inc(pe_o, 1)

            def slot(b, s, par, back=True, ahead=True):
                u = UN * b + s
                early = "zt" not in events[s]
                if s == 0:
                    pe.wait_ge(act_t, done(2 * ROUNDS * b + 2 * ROUNDS - 1))
                pe.wait_ge(v_sm if causal else v_low, done(u - 2))
                for j in range(H):
                    _, rows, blk = place(s, j)
                    last = nc.tensor.matmul(pS[s % 2][:, P * j:P * j + P], qT[rows, par, blk, :], kT[rows, par, blk, :],
                                            start=True, stop=True)
                last.then_inc(pe_s, 1)
                if early:
                    for e in events[s]:
                        if isinstance(e, int) and ahead:
                            turn(b + 1, e)
                if back or s >= 2:
                    turn_prob(u - 2, s)
                if back or s >= 3:
                    s3 = (s - 3) % UN
                    here = s >= 3
                    probs_v(u - 3, b if here else b - 1, s3, par if here else 1 - par)
                for e in events[s]:
                    if ahead:
                        if e == "x":
                            turn_x(b + 1)
                        if e == "q":
                            project_q(b + 1)
                        if e == "k":
                            project_k(b + 1)
                        if e == "v":
                            project_v(b + 1)
                        if isinstance(e, int) and not early:
                            turn(b + 1, e)
                    if back:
                        if e == "zt":
                            turn_z(b - 1)
                        if e == "o":
                            output(b - 1)

            turn_x(0)
            pe.wait_ge(w_in[0], 16)
            project_q(0)
            pe.wait_ge(w_in[1], 16)
            project_k(0)
            pe.wait_ge(w_in[2], 16)
            pe.wait_ge(g_c, 3)
            project_v(0)
            for n in range(2 * ROUNDS):
                turn(0, n)
            pe.wait_ge(w_in[3], 16)
            each_batch(pe, slot)
            last_u = UN * B - 1
            turn_prob(last_u - 1, 0)
            probs_v(last_u - 2, B - 1, UN - 3, 1)
            turn_prob(last_u, 1)
            probs_v(last_u - 1, B - 1, UN - 2, 1)
            probs_v(last_u, B - 1, UN - 1, 1)
            pe.wait_ge(v_z, done(B - 1))
            for c in range(C):
                last = nc.tensor.transpose(pT[:, P * c:P * c + P], zn[:, P * c:P * c + P], ident[:])
            last.then_inc(pe_zt, 1)
            output(B - 1)


EVENTS_8 = [["x"], [], ["q"], ["zt", "k", "o", 0], [1], [2, "n", "v"], [3], []]
EVENTS_4 = [[], ["x"], ["q"], ["zt", "k", 0, "o", 1, "n", "v"]]


class Chain:

    def __init__(self, engine, sem):
        self.engine, self.sem, self.n = engine, sem, 0

    def __call__(self, ins):
        self.n += 1
        ins.then_inc(self.sem, 1)
        self.engine.wait_ge(self.sem, self.n)


def in_turns(engine, slot, rounds, ring):
    slot(0, 0, back=False)
    with engine.Fori(0, rounds - 1) as i:
        for n in range(1, ring):
            slot(i, n)
        slot(i + 1, 0)
    for n in range(1, ring):
        slot(rounds - 1, n, ahead=n < ring - 1)


def following(i, n, ring):
    return (i, n + 1) if n < ring - 1 else (i + 1, 0)


def preceding(i, n, ring):
    return (i, n - 1) if n else (i - 1, ring - 1)


def shared_expert(nc, psum, ident, x_src, w_dram, base, logits, NE):
    R = 4
    with ExitStack() as ctx:
        st = Stage(nc, ctx, "c")
        pX, pG, pU, pL, pO = psum[0:5]
        wg, wu, wd = (st.sbuf(n, [P, C, D]) for n in ("wg", "wu", "wd"))
        rw = st.sbuf("rw", [P, C, NE])
        xin = st.sbuf("xin", [P, R, D])
        xT = st.sbuf("xT", [P, 2, C, P])
        gate = st.sbuf("gate", [P, C, P])
        h = st.sbuf("h", [P, C, P])
        x_in = [st.sem(f"x_in{n}") for n in range(R)]
        w_in, wd_in, pe_x, pe_l, pe_g, pe_u, pe_o = st.sems("w_in", "wd_in", "pe_x", "pe_l", "pe_g", "pe_u", "pe_o")
        act_x, act_g, act_l, v_h, v_b = st.sems("act_x", "act_g", "act_l", "v_h", "v_b")
        block = ctx.enter_context(nc.Block())

        @block.sync
        def _(sp):
            def load(i, n):
                sp.dma_start(xin[:, n, :], x_src[R * i + n]).then_inc(x_in[n], 16)

            load(0, 0)
            sp.dma_start(rw[:], w_dram["rw"]).then_inc(w_in, 16)
            sp.dma_start(wg[:], w_dram["sg"]).then_inc(w_in, 16)
            sp.dma_start(wu[:], w_dram["su"]).then_inc(w_in, 16)
            sp.dma_start(wd[:], w_dram["sd"]).then_inc(wd_in, 16)
            for n in range(1, R):
                load(0, n)
            with sp.Fori(0, B // R - 1) as i:
                for n in range(R):
                    sp.wait_ge(v_b, done(R * i + n))
                    load(i + 1, n)

        @block.scalar
        def _(act):
            head_start(act, act_x, act_g, act_l)

            def take_x(i, n):
                act.wait_ge(pe_x, done(R * i + n))
                nc.scalar.copy(xT[:, n % 2], pX[:, :]).then_inc(act_x, 1)

            def slot(i, n, back=True, ahead=True):
                b = R * i + n
                act.wait_ge(pe_l, done(b))
                nc.scalar.copy(logits[:, b, :], pL[:, 0:NE]).then_inc(act_l, 1)
                act.wait_ge(pe_g, done(b))
                act.wait_ge(v_h, done(b - 1))
                nc.scalar.activation(gate[:], pG[:, :], ACT.Silu).then_inc(act_g, 1)
                if ahead:
                    take_x(*following(i, n, R))

            take_x(0, 0)
            in_turns(act, slot, B // R, R)

        @block.vector
        def _(dve):
            head_start(dve, v_h, v_b)

            def shared(i, n):
                b = R * i + n
                dve.wait_ge(pe_o, done(b))
                nc.vector.tensor_tensor(base[:, b, :], pO[:, :], xin[:, n, :], ALU.add).then_inc(v_b, 1)

            def slot(i, n, back=True, ahead=True):
                b = R * i + n
                if back:
                    shared(*preceding(i, n, R))
                dve.wait_ge(act_g, done(b))
                dve.wait_ge(pe_u, done(b))
                nc.vector.tensor_tensor(h[:], gate[:], pU[:, :].rearrange("p (c t) -> p c t", c=C), ALU.mult).then_inc(v_h, 1)

            in_turns(dve, slot, B // R, R)
            shared(B // R - 1, R - 1)

        @block.tensor
        def _(pe):
            head_start(pe, pe_x, pe_l, pe_g, pe_u, pe_o)

            def turn_x(i, n):
                pe.wait_ge(x_in[n], landed(i))
                for c in range(C):
                    last = nc.tensor.transpose(pX[:, P * c:P * c + P], xin[:, n, P * c:P * c + P], ident[:])
                last.then_inc(pe_x, 1)

            def up(ps, w, n, sem):
                for i in range(C):
                    for c in range(C):
                        last = nc.tensor.matmul(ps[:, P * i:P * i + P], w[:, c, P * i:P * i + P], xT[:, n % 2, c, :],
                                                start=c == 0, stop=c == C - 1)
                last.then_inc(sem, 1)

            def down(b):
                pe.wait_ge(v_h, done(b))
                pe.wait_ge(v_b, done(b - 1))
                for c in range(C):
                    last = nc.tensor.matmul(pO[:, :], h[:, c, :], wd[:, c, :], start=c == 0, stop=c == C - 1)
                last.then_inc(pe_o, 1)

            def slot(i, n, back=True, ahead=True):
                b = R * i + n
                pe.wait_ge(act_x, done(b))
                pe.wait_ge(act_l, done(b - 1))
                for c in range(C):
                    last = nc.tensor.matmul(pL[:, 0:NE], xT[:, n % 2, c, :], rw[:, c, :], start=c == 0, stop=c == C - 1)
                last.then_inc(pe_l, 1)
                if ahead:
                    turn_x(*following(i, n, R))
                pe.wait_ge(act_g, done(b - 1))
                up(pG, wg, n, pe_g)
                if back:
                    down(b - 1)
                pe.wait_ge(v_h, done(b - 1))
                up(pU, wu, n, pe_u)

            turn_x(0, 0)
            pe.wait_ge(w_in, 48)
            pe.wait_ge(wd_in, 16)
            in_turns(pe, slot, B // R, R)
            down(B - 1)


def route(nc, name, psum, tri, ones, logits, w_dram, NE, K, weight, slot_in, slot_out, grouped):
    NG, CAP, DROPPED = 8, 80, 80 * 32
    with ExitStack() as ctx:
        st = Stage(nc, ctx, name)
        pPos, pTot = psum[0], psum[1]
        iota = st.sbuf("iota", [P, 128])
        top = st.sbuf("top", [P, B, 8])
        topi = st.sbuf("topi", [P, B, 8], U32)
        topf = st.sbuf("topf", [P, B, 8])
        hot = st.sbuf("hot", [P, K, B, NE])
        sel = st.sbuf("sel", [P, B, NE])
        pos = st.sbuf("pos", [P, B, NE])
        carry = st.sbuf("carry", [P, B + 1, NE])
        prod = st.sbuf("prod", [P, B, NE])
        rowf = st.sbuf("rowf", [P, B, K])
        wsum = st.sbuf("wsum", [P, B])
        wt = st.sbuf("wt", [P, B, K])
        if grouped:
            bias = st.sbuf("bias", [P, NE])
            score = st.sbuf("score", [P, B, NE])
            biased = st.sbuf("biased", [P, B, NE])
            masked = st.sbuf("masked", [P, B, NE])
            pair = st.sbuf("pair", [P, B * NG])
            gscore = st.sbuf("gscore", [P, B, NG])
            gtop = st.sbuf("gtop", [P, B, 8])
            gtopi = st.sbuf("gtopi", [P, B, 8], U32)
            gtopf = st.sbuf("gtopf", [P, B, 8])
            gmask = st.sbuf("gmask", [P, B, NG])
            geq = st.sbuf("geq", [P, B, NG])
            over = st.sbuf("over", [P, B, NE])
        else:
            NT = slot_out["tiles"]
            expd = st.sbuf("expd", [P, B])
            cmp = st.sbuf("cmp", [P, NE, B])
            ntile = st.sbuf("ntile", [P, NE])
            first = st.sbuf("first", [P, NE + 1])
            tcmp = st.sbuf("tcmp", [P, NT, NE])
            texp = st.sbuf("texp", [P, NT])
        c_in, v, act_s, pe_c = st.sems("c_in", "v", "act_s", "pe_c")
        block = ctx.enter_context(nc.Block())
        n_sel = []

        def flat(t):
            return t[:].rearrange("p b e -> p (b e)")

        @block.sync
        def _(sp):
            sp.dma_start(iota[:], w_dram["iota"]).then_inc(c_in, 16)
            if grouped:
                sp.dma_start(bias[:], w_dram["bias"].partition_broadcast(P)).then_inc(c_in, 16)

        @block.vector
        def _(dve):
            step = Chain(dve, v)
            vec = nc.vector
            iota_e = iota[:, 0:NE].unsqueeze(1).to_broadcast([P, B, NE])
            dve.wait_ge(c_in, 32 if grouped else 16)
            ranked = logits
            if grouped:
                dve.wait_ge(act_s, 1)
                step(vec.tensor_tensor(biased[:], score[:], bias[:].unsqueeze(1).to_broadcast([P, B, NE]), ALU.add))
                q = flat(biased).rearrange("p (g m) -> p g m", m=4)
                gs = flat(gscore)
                for n, (i, j) in enumerate([(0, 1), (0, 2), (0, 3), (1, 2), (1, 3), (2, 3)]):
                    step(vec.tensor_tensor(pair[:] if n else gs, q[:, :, i], q[:, :, j], ALU.add))
                    if n:
                        step(vec.tensor_tensor(gs, gs, pair[:], ALU.max))
                for b in range(B):
                    last = vec.max(gtop[:, b], gscore[:, b])
                step(last)
                for b in range(B):
                    last = vec.max_index(gtopi[:, b], gtop[:, b], gscore[:, b])
                step(last)
                step(vec.tensor_copy(gtopf[:], gtopi[:]))
                iota_g = iota[:, 0:NG].unsqueeze(1).to_broadcast([P, B, NG])
                for k in range(3):
                    step(vec.tensor_tensor(geq[:] if k else gmask[:], iota_g, gtopf[:, :, k:k + 1].to_broadcast([P, B, NG]), ALU.is_equal))
                    if k:
                        step(vec.tensor_tensor(gmask[:], gmask[:], geq[:], ALU.add))
                step(vec.tensor_tensor(flat(masked).rearrange("p (g m) -> p g m", m=4), q,
                                       flat(gmask).unsqueeze(2).to_broadcast([P, B * NG, 4]), ALU.mult))
                ranked = masked
            for b in range(B):
                last = vec.max(top[:, b], ranked[:, b])
            step(last)
            for b in range(B):
                last = vec.max_index(topi[:, b], top[:, b], ranked[:, b])
            step(last)
            step(vec.tensor_copy(topf[:], topi[:]))
            for k in range(K):
                step(vec.tensor_tensor(hot[:, k], iota_e, topf[:, :, k:k + 1].to_broadcast([P, B, NE]), ALU.is_equal))
                if k:
                    step(vec.tensor_tensor(sel[:], hot[:, k] if k > 1 else hot[:, 1], sel[:] if k > 1 else hot[:, 0], ALU.add))
            n_sel.append(step.n)

            if grouped:
                for k in range(K):
                    step(vec.tensor_tensor(prod[:], hot[:, k], score[:], ALU.mult))
                    step(vec.tensor_reduce(wt[:, :, k], prod[:], AX.X, ALU.add))
                step(vec.tensor_reduce(wsum[:], wt[:], AX.X, ALU.add))
                step(vec.tensor_scalar(wsum[:], wsum[:], 1e-20, None, ALU.add))
                step(vec.reciprocal(wsum[:], wsum[:]))
                step(vec.tensor_tensor(wt[:], wt[:], wsum[:].unsqueeze(2).to_broadcast([P, B, K]), ALU.mult))
                step(vec.tensor_scalar(weight[:], wt[:], 2.5, None, ALU.mult))
            else:
                step(vec.tensor_tensor(wsum[:], top[:, :, 1], top[:, :, 0], ALU.subtract))
                n_sel.append(step.n)
                dve.wait_ge(act_s, 1)
                step(vec.tensor_scalar(wsum[:], expd[:], 1.0, None, ALU.add))
                step(vec.reciprocal(weight[:, :, 0], wsum[:]))
                step(vec.tensor_tensor(weight[:, :, 1], weight[:, :, 0], expd[:], ALU.mult))

            step(vec.memset(carry[:, 0], 0.0))
            dve.wait_ge(pe_c, 1)
            for b in range(B):
                step(vec.tensor_tensor(carry[:, b + 1], carry[:, b], pTot[:, NE * b:NE * b + NE], ALU.add))
            step(vec.tensor_tensor(pos[:], pPos[:, 0:B * NE].rearrange("p (b e) -> p b e", b=B), carry[:, 0:B], ALU.add))
            if grouped:
                step(vec.tensor_scalar(over[:], pos[:], float(CAP), 2.0 * DROPPED, ALU.is_ge, ALU.mult))
                step(vec.tensor_tensor(pos[:], pos[:], over[:], ALU.add))
                step(vec.tensor_scalar(prod[:], iota_e, float(CAP), None, ALU.mult))
                step(vec.tensor_tensor(pos[:], pos[:], prod[:], ALU.add))
                step(vec.tensor_scalar(pos[:], pos[:], float(DROPPED), None, ALU.min))
            else:
                step(vec.tensor_scalar(cmp[:], iota[:, 0:B].unsqueeze(1).to_broadcast([P, NE, B]), float(P), None, ALU.mult))
                step(vec.tensor_tensor(cmp[:], carry[:, B].unsqueeze(2).to_broadcast([P, NE, B]), cmp[:], ALU.is_gt))
                step(vec.tensor_reduce(ntile[:], cmp[:], AX.X, ALU.add))
                step(vec.memset(first[:, 0:1], 0.0))
                for e in range(NE):
                    step(vec.tensor_tensor(first[:, e + 1:e + 2], first[:, e:e + 1], ntile[:, e:e + 1], ALU.add))
                step(vec.tensor_scalar(ntile[:], first[:, 0:NE], float(P), None, ALU.mult))
                step(vec.tensor_tensor(pos[:], pos[:], ntile[:].unsqueeze(1).to_broadcast([P, B, NE]), ALU.add))
                step(vec.tensor_tensor(tcmp[:], iota[:, 0:NT].unsqueeze(2).to_broadcast([P, NT, NE]),
                                       first[:, 1:NE + 1].unsqueeze(1).to_broadcast([P, NT, NE]), ALU.is_ge))
                step(vec.tensor_reduce(texp[:], tcmp[:], AX.X, ALU.add))
                step(vec.tensor_scalar(slot_out["expert"][:], texp[:], float(NE - 1), None, ALU.min))
            for k in range(K):
                step(vec.tensor_tensor(prod[:], hot[:, k], pos[:], ALU.mult))
                step(vec.tensor_reduce(rowf[:, :, k], prod[:], AX.X, ALU.add))
            step(vec.tensor_copy(slot_in[:], rowf[:]))

        @block.scalar
        def _(act):
            if grouped:
                nc.scalar.activation(score[:], logits[:], ACT.Sigmoid).then_inc(act_s, 1)
            else:
                act.wait_ge(v, n_sel[1])
                nc.scalar.activation(expd[:], wsum[:], ACT.Exp).then_inc(act_s, 1)

        @block.tensor
        def _(pe):
            pe.wait_ge(v, n_sel[0])
            nc.tensor.matmul(pPos[:, 0:B * NE], tri[:], flat(sel), start=True, stop=True)
            nc.tensor.matmul(pTot[:, 0:B * NE], ones[:], flat(sel), start=True, stop=True).then_inc(pe_c, 1)


def dispatch(nc, name, x_src, rows, packed, K, bound, ready):
    R = 4
    with ExitStack() as ctx:
        st = Stage(nc, ctx, name)
        xs = st.sbuf("xs", [P, R, D])
        idx = st.sbuf("idx", [P, R, K], U32)
        one = st.sbuf("one", [P, 1])
        still = st.sbuf("still", [P, R, 2])
        x_in = [st.sem(f"x_in{n}") for n in range(R)]
        sent = [st.sem(f"sent{n}") for n in range(R)]
        g_i, g_one = st.sems("g_i", "g_one")
        block = ctx.enter_context(nc.Block())

        @block.sync
        def _(sp):
            for n in range(R):
                sp.dma_start(xs[:, n, :], x_src[n]).then_inc(x_in[n], 16)
            with sp.Fori(0, B // R - 1) as i:
                for n in range(R):
                    sp.wait_ge(sent[n], 16 * K * (i + 1))
                    sp.dma_start(xs[:, n, :], x_src[R * i + R + n]).then_inc(x_in[n], 16)

        @block.gpsimd
        def _(pool):
            nc.gpsimd.memset(one[:], 1.0).then_inc(g_one, 1)
            pool.wait_ge(g_one, 1)
            for s, value in ready:
                pool.wait_ge(s, value)

            def tile(i, n):
                nc.gpsimd.tensor_copy(idx[:, n], rows[:, R * i + n]).then_inc(g_i, 1)
                pool.wait_ge(x_in[n], landed(i))
                nc.gpsimd.tensor_tensor(still[:, n, 0:1], one[:], one[:], ALU.add)
                pool.wait_ge(g_i, R * i + n + 1)
                nc.gpsimd.tensor_tensor(still[:, n, 1:2], one[:], one[:], ALU.add)
                for k in range(K):
                    nc.gpsimd.indirect_dma_start(packed, bass.IndirectOffsetOnAxis(ap=idx[:, n, k:k + 1], axis=0),
                                                 xs[:, n, :], None, bounds_check=bound, oob_is_err=False).then_inc(sent[n], 16)

            for n in range(R):
                tile(0, n)
            with pool.Fori(1, B // R) as i:
                for n in range(R):
                    pool.wait_ge(sent[n], 16 * K * i)
                    tile(i, n)
            for n in range(R):
                pool.wait_ge(sent[n], 16 * K * (B // R))


def capped_experts(nc, psum, ident, packed, result, zero, w_dram):
    NE, CAP, F, R = 32, 80, 256, 4
    FC = F // P
    with ExitStack() as ctx:
        st = Stage(nc, ctx, "m")
        pX, pG, pU, pO = psum[0:2], psum[2:4], psum[4:6], psum[6:8]
        xe = st.sbuf("xe", [CAP, R, D])
        wg = st.sbuf("wg", [P, R, C, F])
        wu = st.sbuf("wu", [P, R, C, F])
        wd = st.sbuf("wd", [P, R, FC, D])
        xT = st.sbuf("xT", [P, 2, C, CAP])
        gate = st.sbuf("gate", [P, 2, FC, CAP])
        h = st.sbuf("h", [P, 2, FC, CAP])
        ye = st.sbuf("ye", [CAP, 2, D])
        x_in = [st.sem(f"x_in{n}") for n in range(R)]
        w_in = [st.sem(f"w_in{n}") for n in range(R)]
        y_out = [st.sem(f"y_out{n}") for n in range(2)]
        z_out, pe_x, pe_g, pe_u, pe_o, act_g, act_y, v_x, v_h = st.sems(
            "z_out", "pe_x", "pe_g", "pe_u", "pe_o", "act_g", "act_y", "v_x", "v_h")
        block = ctx.enter_context(nc.Block())

        @block.sync
        def _(sp):
            def load(i, n):
                e = R * i + n
                sp.dma_start(xe[:, n, :], packed[e]).then_inc(x_in[n], 16)
                sp.dma_start(wg[:, n], w_dram["wg"][e]).then_inc(w_in[n], 16)
                sp.dma_start(wu[:, n], w_dram["wu"][e]).then_inc(w_in[n], 16)
                sp.dma_start(wd[:, n], w_dram["wd"][e]).then_inc(w_in[n], 16)

            def store(i, n):
                sp.wait_ge(act_y, done(R * i + n))
                sp.dma_start(result[0:NE * CAP].rearrange("(e r) d -> e r d", r=CAP)[R * i + n], ye[:, n % 2, :]).then_inc(y_out[n % 2], 16)

            for n in range(2):
                sp.sem_inc(y_out[n], 16)
            for n in range(R):
                load(0, n)
            sp.dma_start(result[NE * CAP:NE * CAP + 1, :], zero[0:1, :]).then_inc(z_out, 16)
            with sp.Fori(0, NE // R - 1) as i:
                for n in range(R):
                    sp.wait_ge(pe_o, done(R * i + n))
                    load(i + 1, n)
                    store(i, n)
            for n in range(R):
                store(NE // R - 1, n)
            sp.wait_ge(z_out, 16)
            for n in range(2):
                sp.wait_ge(y_out[n], landed(NE // 2))

        @block.scalar
        def _(act):
            head_start(act, act_g, act_y)

            def take_y(i, n):
                e = R * i + n
                act.wait_ge(pe_o, done(e))
                act.wait_ge(y_out[n % 2], landed(R // 2 * i + n // 2))
                nc.scalar.copy(ye[:, n % 2, :], pO[n % 2][0:CAP, :]).then_inc(act_y, 1)

            def slot(i, n, back=True, ahead=True):
                e = R * i + n
                act.wait_ge(pe_g, done(e))
                act.wait_ge(v_h, done(e - 2))
                nc.scalar.activation(gate[:, n % 2], pG[n % 2][:, 0:FC * CAP].rearrange("p (c t) -> p c t", c=FC),
                                     ACT.Silu).then_inc(act_g, 1)
                if back:
                    take_y(*preceding(i, n, R))

            in_turns(act, slot, NE // R, R)
            take_y(NE // R - 1, R - 1)

        @block.vector
        def _(dve):
            head_start(dve, v_x, v_h)

            def take_x(i, n):
                dve.wait_ge(pe_x, done(R * i + n))
                nc.vector.tensor_copy(xT[:, n % 2], pX[n % 2][:, 0:C * CAP].rearrange("p (c t) -> p c t", c=C)).then_inc(v_x, 1)

            def slot(i, n, back=True, ahead=True):
                e = R * i + n
                if ahead:
                    take_x(*following(i, n, R))
                dve.wait_ge(act_g, done(e))
                dve.wait_ge(pe_u, done(e))
                nc.vector.tensor_tensor(h[:, n % 2], gate[:, n % 2], pU[n % 2][:, 0:FC * CAP].rearrange("p (c t) -> p c t", c=FC),
                                        ALU.mult).then_inc(v_h, 1)

            take_x(0, 0)
            in_turns(dve, slot, NE // R, R)

        @block.tensor
        def _(pe):
            head_start(pe, pe_x, pe_g, pe_u, pe_o)

            def turn_x(i, n):
                pe.wait_ge(x_in[n], landed(i))
                for c in range(C):
                    last = nc.tensor.transpose(pX[n % 2][:, CAP * c:CAP * c + CAP], xe[:, n, P * c:P * c + P], ident[0:CAP, 0:CAP])
                last.then_inc(pe_x, 1)

            def up(ps, w, n, sem):
                for f in range(FC):
                    for c in range(C):
                        last = nc.tensor.matmul(ps[n % 2][:, CAP * f:CAP * f + CAP], w[:, n, c, P * f:P * f + P],
                                                xT[:, n % 2, c, :], start=c == 0, stop=c == C - 1)
                last.then_inc(sem, 1)

            def down(i, n):
                e = R * i + n
                pe.wait_ge(v_h, done(e))
                pe.wait_ge(act_y, done(e - 2))
                for f in range(FC):
                    last = nc.tensor.matmul(pO[n % 2][0:CAP, :], h[:, n % 2, f, :], wd[:, n, f, :], start=f == 0, stop=f == FC - 1)
                last.then_inc(pe_o, 1)

            def slot(i, n, back=True, ahead=True):
                e = R * i + n
                if ahead:
                    turn_x(*following(i, n, R))
                pe.wait_ge(w_in[n], 48 * (i + 1))
                pe.wait_ge(v_x, done(e))
                pe.wait_ge(act_g, done(e - 2))
                up(pG, wg, n, pe_g)
                pe.wait_ge(v_h, done(e - 2))
                up(pU, wu, n, pe_u)
                if back:
                    down(*preceding(i, n, R))

            turn_x(0, 0)
            in_turns(pe, slot, NE // R, R)
            down(NE // R - 1, R - 1)


def routed_experts(nc, psum, ident, packed, result, expert, w_dram, NT):
    NE, F, R = 8, 352, 4
    FC = 3
    rows = [P, P, F - 2 * P]
    with ExitStack() as ctx:
        st = Stage(nc, ctx, "n")
        pX, pH, pG, pU, pO = psum[0], psum[1], psum[2:4], psum[4:6], psum[6:8]
        xe = st.sbuf("xe", [P, R, D])
        wg = st.sbuf("wg", [P, R, C, F])
        wu = st.sbuf("wu", [P, R, C, F])
        wd = st.sbuf("wd", [P, R, FC, D])
        xT = st.sbuf("xT", [P, 2, C, P])
        gate = st.sbuf("gate", [P, 2, F])
        h = st.sbuf("h", [P, 2, F])
        hT = st.sbuf("hT", [P, 2, FC, P])
        ye = st.sbuf("ye", [P, R, D])
        x_in, w_in, d_in, y_out = ([st.sem(f"{s}{n}") for n in range(R)] for s in ("x_in", "w_in", "d_in", "y_out"))
        pe_x, pe_g, pe_u, pe_h, pe_o, act_x, act_g, act_h, v_y, v_h = st.sems(
            "pe_x", "pe_g", "pe_u", "pe_h", "pe_o", "act_x", "act_g", "act_h", "v_y", "v_h")
        block = ctx.enter_context(nc.Block())

        @block.sync
        def _(sp):
            def load(i, n, fresh):
                t = R * i + n
                e = sp.value_load(expert[0:1, bass.ds(t, 1)], min_val=0, max_val=NE - 1)
                sp.dma_start(xe[:, n, :], packed[t]).then_inc(x_in[n], 16)
                if not fresh:
                    sp.wait_ge(pe_u, done(t - R))
                sp.dma_start(wg[:, n], w_dram["wg"][e]).then_inc(w_in[n], 16)
                sp.dma_start(wu[:, n], w_dram["wu"][e]).then_inc(w_in[n], 16)
                if not fresh:
                    sp.wait_ge(pe_o, done(t - R))
                sp.dma_start(wd[:, n, 0:2], w_dram["wd01"][e]).then_inc(d_in[n], 16)
                sp.dma_start(wd[0:rows[2], n, 2], w_dram["wd2"][e]).then_inc(d_in[n], 16)

            def store(i, n):
                sp.wait_ge(v_y, done(R * i + n))
                sp.dma_start(result.rearrange("(t r) d -> t r d", r=P)[R * i + n], ye[:, n, :]).then_inc(y_out[n], 16)

            for n in range(R):
                sp.sem_inc(y_out[n], 16)
                load(0, n, True)
            with sp.Fori(0, NT // R - 1) as i:
                for n in range(R):
                    sp.wait_ge(pe_x, done(R * i + n))
                    load(i + 1, n, False)
                    store(i, n)
            for n in range(R):
                store(NT // R - 1, n)
            for n in range(R):
                sp.wait_ge(y_out[n], landed(NT // R))

        @block.scalar
        def _(act):
            head_start(act, act_x, act_g, act_h)

            def take_x(i, n):
                act.wait_ge(pe_x, done(R * i + n))
                nc.scalar.copy(xT[:, n % 2], pX[:, :]).then_inc(act_x, 1)

            def take_h(i, n):
                act.wait_ge(pe_h, done(R * i + n))
                nc.scalar.copy(hT[:, n % 2, 0:2], pH[:, 0:2 * P])
                nc.scalar.copy(hT[0:rows[2], n % 2, 2], pH[0:rows[2], 2 * P:3 * P]).then_inc(act_h, 1)

            def slot(i, n, back=True, ahead=True):
                t = R * i + n
                if ahead:
                    take_x(*following(i, n, R))
                act.wait_ge(pe_g, done(t))
                act.wait_ge(v_h, done(t - 2))
                nc.scalar.activation(gate[:, n % 2], pG[n % 2][:, 0:F], ACT.Silu).then_inc(act_g, 1)
                if back:
                    take_h(*preceding(i, n, R))

            take_x(0, 0)
            in_turns(act, slot, NT // R, R)
            take_h(NT // R - 1, R - 1)

        @block.vector
        def _(dve):
            head_start(dve, v_y, v_h)

            def take_y(i, n):
                dve.wait_ge(pe_o, done(R * i + n))
                dve.wait_ge(y_out[n], landed(i))
                nc.vector.tensor_copy(ye[:, n, :], pO[n % 2][:, :]).then_inc(v_y, 1)

            def slot(i, n, back=True, ahead=True):
                t = R * i + n
                dve.wait_ge(act_g, done(t))
                dve.wait_ge(pe_u, done(t))
                nc.vector.tensor_tensor(h[:, n % 2], gate[:, n % 2], pU[n % 2][:, 0:F], ALU.mult).then_inc(v_h, 1)
                if back:
                    take_y(*preceding(i, n, R))

            in_turns(dve, slot, NT // R, R)
            take_y(NT // R - 1, R - 1)

        @block.tensor
        def _(pe):
            head_start(pe, pe_x, pe_g, pe_u, pe_h, pe_o)

            def turn_x(i, n):
                pe.wait_ge(x_in[n], landed(i))
                pe.wait_ge(act_x, done(R * i + n - 1))
                for c in range(C):
                    last = nc.tensor.transpose(pX[:, P * c:P * c + P], xe[:, n, P * c:P * c + P], ident[:])
                last.then_inc(pe_x, 1)

            def turn_h(i, n):
                pe.wait_ge(v_h, done(R * i + n))
                pe.wait_ge(act_h, done(R * i + n - 1))
                for f in range(FC):
                    last = nc.tensor.transpose(pH[0:rows[f], P * f:P * f + P], h[:, n % 2, P * f:P * f + rows[f]], ident[:])
                last.then_inc(pe_h, 1)

            def up(ps, w, n, sem):
                for c in range(C):
                    last = nc.tensor.matmul(ps[n % 2][:, 0:F], xT[:, n % 2, c, :], w[:, n, c, :], start=c == 0, stop=c == C - 1)
                last.then_inc(sem, 1)

            def down(i, n):
                t = R * i + n
                pe.wait_ge(act_h, done(t))
                pe.wait_ge(d_in[n], 32 * (i + 1))
                pe.wait_ge(v_y, done(t - 2))
                for f in range(FC):
                    last = nc.tensor.matmul(pO[n % 2][:, :], hT[0:rows[f], n % 2, f, :], wd[0:rows[f], n, f, :], start=f == 0, stop=f == FC - 1)
                last.then_inc(pe_o, 1)

            def slot(i, n, back=True, ahead=True):
                t = R * i + n
                if ahead:
                    turn_x(*following(i, n, R))
                pe.wait_ge(w_in[n], 32 * (i + 1))
                pe.wait_ge(act_x, done(t))
                pe.wait_ge(act_g, done(t - 2))
                up(pG, wg, n, pe_g)
                if back:
                    turn_h(*preceding(i, n, R))
                pe.wait_ge(v_h, done(t - 2))
                up(pU, wu, n, pe_u)
                if back:
                    down(*preceding(i, n, R))

            turn_x(0, 0)
            in_turns(pe, slot, NT // R, R)
            turn_h(NT // R - 1, R - 1)
            down(NT // R - 1, R - 1)


def combine(nc, name, base, x_src, result, rows, weight, x_dst, K):
    R = 4
    with ExitStack() as ctx:
        st = Stage(nc, ctx, name)
        got = st.sbuf("got", [P, R, K, D])
        idx = st.sbuf("idx", [P, R, K], U32)
        acc = st.sbuf("acc", [P, R, D])
        yn = st.sbuf("yn", [P, R, D])
        xin = st.sbuf("xin", [P, R, D]) if base is None else None
        stats = st.sbuf("stats", [P, R, 6])
        mv = st.sbuf("mv", [P, R, 2])
        rstd = st.sbuf("rstd", [P, R])
        mhalf = st.sbuf("mhalf", [P, 1])
        eps = st.sbuf("eps", [P, 1])
        still, gstill = st.sbuf("still", [P, 1]), st.sbuf("gstill", [P, R])
        x_in, g_in, y_out = ([st.sem(f"{s}{n}") for n in range(R)] for s in ("x_in", "g_in", "y_out"))
        g_c, g_i, g_ve, g_rs, v_k, v_acc, v_st, v_mv, v_yn = st.sems("g_c", "g_i", "g_ve", "g_rs", "v_k", "v_acc", "v_st", "v_mv", "v_yn")
        block = ctx.enter_context(nc.Block())

        @block.sync
        def _(sp):
            for n in range(R):
                sp.sem_inc(y_out[n], 16)
                if base is None:
                    sp.dma_start(xin[:, n, :], x_src[n]).then_inc(x_in[n], 16)

            def store(i, n):
                sp.wait_ge(v_yn, done(R * i + n))
                sp.dma_start(x_dst[R * i + n], yn[:, n, :]).then_inc(y_out[n], 16)

            with sp.Fori(0, B // R - 1) as i:
                for n in range(R):
                    store(i, n)
                    if base is None:
                        sp.dma_start(xin[:, n, :], x_src[R * i + R + n]).then_inc(x_in[n], 16)
            for n in range(R):
                store(B // R - 1, n)
            for n in range(R):
                sp.wait_ge(y_out[n], landed(B // R))

        @block.gpsimd
        def _(pool):
            head_start(pool, g_i, g_ve, g_rs)
            nc.gpsimd.memset(mhalf[:], -0.5).then_inc(g_c, 1)
            nc.gpsimd.memset(eps[:], EPS).then_inc(g_c, 1)
            pool.wait_ge(g_c, 2)

            def gather(i, n):
                b = R * i + n
                pool.wait_ge(v_acc, done(b - R))
                nc.gpsimd.tensor_copy(idx[:, n], rows[:, b]).then_inc(g_i, 1)
                pool.wait_ge(g_i, done(b))
                nc.gpsimd.tensor_tensor(gstill[:, n:n + 1], mhalf[:], mhalf[:], ALU.add)
                for k in range(K):
                    nc.gpsimd.indirect_dma_start(got[:, n, k, :], None, result,
                                                 bass.IndirectOffsetOnAxis(ap=idx[:, n, k:k + 1], axis=0)).then_inc(g_in[n], 16)

            def norm(i, n):
                b = R * i + n
                pool.wait_ge(v_mv, done(b))
                nc.gpsimd.tensor_tensor(rstd[:, n:n + 1], mv[:, n, 1:2], eps[:], ALU.add).then_inc(g_ve, 1)
                pool.wait_ge(g_ve, done(b))
                nc.gpsimd.tensor_tensor(rstd[:, n:n + 1], rstd[:, n:n + 1], mhalf[:], ALU.pow).then_inc(g_rs, 1)

            for n in range(R):
                gather(0, n)
            with pool.Fori(0, B // R - 1) as i:
                for n in range(R):
                    norm(i, n)
                    gather(i + 1, n)
            for n in range(R):
                norm(B // R - 1, n)

        @block.vector
        def _(dve):
            head_start(dve, v_k, v_acc, v_st, v_mv, v_yn)

            def tile(i, n):
                b = R * i + n
                dve.wait_ge(g_in[n], 16 * K * (i + 1))
                dve.wait_ge(v_yn, done(b - R))
                if base is None:
                    dve.wait_ge(x_in[n], landed(i))
                for k in range(K):
                    if k:
                        dve.wait_ge(v_k, done((K - 1) * b + k - 1))
                    prev = acc[:, n] if k else (xin[:, n] if base is None else base[:, b])
                    ins = nc.vector.scalar_tensor_tensor(out=acc[:, n], in0=got[:, n, k, :], scalar=weight[:, b, k:k + 1], in1=prev,
                                                         op0=ALU.mult, op1=ALU.add)
                    ins.then_inc(v_k if k < K - 1 else v_acc, 1)
                dve.wait_ge(v_acc, done(b))
                nc.vector.bn_stats(stats[:, n], acc[:, n]).then_inc(v_st, 1)
                dve.wait_ge(v_st, done(b))
                carry_wait(nc.vector, still)
                nc.vector.bn_aggr(mv[:, n], stats[:, n]).then_inc(v_mv, 1)

            def normed(i, n):
                dve.wait_ge(g_rs, done(R * i + n))
                dve.wait_ge(y_out[n], landed(i))
                nc.vector.tensor_scalar(yn[:, n], acc[:, n], mv[:, n, 0:1], rstd[:, n:n + 1], ALU.subtract, ALU.mult).then_inc(v_yn, 1)

            tile(0, 0)
            with dve.Fori(0, B // R - 1) as i:
                for n in range(1, R):
                    tile(i, n)
                    normed(i, n - 1)
                tile(i + 1, 0)
                normed(i, R - 1)
            for n in range(1, R):
                tile(B // R - 1, n)
                normed(B // R - 1, n - 1)
            normed(B // R - 1, R - 1)


def logits_only(nc, psum, ident, x_src, w_dram, logits, NE):
    R = 4
    with ExitStack() as ctx:
        st = Stage(nc, ctx, "r")
        pX, pL = psum[0:2], psum[2:4]
        xin = st.sbuf("xin", [P, R, D])
        xT = st.sbuf("xT", [P, 2, C, P])
        rw = st.sbuf("rw", [P, C, NE])
        x_in = [st.sem(f"x_in{n}") for n in range(R)]
        w_in, pe_x, pe_l, act_x, v_l = st.sems("w_in", "pe_x", "pe_l", "act_x", "v_l")
        block = ctx.enter_context(nc.Block())

        @block.sync
        def _(sp):
            sp.dma_start(rw[:], w_dram["rw"]).then_inc(w_in, 16)
            for n in range(R):
                sp.dma_start(xin[:, n, :], x_src[n]).then_inc(x_in[n], 16)
            with sp.Fori(0, B // R - 1) as i:
                for n in range(R):
                    sp.wait_ge(pe_x, done(R * i + n))
                    sp.dma_start(xin[:, n, :], x_src[R * i + R + n]).then_inc(x_in[n], 16)

        @block.scalar
        def _(act):
            head_start(act, act_x)
            with act.Fori(0, B // 2) as i:
                for n in range(2):
                    act.wait_ge(pe_x, done(2 * i + n))
                    act.wait_ge(pe_l, done(2 * i + n - 2))
                    nc.scalar.copy(xT[:, n], pX[n][:, :]).then_inc(act_x, 1)

        @block.vector
        def _(dve):
            head_start(dve, v_l)
            with dve.Fori(0, B // 2) as i:
                for n in range(2):
                    dve.wait_ge(pe_l, done(2 * i + n))
                    nc.vector.tensor_copy(logits[:, 2 * i + n, :], pL[n][:, 0:NE]).then_inc(v_l, 1)

        @block.tensor
        def _(pe):
            head_start(pe, pe_x, pe_l)

            def turn_x(i, n):
                pe.wait_ge(x_in[n], landed(i))
                pe.wait_ge(act_x, done(R * i + n - 2))
                for c in range(C):
                    last = nc.tensor.transpose(pX[n % 2][:, P * c:P * c + P], xin[:, n, P * c:P * c + P], ident[:])
                last.then_inc(pe_x, 1)

            def slot(i, n, back=True, ahead=True):
                b = R * i + n
                if ahead:
                    turn_x(*following(i, n, R))
                pe.wait_ge(act_x, done(b))
                pe.wait_ge(v_l, done(b - 2))
                for c in range(C):
                    last = nc.tensor.matmul(pL[n % 2][:, 0:NE], xT[:, n % 2, c, :], rw[:, c, :], start=c == 0, stop=c == C - 1)
                last.then_inc(pe_l, 1)

            pe.wait_ge(w_in, 16)
            turn_x(0, 0)
            in_turns(pe, slot, B // R, R)


NT2 = (2 * B * P + 7 * (P - 1)) // P + 1
NT2 += -NT2 % 4


def decoder(nc, x, ctxT, c, out):
    def scratch(name, rows):
        return nc.dram_tensor(name, [rows, D], F32, kind="Internal").ap()

    xs = [scratch(f"x{n}", B * P).rearrange("(b p) d -> b p d", p=P) for n in range(1, 6)]
    packed1, result1 = scratch("packed1", 32 * 80), scratch("result1", 32 * 80 + 1)
    packed2, result2 = scratch("packed2", NT2 * P), scratch("result2", NT2 * P)

    def of(prefix):
        return {n[2:]: a for n, a in c.items() if n.startswith(prefix)}

    with ExitStack() as ctx:
        st = Stage(nc, ctx, "all")
        psum = [ctx.enter_context(nc.psum_tensor(f"bank{n}", [P, 512], F32)) for n in range(8)]
        ident, tri, ones = (st.sbuf(n, [P, P]) for n in ("ident", "tri", "ones"))
        zero = st.sbuf("zero", [P, D])
        c_in, zeroed, packed_out, g_z = st.sems("c_in", "zeroed", "packed_out", "g_z")
        with nc.Block() as block:
            @block.sync
            def _(sp):
                sp.dma_start(ident[:], c["ident"]).then_inc(c_in, 16)
                sp.dma_start(tri[:], c["tri"]).then_inc(c_in, 16)
                sp.dma_start(ones[:], c["ones"]).then_inc(c_in, 16)
                sp.wait_ge(g_z, 1)
                for packed in (packed1, packed2):
                    n = packed.shape[0] // P
                    sp.dma_start(packed.rearrange("(p n) d -> p n d", p=P), zero[:].unsqueeze(1).to_broadcast([P, n, D])).then_inc(packed_out, 16)
                sp.wait_ge(c_in, 48)

            @block.gpsimd
            def _(pool):
                nc.gpsimd.memset(zero[:], 0.0).then_inc(g_z, 1)

        zeroed_rows = [(packed_out, 32)]
        wide_attention(nc, "a", psum, ident, x, xs[0], of("a_"), rope=True)
        narrow_attention(nc, "b", psum, ident, lambda b: xs[0][b], lambda b: xs[1][b], {**of("b_"), "ctxT": ctxT}, 32,
                         EVENTS_8, rope=True)
        with ExitStack() as moe:
            sc = Stage(nc, moe, "moe1")
            base, logits = sc.sbuf("base", [P, B, D]), sc.sbuf("logits", [P, B, 32])
            weight, rows = sc.sbuf("weight", [P, B, 4]), sc.sbuf("rows", [P, B, 4], U32)
            w = of("c_")
            shared_expert(nc, psum, ident, xs[1], w, base, logits, 32)
            route(nc, "cr", psum, tri, ones, logits, w, 32, 4, weight, rows, None, True)
            dispatch(nc, "cd", xs[1], rows, packed1, 4, 32 * 80 - 1, zeroed_rows)
            capped_experts(nc, psum, ident, packed1.rearrange("(e r) d -> e r d", r=80), result1, zero, w)
            combine(nc, "cc", base, None, result1, rows, weight, xs[2], 4)
        steps = [t.rearrange("l (j n) d -> j l n d", n=8) for t in (xs[2], xs[3])]
        narrow_attention(nc, "d", psum, ident, lambda b: steps[0][b], lambda b: steps[1][b], of("d_"), 16, EVENTS_4, causal=True)
        wide_attention(nc, "e", psum, ident, xs[3], xs[4], {**of("e_"), "ctxT": ctxT}, rms=True)
        with ExitStack() as moe:
            sc = Stage(nc, moe, "moe2")
            logits = sc.sbuf("logits", [P, B, 8])
            weight, rows = sc.sbuf("weight", [P, B, 2]), sc.sbuf("rows", [P, B, 2], U32)
            expert = sc.sbuf("expert", [P, NT2], I32)
            w = of("f_")
            logits_only(nc, psum, ident, xs[4], w, logits, 8)
            route(nc, "fr", psum, tri, ones, logits, w, 8, 2, weight, rows, {"tiles": NT2, "expert": expert}, False)
            dispatch(nc, "fd", xs[4], rows, packed2, 2, NT2 * P - 1, [])
            routed_experts(nc, psum, ident, packed2.rearrange("(t r) d -> t r d", r=P), result2, expert, w, NT2)
            combine(nc, "fc", None, xs[4], result2, rows, weight, out, 2)


def rope_tables():
    inv = (np.float32(1.0) / np.power(np.float32(10000.0), np.arange(0, 128, 2, dtype=np.float32) / np.float32(128))).astype(np.float32)
    ang = np.outer(np.arange(P, dtype=np.float32), inv).astype(np.float32)
    c, s = np.cos(ang), np.sin(ang)
    cos, sin = np.concatenate([c, c], 1), np.concatenate([-s, s], 1)
    scale = np.float32(1.0 / np.sqrt(128.0))
    return {"cosq": cos * scale, "sinq": sin * scale, "cosk": cos, "sink": sin}


def causal_mask():
    i = np.arange(P)
    return np.where(i[None, :] <= i[:, None], 0.0, NEG).astype(np.float32)


def by_chunk(w):
    return np.ascontiguousarray(w.reshape(-1, P, w.shape[1]).transpose(1, 0, 2))


def pairs_apart(w, groups):
    r, c = w.shape
    return w.reshape(r, groups, -1, 2).transpose(0, 1, 3, 2).reshape(r, c)


def layout_l0_attn(i):
    flat = {n: i[f"L0_attn_W_{n}"].transpose(1, 0, 2).reshape(D, -1) for n in "QKV"}
    out = {
        "a_wq": by_chunk(pairs_apart(flat["Q"], 16)), "a_wk": by_chunk(pairs_apart(flat["K"], 16)),
        "a_wv": by_chunk(flat["V"]), "a_wo": np.ascontiguousarray(i["L0_attn_W_O"].transpose(1, 0, 2)),
        "a_bq": pairs_apart(i["L0_attn_b_Q"].reshape(1, -1), 16)[0], "a_bk": pairs_apart(i["L0_attn_b_K"].reshape(1, -1), 16)[0],
        "a_bv": i["L0_attn_b_V"].reshape(-1), "a_bo": i["L0_attn_b_O"], "a_mask": causal_mask(),
    }
    out.update({"a_" + n: t.astype(np.float32) for n, t in rope_tables().items()})
    return out


def layout_l1_xattn(i):
    return {
        "e_wq": by_chunk(i["L1_xattn_Wq"]), "e_wk": by_chunk(i["L1_xattn_Wk"]), "e_wv": by_chunk(i["L1_xattn_Wv"]),
        "e_wo": by_chunk(i["L1_xattn_Wo"]), "e_gq": i["L1_xattn_gq"], "e_gk": i["L1_xattn_gk"],
    }


def layout_shared(i):
    return {"x": i["x"], "ctxT": np.ascontiguousarray(i["ctx_1024"].reshape(B, P, 2, P).transpose(3, 0, 2, 1)),
            "ident": np.eye(P, dtype=np.float32)}


def layout_l0_xattn(i):
    wk, wv = i["L0_xattn_Wkv"][:, :D], i["L0_xattn_Wkv"][:, D:]
    freq = np.power(np.float32(10000.0), -np.arange(4, dtype=np.float32) / np.float32(4)).astype(np.float32)
    return {
        "b_wq": by_chunk(pairs_apart(i["L0_xattn_Wq"], 32)), "b_wk": by_chunk(pairs_apart(wk, 32)), "b_wv": by_chunk(wv),
        "b_wo": by_chunk(i["L0_xattn_Wout"]), "b_bo": i["L0_xattn_bout"],
        "b_pos": np.ascontiguousarray(i["fside_BxSx2_0"].transpose(1, 0, 2).reshape(P, 2 * B)),
        "b_freq": np.ascontiguousarray(np.broadcast_to(freq, (P, 4))),
    }


def layout_l1_attn(i):
    w = i["L1_attn_weight_qkv"]
    r = np.arange(P)
    seen = (r[None, :] % 8 == r[:, None] % 8) & (r[None, :] // 8 <= r[:, None] // 8)
    return {
        "d_wq": by_chunk(w[:D].T), "d_wk": by_chunk(w[D:2 * D].T), "d_wv": by_chunk(w[2 * D:].T),
        "d_wo": by_chunk(i["L1_attn_weight_out"].T), "d_mask": np.where(seen, 0.0, NEG).astype(np.float32),
    }


def layout_moe(i):
    def by_expert(w):
        return np.ascontiguousarray(w.reshape(w.shape[0], -1, P, w.shape[2]).transpose(0, 2, 1, 3))

    down = i["L1_ffn_down_proj"].transpose(0, 2, 1)
    iota = np.ascontiguousarray(np.broadcast_to(np.arange(P, dtype=np.float32), (P, P)))
    return {
        "c_rw": by_chunk(i["L0_ffn_router_w"].T), "c_sg": by_chunk(i["L0_ffn_shared_gate"].T),
        "c_su": by_chunk(i["L0_ffn_shared_up"].T), "c_sd": by_chunk(i["L0_ffn_shared_down"].T),
        "c_bias": i["L0_ffn_e_bias"], "c_iota": iota, "c_wg": by_expert(i["L0_ffn_W_gate"]), "c_wu": by_expert(i["L0_ffn_W_up"]),
        "c_wd": by_expert(i["L0_ffn_W_down"]),
        "f_rw": by_chunk(i["L1_ffn_gate_w"].T), "f_iota": iota, "f_wg": by_expert(i["L1_ffn_gate_proj"].transpose(0, 2, 1)),
        "f_wu": by_expert(i["L1_ffn_up_proj"].transpose(0, 2, 1)), "f_wd01": by_expert(down[:, :2 * P]),
        "f_wd2": np.ascontiguousarray(down[:, 2 * P:]),
        "tri": np.triu(np.ones((P, P), np.float32), 1), "ones": np.ones((P, P), np.float32),
    }


def kernel(**inputs):
    import concourse.bacc as bacc
    from concourse.bass_utils import run_bass_kernel_spmd

    i = {n: np.asarray(a) for n, a in inputs.items()}
    arrays = layout_shared(i)
    for part in (layout_l0_attn, layout_l0_xattn, layout_moe, layout_l1_attn, layout_l1_xattn):
        arrays.update(part(i))
    nc = bacc.Bacc("TRN2", target_bir_lowering=False, num_devices=1)
    arrays = {"in_" + n: np.ascontiguousarray(a) for n, a in arrays.items()}
    aps = {n[3:]: nc.dram_tensor(n, a.shape, mybir.dt.from_np(a.dtype), kind="ExternalInput").ap() for n, a in arrays.items()}
    out = nc.dram_tensor("out", (B, P, D), F32, kind="ExternalOutput").ap()
    decoder(nc, aps["x"], aps["ctxT"], aps, out)
    return run_bass_kernel_spmd(nc, [arrays], core_ids=[0]).results[0]["out"]
```

```python
from contextlib import ExitStack

import numpy as np

import concourse.bass as bass
from concourse import mybir
from concourse.alu_op_type import AluOpType

F32 = mybir.dt.float32
F32R = mybir.dt.float32r
I32 = mybir.dt.int32
U32 = mybir.dt.uint32
ALU = mybir.AluOpType
ACT = mybir.ActivationFunctionType
AX = mybir.AxisListType

P = 128
D = 512
C = D // P
B = 16
EPS = 1e-5
LEAD = 4
NEG = -1e30


def done(n):
    return n + 1 + LEAD


def landed(n):
    return 16 * (n + 1)


class Stage:

    def __init__(self, nc, ctx, name):
        self.nc, self.ctx, self.name, self.used = nc, ctx, name, []
        ctx.callback(self.clear)

    def clear(self):
        if self.used:
            self.nc.clear_and_free_semaphores(self.used)
            self.nc.all_engine_barrier()

    def sbuf(self, name, shape, dt=F32):
        return self.ctx.enter_context(self.nc.sbuf_tensor(f"{self.name}_{name}", shape, dt))

    def sem(self, name):
        self.used.append(self.nc.alloc_semaphore(f"{self.name}_{name}"))
        return self.used[-1]

    def sems(self, *names):
        return [self.sem(n) for n in names]


def head_start(engine, *sems):
    for s in sems:
        engine.sem_inc(s, LEAD)


def carry_wait(engine, still):
    engine.memset(still[:], 0.0)


def heads(ap, n):
    return ap.rearrange("p (h d) -> p h d", h=n)


def split_product(nc, ps, a_hi, a_lo, b_hi, b_lo, start=True, stop=True):
    nc.tensor.matmul(ps, a_lo, b_hi, start=start, stop=False)
    nc.tensor.matmul(ps, a_hi, b_lo, start=False, stop=False)
    return nc.tensor.matmul(ps, a_hi, b_hi, start=False, stop=stop)


def wide_attention(nc, name, psum, ident, x_src, x_dst, w_dram, rope=None, rms=None, background=None, keep=None):
    G, H = 4, 4
    KC = C if rope else w_dram["ctxT"].shape[2]
    KINDS = "qkvo"
    QK = "qk" if rope else "kq"
    with ExitStack() as ctx:
        st = Stage(nc, ctx, name)
        pQ, pK, pV, pA, pB, pS, pP, pO = psum

        rows_of = {"q": C, "k": KC, "v": KC, "o": H}
        raw = st.sbuf("raw", [P, 3, C, D])
        RAW = {"q": 0, "k": 1, "v": 2, "o": 0}
        hi = {n: st.sbuf(f"w{n}_hi", [P, rows_of[n], D], F32R) for n in KINDS}
        lo = {n: st.sbuf(f"w{n}_lo", [P, rows_of[n], D], F32R) for n in KINDS}
        xin = st.sbuf("xin", [P, D])
        xall = st.sbuf("xall", [P, B, D])
        x_hi = st.sbuf("x_hi", [P, 2, C, P], F32R)
        x_lo = st.sbuf("x_lo", [P, 2, C, P], F32R)
        yall = st.sbuf("yall", [P, B, D]) if keep is None else keep
        tq = st.sbuf("tq", [P, D])
        tk = st.sbuf("tk", [P, D])
        sq = st.sbuf("sq", [P, D])
        sk = st.sbuf("sk", [P, D])
        kr = st.sbuf("kr", [P, D])
        qT = st.sbuf("qT", [P, H, P])
        kT = st.sbuf("kT", [P, H, P])
        v = st.sbuf("v", [P, 2, D])
        probT = st.sbuf("probT", [P, H, P])
        z_hi = st.sbuf("z_hi", [P, H, P], F32R)
        z_lo = st.sbuf("z_lo", [P, H, P], F32R)
        stats = st.sbuf("stats", [P, 6])
        mv = st.sbuf("mv", [P, 2])
        rstd = st.sbuf("rstd", [P, 1])
        mhalf = st.sbuf("mhalf", [P, H])
        eps = st.sbuf("eps", [P, 1])
        still, idle = st.sbuf("still", [P, 1]), st.sbuf("idle", [P, 1])
        nmax = st.sbuf("nmax", [P, H])
        rsum = st.sbuf("rsum", [P, H])
        rinv = st.sbuf("rinv", [P, H])
        if rope:
            qr = st.sbuf("qr", [P, D])
            prob = sm = st.sbuf("sm", [P, H, P])
            bias = {n: st.sbuf("b" + n, [P, D]) for n in "qkv"}
            bo = st.sbuf("bo", [P, D])
            tab = {n: st.sbuf(n, [P, P]) for n in ("cosq", "sinq", "cosk", "sink", "mask")}
            s_hi, s_lo = x_hi, x_lo
        else:
            prob = st.sbuf("prob", [P, H, P])
            qr = tq
            src = st.sbuf("ctxT", [P, KC, P])
            s_hi = st.sbuf("s_hi", [P, 2, KC, P], F32R)
            s_lo = st.sbuf("s_lo", [P, 2, KC, P], F32R)
            g2 = st.sbuf("g2", [P, 2, P])
            gg = st.sbuf("gg", [P, P])
            ssq = st.sbuf("ssq", [P, H])
            ssk = st.sbuf("ssk", [P, H])
            rq = st.sbuf("rq", [P, 2, H])
            rk = st.sbuf("rk", [P, H])
            nb = st.sbuf("nb", [P, H])
            epsn = st.sbuf("epsn", [P, H])

        c_in, x_in, y_in, ctx_in, b_in, out_st = st.sems("c_in", "x_in", "y_in", "ctx_in", "b_in", "out_st")
        raw_in = st.sems("raw_in0", "raw_in1", "raw_in2")
        w_hi = {n: st.sem(f"hi_{n}") for n in KINDS}
        w_lo = {n: st.sem(f"lo_{n}") for n in KINDS}
        pe_x, pe_q, pe_k, pe_v = st.sems("pe_x", "pe_q", "pe_k", "pe_v")
        pe_qt, pe_kt, pe_s, pe_pt, pe_z, pe_o = st.sems("pe_qt", "pe_kt", "pe_s", "pe_pt", "pe_z", "pe_o")
        pe_used = {"q": pe_q, "k": pe_k, "v": pe_v, "o": pe_o}
        act_x, act_qt, act_kt, act_e, act_z, act_pt, act_hi = st.sems(
            "act_x", "act_qt", "act_kt", "act_e", "act_z", "act_pt", "act_hi")
        v_tq, v_tk, v_q, v_k, v_v = st.sems("v_tq", "v_tk", "v_q", "v_k", "v_v")
        v_aq, v_ak, v_sm, v_nm, v_nb, v_zl, v_ri, v_p = st.sems("v_aq", "v_ak", "v_sm", "v_nm", "v_nb", "v_zl", "v_ri", "v_p")
        v_y, v_st, v_mv, v_yn = st.sems("v_y", "v_st", "v_mv", "v_yn")
        g_q, g_k, g_mq, g_mk, g_rq, g_rk, g_x, g_c, g_ve, g_rs, g_lo = st.sems(
            "g_q", "g_k", "g_mq", "g_mk", "g_rq", "g_rk", "g_x", "g_c", "g_ve", "g_rs", "g_lo")

        n_const = 6 if rope else 2
        block = ctx.enter_context(nc.Block())

        def each_unit(engine, slot):
            for g in range(G):
                slot(g, 0, 0, first=g == 0)
                slot(g, 1, 1)
                with engine.Fori(0, B // 2 - 2) as i:
                    for n in range(2):
                        slot(g, 2 * i + 2 + n, n)
                slot(g, B - 2, 0)
                slot(g, B - 1, 1, last=g == G - 1)

        def ends(b):
            return isinstance(b, int) and b == B - 1

        def before_last(b):
            return not (isinstance(b, int) and b >= B - 2)

        def split_hi(engine, copy, n, g):
            if g > 0:
                engine.wait_ge(pe_used[n], done(B * g - 1))
            engine.wait_ge(raw_in[RAW[n]], landed({"q": 2 * g, "o": 2 * g + 1}.get(n, g)))
            copy(hi[n][:], raw[:, RAW[n], 0:rows_of[n], :]).then_inc(w_hi[n], 1)

        def split_lo(engine, tensor_tensor, n, g):
            engine.wait_ge(w_hi[n], g + 1)
            tensor_tensor(lo[n][:], raw[:, RAW[n], 0:rows_of[n], :], hi[n][:].bitcast(F32), ALU.subtract).then_inc(w_lo[n], 1)

        def is_batch(b, n):
            return isinstance(b, int) and b == n

        @block.sync
        def _(sp):
            def weights(n, g):
                if g or n == "o":
                    sp.wait_ge(w_lo[{"q": "o", "o": "q"}.get(n, n)], g + 1 if n == "o" else g)
                w = w_dram["w" + n]
                part = w[:, H * g:H * g + H] if n == "o" else w[:, :, D * g:D * g + D]
                sp.dma_start(raw[:, RAW[n], 0:rows_of[n], :], part).then_inc(raw_in[RAW[n]], 16)

            def context(u, b):
                if rms:
                    sp.wait_ge(g_lo, done(u - 1))
                    sp.dma_start(src[:], w_dram["ctxT"][:, b]).then_inc(ctx_in, 16)

            def biases(g):
                if rope:
                    for n in "qkv":
                        sp.dma_start(bias[n][:], w_dram["b" + n][D * g:D * g + D].partition_broadcast(P)).then_inc(b_in, 16)

            def slot(g, b, par, first=False, last=False):
                u = B * g + b
                if g == 0 and before_last(b):
                    sp.wait_ge(pe_x, done(b + 1))
                    sp.dma_start(xin[:], x_src[b + 2]).then_inc(x_in, 16)
                if first:
                    weights("o", 0)
                    sp.dma_start(yall[:], x_src.rearrange("b p d -> p b d")).then_inc(y_in, 16)
                if before_last(b):
                    context(u + 2, b + 2)
                elif g < G - 1:
                    context(u + 2, b + 2 - B)
                if is_batch(b, 1) and g < G - 1:
                    for n in "qkv":
                        weights(n, g + 1)
                if ends(b) and g < G - 1:
                    if rope:
                        sp.wait_ge(v_v, done(u))
                    biases(g + 1)
                    weights("o", g + 1)
                if background and g >= G - 2:
                    background(sp, u - B * (G - 2))
                if g == G - 1 and not is_batch(b, 0) and not is_batch(b, 1):
                    store(b - 2)

            def store(b):
                if keep is None:
                    sp.wait_ge(v_yn, done(b))
                    sp.dma_start(x_dst[b], yall[:, b, :]).then_inc(out_st, 16)

            sp.dma_start(xin[:], x_src[0]).then_inc(x_in, 16)
            context(0, 0)
            for n in QK:
                weights(n, 0)
            biases(0)
            weights("v", 0)
            sp.wait_ge(pe_x, done(0))
            sp.dma_start(xin[:], x_src[1]).then_inc(x_in, 16)
            context(1, 1)
            each_unit(sp, slot)
            store(B - 2)
            store(B - 1)
            if keep is None:
                sp.wait_ge(out_st, 16 * B)

        @block.scalar
        def _(act):
            head_start(act, act_x, act_qt, act_kt, act_e, act_z, act_pt, act_hi)
            if rope:
                for n in tab:
                    act.dma_start(tab[n][:], w_dram[n]).then_inc(c_in, 16)
                act.dma_start(bo[:], w_dram["bo"].partition_broadcast(P)).then_inc(c_in, 16)
            else:
                act.dma_start(g2[:, 0, :], w_dram["gq"].partition_broadcast(P)).then_inc(c_in, 16)
                act.dma_start(g2[:, 1, :], w_dram["gk"].partition_broadcast(P)).then_inc(c_in, 16)

            def take_x(b):
                act.wait_ge(pe_x, done(b))
                nc.scalar.copy(xall[:, b, :], pP[:, :]).then_inc(act_x, 1)

            def source(g, b, par):
                u = B * g + b
                act.wait_ge(act_x, done(b) if g == 0 else done(B - 1))
                act.wait_ge(pe_v, done(u - 2))
                nc.scalar.copy(idle[:], ident[:, 0:1])
                copy = nc.scalar.copy(x_hi[:, par], xall[:, b, :])
                if rms:
                    act.wait_ge(ctx_in, landed(u))
                    copy = nc.scalar.copy(s_hi[:, par], src[:])
                copy.then_inc(act_hi, 1)

            def take_z(u):
                act.wait_ge(pe_z, done(u))
                act.wait_ge(pe_o, done(u - 1))
                nc.scalar.copy(z_hi[:], pA[:, :]).then_inc(act_z, 1)

            def slot(g, b, par, first=False, last=False):
                u = B * g + b
                if is_batch(b, 1):
                    split_hi(act, nc.scalar.copy, "o", g)
                if not last:
                    source(g + 1 if ends(b) else g, 0 if ends(b) else b + 1, 1 - par)
                act.wait_ge(pe_qt, done(u))
                nc.scalar.copy(qT[:], pA[:, :]).then_inc(act_qt, 1)
                act.wait_ge(pe_kt, done(u))
                nc.scalar.copy(kT[:], pB[:, :]).then_inc(act_kt, 1)
                if not first:
                    take_z(u - 1)
                if ends(b) and not last:
                    split_hi(act, nc.scalar.copy, "v", g + 1)
                if g == 0 and before_last(b):
                    take_x(b + 2)
                if rope:
                    act.wait_ge(v_nm, done(u))
                    for j in range(H):
                        step = nc.scalar.activation(prob[:, j, :], sm[:, j, :], ACT.Exp, bias=nmax[:, j:j + 1],
                                                    accum_out=rsum[:, j:j + 1])
                else:
                    act.wait_ge(v_nb, done(u))
                    for j in range(H):
                        step = nc.scalar.activation(prob[:, j, :], pS[:, P * j:P * j + P], ACT.Exp,
                                                    bias=nb[:, j:j + 1], scale=rq[:, par, j:j + 1],
                                                    accum_out=rsum[:, j:j + 1])
                step.then_inc(act_e, 1)
                act.wait_ge(pe_pt, done(u))
                nc.scalar.copy(probT[:], pP[:, :]).then_inc(act_pt, 1)
                if is_batch(b, B - 2) and g < G - 1:
                    split_hi(act, nc.scalar.copy, "q", g + 1)

            take_x(0)
            source(0, 0, 0)
            for n in "qv":
                split_hi(act, nc.scalar.copy, n, 0)
            take_x(1)
            each_unit(act, slot)
            take_z(G * B - 1)

        @block.gpsimd
        def _(pool):
            head_start(pool, g_q, g_k, g_mq, g_mk, g_rq, g_rk, g_x, g_ve, g_rs, g_lo)
            nc.gpsimd.memset(mhalf[:], -0.5).then_inc(g_c, 1)
            nc.gpsimd.memset(eps[:], EPS).then_inc(g_c, 1)
            pool.wait_ge(g_c, 2)

            def source(g, b, par):
                pool.wait_ge(act_hi, done(B * g + b))
                sub = nc.gpsimd.tensor_tensor(x_lo[:, par].rearrange("p c t -> p (c t)"), xall[:, b, :],
                                              x_hi[:, par].rearrange("p c t -> p (c t)").bitcast(F32), ALU.subtract)
                if rms:
                    sub = nc.gpsimd.tensor_tensor(s_lo[:, par], src[:], s_hi[:, par].bitcast(F32), ALU.subtract)
                sub.then_inc(g_lo, 1)

            def turned(out, t, sin):
                for half in range(2):
                    o = heads(out[:], H)[:, :, 64 * half:64 * half + 64]
                    i = heads(t[:], H)[:, :, 64 - 64 * half:128 - 64 * half]
                    s = tab[sin][:, 64 * half:64 * half + 64].unsqueeze(1).to_broadcast([P, H, 64])
                    step = nc.gpsimd.tensor_tensor(o, i, s, ALU.mult)
                return step

            def project(u, par):
                if rope:
                    pool.wait_ge(v_tq, done(u))
                    pool.wait_ge(v_q, done(u - 1))
                    turned(sq, tq, "sinq").then_inc(g_q, 1)
                    pool.wait_ge(v_tk, done(u))
                    pool.wait_ge(v_k, done(u - 1))
                    turned(sk, tk, "sink").then_inc(g_k, 1)
                    return
                pool.wait_ge(v_tk, done(u))
                nc.gpsimd.tensor_tensor(sk[:], tk[:], tk[:], ALU.mult).then_inc(g_k, 1)
                pool.wait_ge(v_tq, done(u))
                nc.gpsimd.tensor_tensor(sq[:], tq[:], tq[:], ALU.mult).then_inc(g_q, 1)
                pool.wait_ge(v_ak, done(u))
                nc.gpsimd.tensor_tensor(rk[:], ssk[:], epsn[:], ALU.add).then_inc(g_mk, 1)
                pool.wait_ge(g_mk, done(u))
                nc.gpsimd.tensor_tensor(rk[:], rk[:], mhalf[:], ALU.pow).then_inc(g_rk, 1)
                pool.wait_ge(v_aq, done(u))
                nc.gpsimd.tensor_tensor(rq[:, par, :], ssq[:], epsn[:], ALU.add).then_inc(g_mq, 1)
                pool.wait_ge(g_mq, done(u))
                nc.gpsimd.tensor_tensor(rq[:, par, :], rq[:, par, :], mhalf[:], ALU.pow).then_inc(g_rq, 1)

            def residual(b):
                if rope:
                    nc.gpsimd.tensor_tensor(yall[:, b, :], yall[:, b, :], bo[:], ALU.add).then_inc(g_x, 1)

            def norm(b):
                pool.wait_ge(v_mv, done(b))
                nc.gpsimd.tensor_tensor(rstd[:], mv[:, 1:2], eps[:], ALU.add).then_inc(g_ve, 1)
                pool.wait_ge(g_ve, done(b))
                nc.gpsimd.tensor_tensor(rstd[:], rstd[:], mhalf[:, 0:1], ALU.pow).then_inc(g_rs, 1)

            def slot(g, b, par, first=False, last=False):
                u = B * g + b
                if not last:
                    source(g + 1 if ends(b) else g, 0 if ends(b) else b + 1, 1 - par)
                if g == G - 1 and not is_batch(b, 0) and not is_batch(b, 1):
                    norm(b - 2)
                if is_batch(b, 1):
                    split_lo(pool, nc.gpsimd.tensor_tensor, "o", g)
                if ends(b) and not last:
                    split_lo(pool, nc.gpsimd.tensor_tensor, "v", g + 1)
                if not last:
                    project(u + 1, 1 - par)
                if first:
                    pool.wait_ge(y_in, 16)
                if g == 0:
                    residual(b)

            source(0, 0, 0)
            split_lo(pool, nc.gpsimd.tensor_tensor, "v", 0)
            pool.wait_ge(c_in, 16 * n_const)
            if rms:
                nc.gpsimd.memset(epsn[:], EPS * P).then_inc(g_c, 1)
                nc.gpsimd.tensor_tensor(gg[:], g2[:, 0, :], g2[:, 1, :], ALU.mult).then_inc(g_c, 1)
                pool.wait_ge(g_c, 4)
                nc.gpsimd.tensor_scalar(gg[:], gg[:], float(np.sqrt(P)), 0.0, ALU.mult, ALU.add).then_inc(g_c, 1)
            project(0, 0)
            each_unit(pool, slot)
            norm(B - 2)
            norm(B - 1)

        @block.vector
        def _(dve):
            head_start(dve, v_tq, v_tk, v_q, v_k, v_v, v_aq, v_ak, v_sm, v_nm, v_nb, v_zl, v_ri, v_p, v_y, v_st, v_mv, v_yn)

            def rotate(u, ps, t, a, bias_n, cos, t_sem, a_sem):
                nc.vector.tensor_tensor(t[:], ps[:, :], bias_n[:], ALU.add).then_inc(t_sem, 1)
                dve.wait_ge(t_sem, done(u))
                c = tab[cos][:].unsqueeze(1).to_broadcast([P, H, P])
                nc.vector.tensor_tensor(heads(a[:], H), heads(t[:], H), c, ALU.mult).then_inc(a_sem, 1)
                dve.wait_ge(a_sem, done(u))

            def project(g, b, par, before=True):
                u = B * g + b
                if rope:
                    dve.wait_ge(pe_q, done(u))
                    if is_batch(b, 0):
                        dve.wait_ge(b_in, 48 * (g + 1))
                    rotate(u, pQ, tq, qr, bias["q"], "cosq", v_tq, v_aq)
                    if before:
                        normalise(u - 1)
                    dve.wait_ge(g_q, done(u))
                    nc.vector.tensor_tensor(qr[:], qr[:], sq[:], ALU.add).then_inc(v_q, 1)
                    dve.wait_ge(pe_k, done(u))
                    rotate(u, pK, tk, kr, bias["k"], "cosk", v_tk, v_ak)
                    dve.wait_ge(g_k, done(u))
                    nc.vector.tensor_tensor(kr[:], kr[:], sk[:], ALU.add).then_inc(v_k, 1)
                    dve.wait_ge(pe_v, done(u))
                    nc.vector.tensor_tensor(v[:, par, :], pV[:, :], bias["v"][:], ALU.add).then_inc(v_v, 1)
                    return
                dve.wait_ge(pe_k, done(u))
                nc.vector.tensor_copy(tk[:], pK[:, :]).then_inc(v_tk, 1)
                if before:
                    normalise(u - 1)
                dve.wait_ge(pe_q, done(u))
                nc.vector.tensor_copy(tq[:], pQ[:, :]).then_inc(v_tq, 1)
                dve.wait_ge(g_k, done(u))
                nc.vector.tensor_reduce(ssk[:], heads(sk[:], H), AX.X, ALU.add).then_inc(v_ak, 1)
                dve.wait_ge(g_q, done(u))
                nc.vector.tensor_reduce(ssq[:], heads(sq[:], H), AX.X, ALU.add).then_inc(v_aq, 1)
                dve.wait_ge(pe_v, done(u))
                nc.vector.tensor_copy(v[:, par, :], pV[:, :]).then_inc(v_v, 1)
                dve.wait_ge(g_rk, done(u))
                for j in range(H):
                    step = nc.vector.scalar_tensor_tensor(
                        out=kr[:, P * j:P * j + P], in0=tk[:, P * j:P * j + P], scalar=rk[:, j:j + 1], in1=gg[:],
                        op0=ALU.mult, op1=ALU.mult)
                step.then_inc(v_k, 1)

            def normalise(u):
                dve.wait_ge(act_e, done(u))
                nc.vector.reciprocal(rinv[:], rsum[:]).then_inc(v_ri, 1)
                dve.wait_ge(v_ri, done(u))
                nc.vector.tensor_tensor(prob[:], prob[:], rinv[:].unsqueeze(2).to_broadcast([P, H, P]), ALU.mult).then_inc(v_p, 1)

            def take_z_lo(u):
                dve.wait_ge(act_z, done(u))
                dve.wait_ge(pe_o, done(u - 1))
                nc.vector.tensor_tensor(z_lo[:], heads(pA[:, :], H), z_hi[:].bitcast(F32), ALU.subtract).then_inc(v_zl, 1)

            def add_output(g, b):
                u = B * g + b
                dve.wait_ge(pe_o, done(u))
                if g == 0:
                    if rope:
                        dve.wait_ge(g_x, done(b))
                    elif is_batch(b, 0):
                        dve.wait_ge(y_in, 16)
                nc.vector.tensor_tensor(yall[:, b, :], pO[:, :], yall[:, b, :], ALU.add).then_inc(v_y, 1)
                if g == G - 1:
                    dve.wait_ge(v_y, done(u))
                    carry_wait(nc.vector, still)
                    nc.vector.bn_stats(stats[:], yall[:, b, :]).then_inc(v_st, 1)
                    dve.wait_ge(v_st, done(b))
                    carry_wait(nc.vector, still)
                    nc.vector.bn_aggr(mv[:], stats[:]).then_inc(v_mv, 1)

            def normed(b):
                dve.wait_ge(g_rs, done(b))
                nc.vector.tensor_scalar(yall[:, b, :], yall[:, b, :], mv[:, 0:1], rstd[:], ALU.subtract, ALU.mult).then_inc(v_yn, 1)

            def slot(g, b, par, first=False, last=False):
                u = B * g + b
                inner = not is_batch(b, 0)
                dve.wait_ge(pe_s, done(u))
                if rope:
                    nc.vector.tensor_tensor(sm[:], heads(pS[:, :], H), tab["mask"][:].unsqueeze(1).to_broadcast([P, H, P]),
                                            ALU.add).then_inc(v_sm, 1)
                    dve.wait_ge(v_sm, done(u))
                    nc.vector.tensor_reduce(nmax[:], sm[:], AX.X, ALU.max, negate=True).then_inc(v_nm, 1)
                else:
                    nc.vector.tensor_reduce(nmax[:], heads(pS[:, :], H), AX.X, ALU.max, negate=True).then_inc(v_nm, 1)
                    dve.wait_ge(v_nm, done(u))
                    dve.wait_ge(g_rq, done(u))
                    nc.vector.tensor_tensor(nb[:], nmax[:], rq[:, par, :], ALU.mult).then_inc(v_nb, 1)
                if not first:
                    take_z_lo(u - 1)
                if g == G - 1 and not is_batch(b, 0) and not is_batch(b, 1):
                    normed(b - 2)
                if not last:
                    project(g + 1 if ends(b) else g, 0 if ends(b) else b + 1, 1 - par)
                if last:
                    normalise(u)
                if not first:
                    add_output(g if inner else g - 1, b - 1 if inner else B - 1)
                if is_batch(b, B - 2) and g < G - 1:
                    split_lo(dve, nc.vector.tensor_tensor, "q", g + 1)
                    split_hi(dve, nc.vector.tensor_copy, "k", g + 1)
                    split_lo(dve, nc.vector.tensor_tensor, "k", g + 1)

            for n in QK:
                if n == "k":
                    split_hi(dve, nc.vector.tensor_copy, "k", 0)
                split_lo(dve, nc.vector.tensor_tensor, n, 0)
            dve.wait_ge(c_in, 16 * n_const)
            if rms:
                dve.wait_ge(g_c, 5)
            project(0, 0, 0, before=False)
            each_unit(dve, slot)
            normed(B - 2)
            take_z_lo(G * B - 1)
            add_output(G - 1, B - 1)
            normed(B - 1)

        @block.tensor
        def _(pe):
            head_start(pe, pe_x, pe_q, pe_k, pe_v, pe_qt, pe_kt, pe_s, pe_pt, pe_z, pe_o)

            def turn_x(b):
                pe.wait_ge(x_in, landed(b))
                for c in range(C):
                    step = nc.tensor.transpose(pP[:, P * c:P * c + P], xin[:, P * c:P * c + P], ident[:])
                step.then_inc(pe_x, 1)

            def ready(n, g, b):
                if is_batch(b, 0):
                    pe.wait_ge(w_lo[n], g + 1)

            def project(n, ps, a_hi, a_lo, g, b, par, sem):
                ready(n, g, b)
                for c in range(rows_of[n]):
                    step = split_product(nc, ps[:, :], a_hi[:, par, c, :], a_lo[:, par, c, :], hi[n][:, c, :], lo[n][:, c, :],
                                         start=c == 0, stop=c == rows_of[n] - 1)
                step.then_inc(sem, 1)

            def project_qk(g, b, par):
                for n in QK:
                    if n == "q":
                        project("q", pQ, x_hi, x_lo, g, b, par, pe_q)
                    else:
                        project("k", pK, s_hi, s_lo, g, b, par, pe_k)

            def turn_q(u):
                pe.wait_ge(v_q if rope else v_tq, done(u))
                pe.wait_ge(v_zl, done(u - 2))
                for j in range(H):
                    step = nc.tensor.transpose(pA[:, P * j:P * j + P], qr[:, P * j:P * j + P], ident[:])
                step.then_inc(pe_qt, 1)

            def turn_k(u):
                pe.wait_ge(v_k, done(u))
                for j in range(H):
                    step = nc.tensor.transpose(pB[:, P * j:P * j + P], kr[:, P * j:P * j + P], ident[:])
                step.then_inc(pe_kt, 1)

            def probs_v(u, par):
                pe.wait_ge(act_pt, done(u))
                pe.wait_ge(v_v, done(u))
                for j in range(H):
                    step = nc.tensor.matmul(pA[:, P * j:P * j + P], v[:, par, P * j:P * j + P], probT[:, j, :],
                                            start=True, stop=True)
                step.then_inc(pe_z, 1)

            def output(g, b):
                u = B * g + b
                pe.wait_ge(v_zl, done(u))
                pe.wait_ge(v_y, done(u - 1))
                ready("o", g, b)
                for j in range(H):
                    step = split_product(nc, pO[:, :], z_hi[:, j, :], z_lo[:, j, :], hi["o"][:, j, :], lo["o"][:, j, :],
                                         start=j == 0, stop=j == H - 1)
                step.then_inc(pe_o, 1)

            def slot(g, b, par, first=False, last=False):
                u = B * g + b
                following_unit = (g + 1, 0) if ends(b) else (g, b + 1)
                if g == 0 and before_last(b):
                    pe.wait_ge(act_x, done(b + 1))
                    pe.wait_ge(act_pt, done(u - 1))
                    turn_x(b + 2)
                pe.wait_ge(act_qt, done(u))
                if not first:
                    probs_v(u - 1, 1 - par)
                pe.wait_ge(act_kt, done(u))
                for j in range(H):
                    step = nc.tensor.matmul(pS[:, P * j:P * j + P], qT[:, j, :], kT[:, j, :], start=True, stop=True)
                step.then_inc(pe_s, 1)
                if not last:
                    pe.wait_ge(g_lo, done(u + 1))
                    project_qk(*following_unit, 1 - par)
                    pe.wait_ge(v_v, done(u))
                    project("v", pV, s_hi, s_lo, *following_unit, 1 - par, pe_v)
                pe.wait_ge(v_p, done(u))
                for j in range(H):
                    step = nc.tensor.transpose(pP[:, P * j:P * j + P], prob[:, j, :], ident[:])
                step.then_inc(pe_pt, 1)
                if not last:
                    turn_q(u + 1)
                if not last and rope:
                    turn_k(u + 1)
                if not first:
                    inner = not is_batch(b, 0)
                    output(g if inner else g - 1, b - 1 if inner else B - 1)
                if not last and rms:
                    turn_k(u + 1)

            turn_x(0)
            pe.wait_ge(g_lo, done(0))
            project_qk(0, 0, 0)
            pe.wait_ge(act_x, done(0))
            turn_x(1)
            project("v", pV, s_hi, s_lo, 0, 0, 0, pe_v)
            turn_q(0)
            turn_k(0)
            each_unit(pe, slot)
            u = G * B - 1
            probs_v(u, 1)
            output(G - 1, B - 1)


def narrow_attention(nc, name, psum, ident, x_src, x_dst, w_dram, NH, events, rope=False, causal=False, keep=None):
    DH = D // NH
    H = 4
    UN = NH // H
    W = 32
    NBLK = NH * W // P
    ROUNDS = NBLK // 4
    HB = NH // 2
    KC = C if causal else w_dram["ctxT"].shape[2]
    SCALE = float(1.0 / np.sqrt(float(DH)))
    with ExitStack() as ctx:
        st = Stage(nc, ctx, name)
        pJ, pT, pS0, pS1, pP, pO, pZ0, pZ1 = psum
        pS, pZ = (pS0, pS1), (pZ0, pZ1)

        KINDS = "qkvo"
        rows_of = {"q": C, "k": KC, "v": KC, "o": C}
        raw = {n: st.sbuf(f"w{n}", [P, rows_of[n], D]) for n in KINDS}
        hi = {n: st.sbuf(f"w{n}_hi", [P, rows_of[n], D], F32R) for n in KINDS}
        lo = {n: st.sbuf(f"w{n}_lo", [P, rows_of[n], D], F32R) for n in KINDS}
        xin = st.sbuf("xin", [P, D])
        xres = st.sbuf("xres", [P, D])
        x_hi = st.sbuf("x_hi", [P, C, P], F32R)
        x_lo = st.sbuf("x_lo", [P, C, P], F32R)
        qs = st.sbuf("qs", [P, NH, W])
        ks = st.sbuf("ks", [P, NH, W])
        qT = st.sbuf("qT", [P, 2, NBLK, P])
        kT = st.sbuf("kT", [P, 2, NBLK, P])
        va = st.sbuf("va", [P, 2, NH, DH + 1])
        nmax = st.sbuf("nmax", [P, 2, H])
        low = st.sbuf("low", [P, 2, H, P])
        prob = st.sbuf("prob", [P, 2, H, P])
        probT = st.sbuf("probT", [P, 2, H, P])
        zn = st.sbuf("zn", [P, D])
        z_hi = st.sbuf("z_hi", [P, C, P], F32R)
        z_lo = st.sbuf("z_lo", [P, C, P], F32R)
        rinv = st.sbuf("rinv", [P, 2, HB])
        y = st.sbuf("y", [P, D])
        yn = st.sbuf("yn", [P, D]) if keep is None else None
        stats = st.sbuf("stats", [P, 6])
        mv = st.sbuf("mv", [P, 2])
        rstd = st.sbuf("rstd", [P, 1])
        mhalf = st.sbuf("mhalf", [P, 1])
        eps = st.sbuf("eps", [P, 1])
        still = st.sbuf("still", [P, 1])
        if causal:
            sm = st.sbuf("sm", [P, 2, H, P])
            mask = st.sbuf("mask", [P, P])
        if rope:
            src = st.sbuf("ctxT", [P, KC, P])
            s_hi = st.sbuf("s_hi", [P, KC, P], F32R)
            s_lo = st.sbuf("s_lo", [P, KC, P], F32R)
            bo = st.sbuf("bo", [P, D])
            pos = st.sbuf("pos", [P, 2 * B])
            freq = st.sbuf("freq", [P, 4])
            ang = st.sbuf("ang", [P, 2, 8 * B])
            turns = st.sbuf("turns", [P, 2, 8 * B])
            tab = st.sbuf("tab", [P, 3, B, 8])
            tc = {n: st.sbuf("tc" + n, [P, D]) for n in "qk"}
            ts = {n: st.sbuf("ts" + n, [P, D]) for n in "qk"}
        else:
            s_hi, s_lo = x_hi, x_lo

        c_in, x_in, r_in, ctx_in, out_st = st.sems("c_in", "x_in", "r_in", "ctx_in", "out_st")
        w_in, w_hi, w_lo = ({n: st.sem(f"{s}_{n}") for n in KINDS} for s in ("in", "hi", "lo"))
        act_sh, g_sl, v_xl, v_zl = st.sems("act_sh", "g_sl", "v_xl", "v_zl")
        pe_x, pe_q, pe_k, pe_v, pe_t, pe_s, pe_pt, pe_z, pe_zt, pe_o = st.sems(
            "pe_x", "pe_q", "pe_k", "pe_v", "pe_t", "pe_s", "pe_pt", "pe_z", "pe_zt", "pe_o")
        act_x, act_v, act_t, act_e, act_pt, act_zt, act_tab = st.sems("act_x", "act_v", "act_t", "act_e", "act_pt", "act_zt", "act_tab")
        v_q, v_k, v_sm, v_nm, v_low, v_ri, v_z, v_y, v_st, v_mv, v_yn, v_tab = st.sems(
            "v_q", "v_k", "v_sm", "v_nm", "v_low", "v_ri", "v_z", "v_y", "v_st", "v_mv", "v_yn", "v_tab")
        g_c, g_q, g_k, g_low, g_x, g_ve, g_rs = st.sems("g_c", "g_q", "g_k", "g_low", "g_x", "g_ve", "g_rs")
        q_ready, k_ready = (g_q, g_k) if rope else (v_q, v_k)
        low_ready = g_low if causal else v_low

        n_const = 16 * (3 if rope else 1)
        block = ctx.enter_context(nc.Block())

        def each_batch(engine, slot):
            for s in range(UN):
                slot(0, s, 0, back=False)
            with engine.Fori(0, B // 2 - 1) as i:
                for par in (1, 0):
                    for s in range(UN):
                        slot(2 * i + 2 - par, s, par)
            for s in range(UN):
                slot(B - 1, s, 1, ahead=False)

        @block.sync
        def _(sp):
            sp.sem_inc(out_st, 16)
            sp.dma_start(xin[:], x_src(0)).then_inc(x_in, 16)
            if rope:
                sp.dma_start(src[:], w_dram["ctxT"][:, 0]).then_inc(ctx_in, 16)
            for n in KINDS:
                sp.dma_start(raw[n][:], w_dram["w" + n]).then_inc(w_in[n], 16)
            sp.dma_start(xres[:], x_src(0)).then_inc(r_in, 16)

            def next_tiles(b):
                sp.wait_ge(pe_x, done(b))
                sp.dma_start(xin[:], x_src(b + 1)).then_inc(x_in, 16)
                if rope:
                    sp.wait_ge(g_sl, done(b))
                    sp.dma_start(src[:], w_dram["ctxT"][:, b + 1]).then_inc(ctx_in, 16)

            def store(b):
                if keep is None:
                    sp.wait_ge(v_yn, done(b))
                    sp.dma_start(x_dst(b), yn[:]).then_inc(out_st, 16)

            def next_residual(b):
                sp.wait_ge(v_y, done(b))
                sp.dma_start(xres[:], x_src(b + 1)).then_inc(r_in, 16)

            next_tiles(0)
            with sp.Fori(0, B - 2) as b:
                next_tiles(b + 1)
                next_residual(b)
                store(b)
            next_residual(B - 2)
            store(B - 2)
            store(B - 1)
            if keep is None:
                sp.wait_ge(out_st, landed(B))

        @block.scalar
        def _(act):
            head_start(act, act_x, act_v, act_t, act_e, act_pt, act_zt, act_sh)
            if rope:
                act.dma_start(pos[:], w_dram["pos"]).then_inc(c_in, 16)
                act.dma_start(freq[:], w_dram["freq"]).then_inc(c_in, 16)
                act.dma_start(bo[:], w_dram["bo"].partition_broadcast(P)).then_inc(c_in, 16)
            else:
                act.dma_start(mask[:], w_dram["mask"]).then_inc(c_in, 16)

            def take_x(b):
                act.wait_ge(pe_x, done(b))
                if not rope:
                    act.wait_ge(pe_v, done(b - 1))
                nc.scalar.copy(x_hi[:], pJ[:, :]).then_inc(act_x, 1)

            def take_context(b):
                if rope:
                    act.wait_ge(ctx_in, landed(b))
                    act.wait_ge(pe_v, done(b - 1))
                    nc.scalar.copy(s_hi[:], src[:]).then_inc(act_sh, 1)

            def take_z(b):
                act.wait_ge(pe_zt, done(b))
                act.wait_ge(pe_o, done(b - 1))
                nc.scalar.copy(z_hi[:], pT[:, :]).then_inc(act_zt, 1)

            def split_hi(n):
                act.wait_ge(w_in[n], 16)
                nc.scalar.copy(hi[n][:], raw[n][:]).then_inc(w_hi[n], 1)

            def take_v(b, par):
                act.wait_ge(pe_v, done(b))
                nc.scalar.copy(va[:, par, :, 0:DH], heads(pJ[:, :], NH)).then_inc(act_v, 1)

            def take_t(b, par, n):
                act.wait_ge(pe_t, done(2 * ROUNDS * b + n))
                t, r = (qT, n) if n < ROUNDS else (kT, n - ROUNDS)
                nc.scalar.copy(t[:, par, 4 * r:4 * r + 4, :], pT[:, :]).then_inc(act_t, 1)

            def take_prob(u, s):
                act.wait_ge(pe_pt, done(u))
                nc.scalar.copy(probT[:, s % 2], pP[:, :]).then_inc(act_pt, 1)

            def slot(b, s, par, back=True, ahead=True):
                u = UN * b + s
                if back or s >= 2:
                    take_prob(u - 2, s)
                act.wait_ge(low_ready, done(u))
                nc.scalar.activation(prob[:, s % 2], low[:, s % 2], ACT.Exp, scale=SCALE).then_inc(act_e, 1)
                for e in events[s]:
                    if e == "x" and ahead:
                        take_x(b + 1)
                    if e == "q" and ahead:
                        take_context(b + 1)
                    if e == "v" and ahead:
                        take_v(b + 1, 1 - par)
                    if e == "zt" and back:
                        take_z(b - 1)
                    if isinstance(e, int) and ahead:
                        take_t(b + 1, 1 - par, e)

            take_x(0)
            take_context(0)
            split_hi("q")
            split_hi("k")
            if rope:
                act.wait_ge(v_tab, 8)
                nc.scalar.activation(tab[:, 1].rearrange("p b f -> p (b f)"), ang[:, 0], ACT.Sin).then_inc(act_tab, 1)
                nc.scalar.activation(tab[:, 0].rearrange("p b f -> p (b f)"), ang[:, 1], ACT.Sin).then_inc(act_tab, 1)
            split_hi("v")
            split_hi("o")
            take_v(0, 0)
            for n in range(2 * ROUNDS):
                take_t(0, 0, n)
            each_batch(act, slot)
            take_prob(UN * B - 2, 0)
            take_prob(UN * B - 1, 1)
            take_z(B - 1)

        @block.gpsimd
        def _(pool):
            head_start(pool, g_q, g_k, g_low, g_x, g_ve, g_rs, g_sl)
            nc.gpsimd.memset(mhalf[:], -0.5).then_inc(g_c, 1)
            nc.gpsimd.memset(va[:], 1.0).then_inc(g_c, 1)
            nc.gpsimd.memset(eps[:], EPS).then_inc(g_c, 1)
            if rope:
                nc.gpsimd.memset(qs[:], 0.0).then_inc(g_c, 1)
                nc.gpsimd.memset(ks[:], 0.0).then_inc(g_c, 1)
            pool.wait_ge(g_c, 5 if rope else 3)
            pool.wait_ge(c_in, n_const)

            def rotated(b):
                for t, o, v_sem, g_sem in (("q", qs, v_q, g_q), ("k", ks, v_k, g_k)):
                    pool.wait_ge(v_sem, done(b))
                    nc.gpsimd.tensor_tensor(o[:, :, 0:DH], heads(tc[t][:], NH), heads(ts[t][:], NH), ALU.add).then_inc(g_sem, 1)

            def context_lo(b):
                if rope:
                    pool.wait_ge(act_sh, done(b))
                    nc.gpsimd.tensor_tensor(s_lo[:], src[:], s_hi[:].bitcast(F32), ALU.subtract).then_inc(g_sl, 1)

            def split_lo(n):
                pool.wait_ge(w_hi[n], 1)
                nc.gpsimd.tensor_tensor(lo[n][:], raw[n][:], hi[n][:].bitcast(F32), ALU.subtract).then_inc(w_lo[n], 1)

            def residual(b):
                if rope:
                    pool.wait_ge(r_in, landed(b))
                    nc.gpsimd.tensor_tensor(xres[:], xres[:], bo[:], ALU.add).then_inc(g_x, 1)

            def norm(b):
                pool.wait_ge(v_mv, done(b))
                nc.gpsimd.tensor_tensor(rstd[:], mv[:, 1:2], eps[:], ALU.add).then_inc(g_ve, 1)
                pool.wait_ge(g_ve, done(b))
                nc.gpsimd.tensor_tensor(rstd[:], rstd[:], mhalf[:], ALU.pow).then_inc(g_rs, 1)

            def slot(b, s, par, back=True, ahead=True):
                u = UN * b + s
                if causal:
                    pool.wait_ge(v_nm, done(u))
                    pool.wait_ge(act_e, done(u - 2))
                    nc.gpsimd.tensor_tensor(low[:, s % 2], sm[:, s % 2], nmax[:, s % 2].unsqueeze(2).to_broadcast([P, H, P]),
                                            ALU.add).then_inc(g_low, 1)
                for e in events[s]:
                    if e == "q" and ahead:
                        context_lo(b + 1)
                    if e == "k" and ahead and rope:
                        rotated(b + 1)
                    if e == "o" and back:
                        norm(b - 1)
                        residual(b)

            context_lo(0)
            split_lo("v")
            if rope:
                rotated(0)
            split_lo("o")
            residual(0)
            each_batch(pool, slot)
            norm(B - 1)

        @block.vector
        def _(dve):
            head_start(dve, v_q, v_k, v_sm, v_nm, v_low, v_ri, v_z, v_y, v_st, v_mv, v_yn, v_xl, v_zl)
            def take(b, ps, t, out, pe_sem, v_sem):
                dve.wait_ge(pe_sem, done(b))
                if not rope:
                    nc.vector.tensor_copy(out[:].rearrange("p h w -> p (h w)"), ps[:, :]).then_inc(v_sem, 1)
                    return
                nc.vector.tensor_tensor(tc[t][:].rearrange("p (n f) -> p n f", f=8), ps[:, :].rearrange("p (n f) -> p n f", f=8),
                                        tab[:, 0, b].unsqueeze(1).to_broadcast([P, 2 * NH, 8]), ALU.mult)
                for half in range(2):
                    o = heads(ts[t][:], NH)[:, :, 8 * half:8 * half + 8]
                    i = heads(ps[:, :], NH)[:, :, 8 - 8 * half:16 - 8 * half]
                    last = nc.vector.tensor_tensor(o, i, tab[:, 2 - half, b].unsqueeze(1).to_broadcast([P, NH, 8]), ALU.mult)
                last.then_inc(v_sem, 1)

            def take_x_lo(b):
                dve.wait_ge(act_x, done(b))
                nc.vector.tensor_tensor(x_lo[:], pJ[:, :].rearrange("p (c t) -> p c t", c=C), x_hi[:].bitcast(F32),
                                        ALU.subtract).then_inc(v_xl, 1)

            def take_z_lo(b):
                dve.wait_ge(act_zt, done(b))
                nc.vector.tensor_tensor(z_lo[:], pT[:, :].rearrange("p (c t) -> p c t", c=C), z_hi[:].bitcast(F32),
                                        ALU.subtract).then_inc(v_zl, 1)

            def split_lo(n):
                dve.wait_ge(w_hi[n], 1)
                nc.vector.tensor_tensor(lo[n][:], raw[n][:], hi[n][:].bitcast(F32), ALU.subtract).then_inc(w_lo[n], 1)

            def take_z(b):
                dve.wait_ge(pe_z, done(UN * b + UN - 1))
                for n in range(2):
                    z = pZ[n][:, 0:HB * (DH + 1)].rearrange("p (h d) -> p h d", h=HB)
                    last = nc.vector.reciprocal(rinv[:, n], z[:, :, DH])
                last.then_inc(v_ri, 1)
                dve.wait_ge(v_ri, done(b))
                for n in range(2):
                    z = pZ[n][:, 0:HB * (DH + 1)].rearrange("p (h d) -> p h d", h=HB)
                    last = nc.vector.tensor_tensor(heads(zn[:, n * D // 2:(n + 1) * D // 2], HB), z[:, :, 0:DH],
                                                   rinv[:, n].unsqueeze(2).to_broadcast([P, HB, DH]), ALU.mult)
                last.then_inc(v_z, 1)

            def norm(b):
                dve.wait_ge(pe_o, done(b))
                if rope:
                    dve.wait_ge(g_x, done(b))
                else:
                    dve.wait_ge(r_in, landed(b))
                nc.vector.tensor_tensor(y[:], pO[:, :], xres[:], ALU.add).then_inc(v_y, 1)
                dve.wait_ge(v_y, done(b))
                nc.vector.bn_stats(stats[:], y[:]).then_inc(v_st, 1)
                dve.wait_ge(v_st, done(b))
                carry_wait(nc.vector, still)
                nc.vector.bn_aggr(mv[:], stats[:]).then_inc(v_mv, 1)

            def normed(b):
                dve.wait_ge(g_rs, done(b))
                if keep is None:
                    dve.wait_ge(out_st, landed(b))
                nc.vector.tensor_scalar(yn[:] if keep is None else keep[:, b, :], y[:], mv[:, 0:1], rstd[:], ALU.subtract, ALU.mult).then_inc(v_yn, 1)

            def slot(b, s, par, back=True, ahead=True):
                u = UN * b + s
                dve.wait_ge(pe_s, done(u))
                nb = nmax[:, s % 2].unsqueeze(2).to_broadcast([P, H, P])
                if causal:
                    dve.wait_ge(g_low, done(u - 2))
                    nc.vector.tensor_tensor(sm[:, s % 2], heads(pS[s % 2][:, :], H), mask[:].unsqueeze(1).to_broadcast([P, H, P]),
                                            ALU.add).then_inc(v_sm, 1)
                    dve.wait_ge(v_sm, done(u))
                    nc.vector.tensor_reduce(nmax[:, s % 2], sm[:, s % 2], AX.X, ALU.max, negate=True).then_inc(v_nm, 1)
                else:
                    nc.vector.tensor_reduce(nmax[:, s % 2], heads(pS[s % 2][:, :], H), AX.X, ALU.max, negate=True).then_inc(v_nm, 1)
                    dve.wait_ge(v_nm, done(u))
                    dve.wait_ge(act_e, done(u - 2))
                    nc.vector.tensor_tensor(low[:, s % 2], heads(pS[s % 2][:, :], H), nb, ALU.add).then_inc(v_low, 1)
                if s == 2 and back:
                    take_z(b - 1)
                for e in events[s]:
                    if e == "x" and ahead:
                        take_x_lo(b + 1)
                    if e == "zt" and back:
                        take_z_lo(b - 1)
                    if e == "q" and ahead:
                        take(b + 1, pJ, "q", qs, pe_q, v_q)
                    if e == "k" and ahead:
                        take(b + 1, pJ, "k", ks, pe_k, v_k)
                    if e == "o" and back:
                        norm(b - 1)
                    if e == "n" and back:
                        normed(b - 1)

            take_x_lo(0)
            split_lo("q")
            split_lo("k")
            dve.wait_ge(c_in, n_const)
            if rope:
                two_pi = 2 * np.pi
                pi_hi = float(np.float32(6.28125))
                pi_lo = float(np.float32(two_pi - pi_hi))
                magic = 12582912.0
                nc.vector.tensor_tensor(ang[:, 0].rearrange("p (n f) -> p n f", f=4), pos[:].unsqueeze(2).to_broadcast([P, 2 * B, 4]),
                                        freq[:].unsqueeze(1).to_broadcast([P, 2 * B, 4]), ALU.mult).then_inc(v_tab, 1)
                dve.wait_ge(v_tab, 1)
                nc.vector.tensor_scalar(ang[:, 1], ang[:, 0], float(np.pi / 2), None, ALU.add).then_inc(v_tab, 1)
                dve.wait_ge(v_tab, 2)
                nc.vector.tensor_scalar(turns[:], ang[:], float(1 / two_pi), magic, ALU.mult, ALU.add).then_inc(v_tab, 1)
                dve.wait_ge(v_tab, 3)
                nc.vector.tensor_scalar(turns[:], turns[:], -magic, None, ALU.add).then_inc(v_tab, 1)
                dve.wait_ge(v_tab, 4)
                nc.vector.scalar_tensor_tensor(out=ang[:], in0=turns[:], scalar=-pi_hi, in1=ang[:], op0=ALU.mult, op1=ALU.add).then_inc(v_tab, 1)
                dve.wait_ge(v_tab, 5)
                nc.vector.scalar_tensor_tensor(out=ang[:], in0=turns[:], scalar=-pi_lo, in1=ang[:], op0=ALU.mult, op1=ALU.add).then_inc(v_tab, 1)
                dve.wait_ge(v_tab, 6)
                nc.vector.tensor_scalar(ang[:], ang[:], 3.1415925, -3.1415925, ALU.min, ALU.max).then_inc(v_tab, 2)
                dve.wait_ge(act_tab, 2)
                nc.vector.tensor_scalar(tab[:, 2], tab[:, 1], -1.0, None, ALU.mult).then_inc(v_tab, 1)
                dve.wait_ge(v_tab, 9)
                dve.wait_ge(g_c, 5)
            take(0, pJ, "q", qs, pe_q, v_q)
            take(0, pJ, "k", ks, pe_k, v_k)
            each_batch(dve, slot)
            take_z(B - 1)
            take_z_lo(B - 1)
            norm(B - 1)
            normed(B - 1)

        @block.tensor
        def _(pe):
            head_start(pe, pe_x, pe_q, pe_k, pe_v, pe_t, pe_s, pe_pt, pe_z, pe_zt, pe_o)

            def turn_x(b):
                pe.wait_ge(x_in, landed(b))
                pe.wait_ge(act_v, done(b - 1))
                for c in range(C):
                    last = nc.tensor.transpose(pJ[:, P * c:P * c + P], xin[:, P * c:P * c + P], ident[:])
                last.then_inc(pe_x, 1)

            def project(n, ps, a_hi, a_lo, sem):
                for c in range(rows_of[n]):
                    last = split_product(nc, ps[:, :], a_hi[:, c, :], a_lo[:, c, :], hi[n][:, c, :], lo[n][:, c, :],
                                         start=c == 0, stop=c == rows_of[n] - 1)
                last.then_inc(sem, 1)

            def project_q(b):
                pe.wait_ge(v_xl, done(b))
                project("q", pJ, x_hi, x_lo, pe_q)

            def project_k(b):
                if rope:
                    pe.wait_ge(g_sl, done(b))
                pe.wait_ge(v_q, done(b))
                project("k", pJ, s_hi, s_lo, pe_k)

            def project_v(b):
                pe.wait_ge(v_k, done(b))
                project("v", pJ, s_hi, s_lo, pe_v)

            def turn(b, n):
                src, r = (qs, n) if n < ROUNDS else (ks, n - ROUNDS)
                pe.wait_ge(q_ready if n < ROUNDS else k_ready, done(b))
                pe.wait_ge(act_t, done(2 * ROUNDS * b + n - 1))
                pe.wait_ge(v_zl, done(b - 2))
                flat = src[:].rearrange("p h w -> p (h w)")
                for j in range(4):
                    last = nc.tensor.transpose(pT[:, P * j:P * j + P], flat[:, P * (4 * r + j):P * (4 * r + j + 1)], ident[:])
                last.then_inc(pe_t, 1)

            def place(s, j):
                r, block_ = s % 4, 4 * (s // 4) + j
                return 4 * block_ + r, slice(W * r, W * r + W), block_

            def turn_prob(u, s):
                pe.wait_ge(act_e, done(u))
                pe.wait_ge(act_pt, done(u - 1))
                for j in range(H):
                    last = nc.tensor.transpose(pP[:, P * j:P * j + P], prob[:, s % 2, j, :], ident[:])
                last.then_inc(pe_pt, 1)

            def probs_v(u, b, s, par):
                pe.wait_ge(act_pt, done(u))
                if s == 0:
                    pe.wait_ge(act_v, done(b))
                    pe.wait_ge(v_z, done(b - 1))
                for j in range(H):
                    h = place(s, j)[0]
                    col = (h % HB) * (DH + 1)
                    last = nc.tensor.matmul(pZ[h // HB][:, col:col + DH + 1], probT[:, s % 2, j, :], va[:, par, h, :],
                                            start=True, stop=True)
                last.then_inc(pe_z, 1)

            def turn_z(b):
                pe.wait_ge(v_z, done(b))
                pe.wait_ge(act_t, done(2 * ROUNDS * (b + 1) + 2 * ROUNDS - 1))
                for c in range(C):
                    last = nc.tensor.transpose(pT[:, P * c:P * c + P], zn[:, P * c:P * c + P], ident[:])
                last.then_inc(pe_zt, 1)

            def output(b):
                pe.wait_ge(v_zl, done(b))
                pe.wait_ge(v_y, done(b - 1))
                project("o", pO, z_hi, z_lo, pe_o)

            def slot(b, s, par, back=True, ahead=True):
                u = UN * b + s
                early = "zt" not in events[s]
                if s == 0:
                    pe.wait_ge(act_t, done(2 * ROUNDS * b + 2 * ROUNDS - 1))
                pe.wait_ge(v_sm if causal else v_low, done(u - 2))
                for j in range(H):
                    _, rows, blk = place(s, j)
                    last = nc.tensor.matmul(pS[s % 2][:, P * j:P * j + P], qT[rows, par, blk, :], kT[rows, par, blk, :],
                                            start=True, stop=True)
                last.then_inc(pe_s, 1)
                if early:
                    for e in events[s]:
                        if isinstance(e, int) and ahead:
                            turn(b + 1, e)
                if back or s >= 2:
                    turn_prob(u - 2, s)
                if back or s >= 3:
                    s3 = (s - 3) % UN
                    here = s >= 3
                    probs_v(u - 3, b if here else b - 1, s3, par if here else 1 - par)
                for e in events[s]:
                    if ahead:
                        if e == "x":
                            turn_x(b + 1)
                        if e == "q":
                            project_q(b + 1)
                        if e == "k":
                            project_k(b + 1)
                        if e == "v":
                            project_v(b + 1)
                        if isinstance(e, int) and not early:
                            turn(b + 1, e)
                    if back:
                        if e == "zt":
                            turn_z(b - 1)
                        if e == "o":
                            output(b - 1)

            turn_x(0)
            pe.wait_ge(w_lo["q"], 1)
            project_q(0)
            pe.wait_ge(w_lo["k"], 1)
            project_k(0)
            pe.wait_ge(w_lo["v"], 1)
            pe.wait_ge(g_c, 3)
            project_v(0)
            for n in range(2 * ROUNDS):
                turn(0, n)
            pe.wait_ge(w_lo["o"], 1)
            each_batch(pe, slot)
            last_u = UN * B - 1
            turn_prob(last_u - 1, 0)
            probs_v(last_u - 2, B - 1, UN - 3, 1)
            turn_prob(last_u, 1)
            probs_v(last_u - 1, B - 1, UN - 2, 1)
            probs_v(last_u, B - 1, UN - 1, 1)
            pe.wait_ge(v_z, done(B - 1))
            for c in range(C):
                last = nc.tensor.transpose(pT[:, P * c:P * c + P], zn[:, P * c:P * c + P], ident[:])
            last.then_inc(pe_zt, 1)
            output(B - 1)


EVENTS_8 = [["x"], [], ["q"], ["zt", "k", 0], [1], [2, "o"], [3, "n", "v"], []]
EVENTS_4 = [[], [], ["x"], ["q", "zt", "k", 0, "o", 1, "n", "v"]]


class Chain:

    def __init__(self, engine, sem):
        self.engine, self.sem, self.n = engine, sem, 0

    def __call__(self, ins):
        self.n += 1
        ins.then_inc(self.sem, 1)
        self.engine.wait_ge(self.sem, self.n)


def in_turns(engine, slot, rounds, ring):
    slot(0, 0, back=False)
    with engine.Fori(0, rounds - 1) as i:
        for n in range(1, ring):
            slot(i, n)
        slot(i + 1, 0)
    for n in range(1, ring):
        slot(rounds - 1, n, ahead=n < ring - 1)


def following(i, n, ring):
    return (i, n + 1) if n < ring - 1 else (i + 1, 0)


def preceding(i, n, ring):
    return (i, n - 1) if n else (i - 1, ring - 1)


class SharedExpert:

    COUNT = 8

    def __init__(self, nc, st, psum, ident, xall, w_dram, base, first):
        self.nc, self.ident, self.xall, self.w_dram, self.base, self.first = nc, ident, xall, w_dram, base, first
        self.pX, self.pG, self.pU, self.pO = psum[0:4]
        self.wg, self.wu, self.wd = (st.sbuf(n, [P, C, D]) for n in ("wg", "wu", "wd"))
        self.xT = st.sbuf("sxT", [P, 2, C, P])
        self.gate = st.sbuf("gate", [P, C, P])
        self.h = st.sbuf("h", [P, C, P])
        self.wg_in, self.wu_in, self.wd_in, self.pe_x, self.pe_g, self.pe_u, self.pe_o = st.sems(
            "wg_in", "wu_in", "wd_in", "pe_x", "pe_g", "pe_u", "pe_o")
        self.act_x, self.act_g, self.v_h, self.v_b = st.sems("act_x", "act_g", "v_h", "v_b")

    def load(self, sp):
        sp.dma_start(self.wg[:], self.w_dram["sg"]).then_inc(self.wg_in, 16)
        sp.dma_start(self.wu[:], self.w_dram["su"]).then_inc(self.wu_in, 16)
        sp.dma_start(self.wd[:], self.w_dram["sd"]).then_inc(self.wd_in, 16)

    def scalar(self, act):
        nc = self.nc
        head_start(act, self.act_x, self.act_g)
        for k in range(-1, self.COUNT):
            if k >= 0:
                act.wait_ge(self.pe_g, done(k))
                act.wait_ge(self.v_h, done(k - 1))
                nc.scalar.activation(self.gate[:], self.pG[:, :], ACT.Silu).then_inc(self.act_g, 1)
            if k < self.COUNT - 1:
                act.wait_ge(self.pe_x, done(k + 1))
                nc.scalar.copy(self.xT[:, (k + 1) % 2], self.pX[:, :]).then_inc(self.act_x, 1)

    def hidden(self, dve, k):
        dve.wait_ge(self.act_g, done(k))
        dve.wait_ge(self.pe_u, done(k))
        self.nc.vector.tensor_tensor(self.h[:], self.gate[:], self.pU[:, :].rearrange("p (c t) -> p c t", c=C),
                                     ALU.mult).then_inc(self.v_h, 1)

    def add(self, dve, k):
        dve.wait_ge(self.pe_o, done(k))
        self.nc.vector.tensor_tensor(self.base[:, self.first + k, :], self.pO[:, :], self.xall[:, self.first + k, :],
                                     ALU.add).then_inc(self.v_b, 1)

    def tensor(self, pe):
        nc = self.nc
        head_start(pe, self.pe_x, self.pe_g, self.pe_u, self.pe_o)

        def turn_x(k):
            pe.wait_ge(self.act_x, done(k - 1))
            for c in range(C):
                step = nc.tensor.transpose(self.pX[:, P * c:P * c + P], self.xall[:, self.first + k, P * c:P * c + P],
                                           self.ident[:])
            step.then_inc(self.pe_x, 1)

        def up(ps, w, k, sem):
            for i in range(C):
                for c in range(C):
                    step = nc.tensor.matmul(ps[:, P * i:P * i + P], w[:, c, P * i:P * i + P], self.xT[:, k % 2, c, :],
                                            start=c == 0, stop=c == C - 1)
            step.then_inc(sem, 1)

        def down(k):
            pe.wait_ge(self.v_h, done(k))
            pe.wait_ge(self.v_b, done(k - 1))
            for c in range(C):
                step = nc.tensor.matmul(self.pO[:, :], self.h[:, c, :], self.wd[:, c, :], start=c == 0, stop=c == C - 1)
            step.then_inc(self.pe_o, 1)

        turn_x(0)
        pe.wait_ge(self.wg_in, 16)
        for k in range(self.COUNT):
            pe.wait_ge(self.act_x, done(k))
            if k < self.COUNT - 1:
                turn_x(k + 1)
            pe.wait_ge(self.act_g, done(k - 1))
            up(self.pG, self.wg, k, self.pe_g)
            if k == 1:
                pe.wait_ge(self.wd_in, 16)
            if k:
                down(k - 1)
            else:
                pe.wait_ge(self.wu_in, 16)
            pe.wait_ge(self.v_h, done(k - 1))
            up(self.pU, self.wu, k, self.pe_u)
        down(self.COUNT - 1)


def route(nc, name, psum, tri, ones, logits, w_dram, NE, K, weight, slot_in, slot_out, grouped):
    NG, CAP, DROPPED = 8, 80, 80 * 32
    with ExitStack() as ctx:
        st = Stage(nc, ctx, name)
        pPos, pTot = psum[0], psum[1]
        iota = st.sbuf("iota", [P, 128])
        top = st.sbuf("top", [P, B, 8])
        topi = st.sbuf("topi", [P, B, 8], U32)
        topf = st.sbuf("topf", [P, B, 8])
        hot = st.sbuf("hot", [P, K, B, NE])
        sel = st.sbuf("sel", [P, B, NE])
        pos = st.sbuf("pos", [P, B, NE])
        carry = st.sbuf("carry", [P, B + 1, NE])
        prod = st.sbuf("prod", [P, B, NE])
        rowf = st.sbuf("rowf", [P, B, K])
        wsum = st.sbuf("wsum", [P, B])
        wt = st.sbuf("wt", [P, B, K])
        if grouped:
            bias = st.sbuf("bias", [P, NE])
            score = st.sbuf("score", [P, B, NE])
            biased = st.sbuf("biased", [P, B, NE])
            masked = st.sbuf("masked", [P, B, NE])
            pair = st.sbuf("pair", [P, B * NG])
            gscore = st.sbuf("gscore", [P, B, NG])
            gtop = st.sbuf("gtop", [P, B, 8])
            gtopi = st.sbuf("gtopi", [P, B, 8], U32)
            gtopf = st.sbuf("gtopf", [P, B, 8])
            gmask = st.sbuf("gmask", [P, B, NG])
            geq = st.sbuf("geq", [P, B, NG])
            over = st.sbuf("over", [P, B, NE])
        else:
            NT, PAIR = slot_out["pairs"], 2 * P
            expd = st.sbuf("expd", [P, B])
            cmp = st.sbuf("cmp", [P, NE, B])
            ntile = st.sbuf("ntile", [P, NE])
            first = st.sbuf("first", [P, NE + 1])
            tcmp = st.sbuf("tcmp", [P, NT, NE])
            texp = st.sbuf("texp", [P, NT])
        c_in, v, act_s, pe_c = st.sems("c_in", "v", "act_s", "pe_c")
        block = ctx.enter_context(nc.Block())
        n_sel = []

        def flat(t):
            return t[:].rearrange("p b e -> p (b e)")

        @block.sync
        def _(sp):
            sp.dma_start(iota[:], w_dram["iota"]).then_inc(c_in, 16)
            if grouped:
                sp.dma_start(bias[:], w_dram["bias"].partition_broadcast(P)).then_inc(c_in, 16)

        @block.vector
        def _(dve):
            step = Chain(dve, v)
            vec = nc.vector
            iota_e = iota[:, 0:NE].unsqueeze(1).to_broadcast([P, B, NE])
            dve.wait_ge(c_in, 32 if grouped else 16)
            ranked = logits
            if grouped:
                dve.wait_ge(act_s, 1)
                step(vec.tensor_tensor(biased[:], score[:], bias[:].unsqueeze(1).to_broadcast([P, B, NE]), ALU.add))
                q = flat(biased).rearrange("p (g m) -> p g m", m=4)
                gs = flat(gscore)
                for n, (i, j) in enumerate([(0, 1), (0, 2), (0, 3), (1, 2), (1, 3), (2, 3)]):
                    step(vec.tensor_tensor(pair[:] if n else gs, q[:, :, i], q[:, :, j], ALU.add))
                    if n:
                        step(vec.tensor_tensor(gs, gs, pair[:], ALU.max))
                for b in range(B):
                    last = vec.max(gtop[:, b], gscore[:, b])
                step(last)
                for b in range(B):
                    last = vec.max_index(gtopi[:, b], gtop[:, b], gscore[:, b])
                step(last)
                step(vec.tensor_copy(gtopf[:], gtopi[:]))
                iota_g = iota[:, 0:NG].unsqueeze(1).to_broadcast([P, B, NG])
                for k in range(3):
                    step(vec.tensor_tensor(geq[:] if k else gmask[:], iota_g, gtopf[:, :, k:k + 1].to_broadcast([P, B, NG]), ALU.is_equal))
                    if k:
                        step(vec.tensor_tensor(gmask[:], gmask[:], geq[:], ALU.add))
                step(vec.tensor_tensor(flat(masked).rearrange("p (g m) -> p g m", m=4), q,
                                       flat(gmask).unsqueeze(2).to_broadcast([P, B * NG, 4]), ALU.mult))
                ranked = masked
            for b in range(B):
                last = vec.max(top[:, b], ranked[:, b])
            step(last)
            for b in range(B):
                last = vec.max_index(topi[:, b], top[:, b], ranked[:, b])
            step(last)
            step(vec.tensor_copy(topf[:], topi[:]))
            for k in range(K):
                step(vec.tensor_tensor(hot[:, k], iota_e, topf[:, :, k:k + 1].to_broadcast([P, B, NE]), ALU.is_equal))
                if k:
                    step(vec.tensor_tensor(sel[:], hot[:, k] if k > 1 else hot[:, 1], sel[:] if k > 1 else hot[:, 0], ALU.add))
            n_sel.append(step.n)

            if grouped:
                for k in range(K):
                    step(vec.tensor_tensor(prod[:], hot[:, k], score[:], ALU.mult))
                    step(vec.tensor_reduce(wt[:, :, k], prod[:], AX.X, ALU.add))
                step(vec.tensor_reduce(wsum[:], wt[:], AX.X, ALU.add))
                step(vec.tensor_scalar(wsum[:], wsum[:], 1e-20, None, ALU.add))
                step(vec.reciprocal(wsum[:], wsum[:]))
                step(vec.tensor_tensor(wt[:], wt[:], wsum[:].unsqueeze(2).to_broadcast([P, B, K]), ALU.mult))
                step(vec.tensor_scalar(weight[:], wt[:], 2.5, None, ALU.mult))
            else:
                step(vec.tensor_tensor(wsum[:], top[:, :, 1], top[:, :, 0], ALU.subtract))
                n_sel.append(step.n)
                dve.wait_ge(act_s, 1)
                step(vec.tensor_scalar(wsum[:], expd[:], 1.0, None, ALU.add))
                step(vec.reciprocal(weight[:, :, 0], wsum[:]))
                step(vec.tensor_tensor(weight[:, :, 1], weight[:, :, 0], expd[:], ALU.mult))

            step(vec.memset(carry[:, 0], 0.0))
            dve.wait_ge(pe_c, 1)
            for b in range(B):
                step(vec.tensor_tensor(carry[:, b + 1], carry[:, b], pTot[:, NE * b:NE * b + NE], ALU.add))
            step(vec.tensor_tensor(pos[:], pPos[:, 0:B * NE].rearrange("p (b e) -> p b e", b=B), carry[:, 0:B], ALU.add))
            if grouped:
                step(vec.tensor_scalar(over[:], pos[:], float(CAP), 2.0 * DROPPED, ALU.is_ge, ALU.mult))
                step(vec.tensor_tensor(pos[:], pos[:], over[:], ALU.add))
                step(vec.tensor_scalar(prod[:], iota_e, float(CAP), None, ALU.mult))
                step(vec.tensor_tensor(pos[:], pos[:], prod[:], ALU.add))
                step(vec.tensor_scalar(pos[:], pos[:], float(DROPPED), None, ALU.min))
            else:
                step(vec.tensor_scalar(cmp[:], iota[:, 0:B].unsqueeze(1).to_broadcast([P, NE, B]), float(PAIR), None, ALU.mult))
                step(vec.tensor_tensor(cmp[:], carry[:, B].unsqueeze(2).to_broadcast([P, NE, B]), cmp[:], ALU.is_gt))
                step(vec.tensor_reduce(ntile[:], cmp[:], AX.X, ALU.add))
                step(vec.memset(first[:, 0:1], 0.0))
                for e in range(NE):
                    step(vec.tensor_tensor(first[:, e + 1:e + 2], first[:, e:e + 1], ntile[:, e:e + 1], ALU.add))
                step(vec.tensor_scalar(ntile[:], first[:, 0:NE], float(PAIR), None, ALU.mult))
                step(vec.tensor_tensor(pos[:], pos[:], ntile[:].unsqueeze(1).to_broadcast([P, B, NE]), ALU.add))
                step(vec.tensor_tensor(tcmp[:], iota[:, 0:NT].unsqueeze(2).to_broadcast([P, NT, NE]),
                                       first[:, 1:NE + 1].unsqueeze(1).to_broadcast([P, NT, NE]), ALU.is_ge))
                step(vec.tensor_reduce(texp[:], tcmp[:], AX.X, ALU.add))
                step(vec.tensor_scalar(slot_out["expert"][:], texp[:], float(NE - 1), None, ALU.min))
            for k in range(K):
                step(vec.tensor_tensor(prod[:], hot[:, k], pos[:], ALU.mult))
                step(vec.tensor_reduce(rowf[:, :, k], prod[:], AX.X, ALU.add))
            step(vec.tensor_copy(slot_in[:], rowf[:]))

        @block.scalar
        def _(act):
            if grouped:
                nc.scalar.activation(score[:], logits[:], ACT.Sigmoid).then_inc(act_s, 1)
            else:
                act.wait_ge(v, n_sel[1])
                nc.scalar.activation(expd[:], wsum[:], ACT.Exp).then_inc(act_s, 1)

        @block.tensor
        def _(pe):
            pe.wait_ge(v, n_sel[0])
            nc.tensor.matmul(pPos[:, 0:B * NE], tri[:], flat(sel), start=True, stop=True)
            nc.tensor.matmul(pTot[:, 0:B * NE], ones[:], flat(sel), start=True, stop=True).then_inc(pe_c, 1)


def dispatch(nc, name, xall, rows, packed, K, bound, ready, shared=None):
    with ExitStack() as ctx:
        st = Stage(nc, ctx, name)
        sent = st.sem("sent")
        if shared:
            part = shared(st)
        block = ctx.enter_context(nc.Block())

        if shared:
            @block.sync
            def _(sp):
                part.load(sp)

        @block.gpsimd
        def _(pool):
            for s, value in ready:
                pool.wait_ge(s, value)
            for b in range(B):
                for k in range(K):
                    nc.gpsimd.indirect_dma_start(packed, bass.IndirectOffsetOnAxis(ap=rows[:, b, k:k + 1], axis=0),
                                                 xall[:, b, :], None, bounds_check=bound, oob_is_err=False).then_inc(sent, 16)
            pool.wait_ge(sent, 16 * K * B)

        if shared:
            @block.scalar
            def _(act):
                part.scalar(act)

            @block.vector
            def _(dve):
                head_start(dve, part.v_h, part.v_b)
                for k in range(part.COUNT):
                    part.hidden(dve, k)
                    if k:
                        part.add(dve, k - 1)
                part.add(dve, part.COUNT - 1)

            @block.tensor
            def _(pe):
                part.tensor(pe)


class CappedWeights:

    NE, F, R = 32, 256, 8

    def __init__(self, st, w_dram):
        self.w_dram = w_dram
        self.wg = st.sbuf("wg", [P, self.R, C, self.F])
        self.wu = st.sbuf("wu", [P, self.R, C, self.F])
        self.wd = st.sbuf("wd", [P, self.R, self.F // P, D])
        self.w_in = [st.sem(f"w_in{n}") for n in range(self.R)]

    def load(self, sp, e, n):
        for t, name in ((self.wg, "wg"), (self.wu, "wu"), (self.wd, "wd")):
            sp.dma_start(t[:, n], self.w_dram[name][e]).then_inc(self.w_in[n], 16)

    def load_first(self, sp):
        for n in range(self.R):
            self.load(sp, n, n)


def capped_experts(nc, psum, ident, packed, result, zero, weights):
    NE, CAP, F, R = weights.NE, 80, weights.F, weights.R
    FC = F // P
    with ExitStack() as ctx:
        st = Stage(nc, ctx, "m")
        pX, pG, pU, pO = psum[0:2], psum[2:4], psum[4:6], psum[6:8]
        xe = st.sbuf("xe", [CAP, R, D])
        wg, wu, wd, w_in = weights.wg, weights.wu, weights.wd, weights.w_in
        xT = st.sbuf("xT", [P, 2, C, CAP])
        gate = st.sbuf("gate", [P, 2, FC, CAP])
        h = st.sbuf("h", [P, 2, FC, CAP])
        ye = st.sbuf("ye", [CAP, 2, D])
        x_in = [st.sem(f"x_in{n}") for n in range(R)]
        y_out = [st.sem(f"y_out{n}") for n in range(2)]
        z_out, pe_x, pe_g, pe_u, pe_o, act_g, act_y, v_x, v_h = st.sems(
            "z_out", "pe_x", "pe_g", "pe_u", "pe_o", "act_g", "act_y", "v_x", "v_h")
        block = ctx.enter_context(nc.Block())

        @block.sync
        def _(sp):
            def load(i, n):
                sp.dma_start(xe[:, n, :], packed[R * i + n]).then_inc(x_in[n], 16)
                if not (isinstance(i, int) and i == 0):
                    weights.load(sp, R * i + n, n)

            def store(i, n):
                sp.wait_ge(act_y, done(R * i + n))
                sp.dma_start(result[0:NE * CAP].rearrange("(e r) d -> e r d", r=CAP)[R * i + n], ye[:, n % 2, :]).then_inc(y_out[n % 2], 16)

            for n in range(2):
                sp.sem_inc(y_out[n], 16)
            for n in range(R):
                load(0, n)
            sp.dma_start(result[NE * CAP:NE * CAP + 1, :], zero[0:1, :]).then_inc(z_out, 16)
            with sp.Fori(0, NE // R - 1) as i:
                for n in range(R):
                    sp.wait_ge(pe_o, done(R * i + n))
                    load(i + 1, n)
                    store(i, n)
            for n in range(R):
                store(NE // R - 1, n)
            sp.wait_ge(z_out, 16)
            for n in range(2):
                sp.wait_ge(y_out[n], landed(NE // 2))

        @block.scalar
        def _(act):
            head_start(act, act_g, act_y)

            def take_y(i, n):
                e = R * i + n
                act.wait_ge(pe_o, done(e))
                act.wait_ge(y_out[n % 2], landed(R // 2 * i + n // 2))
                nc.scalar.copy(ye[:, n % 2, :], pO[n % 2][0:CAP, :]).then_inc(act_y, 1)

            def slot(i, n, back=True, ahead=True):
                e = R * i + n
                act.wait_ge(pe_g, done(e))
                act.wait_ge(v_h, done(e - 2))
                nc.scalar.activation(gate[:, n % 2], pG[n % 2][:, 0:FC * CAP].rearrange("p (c t) -> p c t", c=FC),
                                     ACT.Silu).then_inc(act_g, 1)
                if back:
                    take_y(*preceding(i, n, R))

            in_turns(act, slot, NE // R, R)
            take_y(NE // R - 1, R - 1)

        @block.vector
        def _(dve):
            head_start(dve, v_x, v_h)

            def take_x(i, n):
                dve.wait_ge(pe_x, done(R * i + n))
                nc.vector.tensor_copy(xT[:, n % 2], pX[n % 2][:, 0:C * CAP].rearrange("p (c t) -> p c t", c=C)).then_inc(v_x, 1)

            def slot(i, n, back=True, ahead=True):
                e = R * i + n
                if ahead:
                    take_x(*following(i, n, R))
                dve.wait_ge(act_g, done(e))
                dve.wait_ge(pe_u, done(e))
                nc.vector.tensor_tensor(h[:, n % 2], gate[:, n % 2], pU[n % 2][:, 0:FC * CAP].rearrange("p (c t) -> p c t", c=FC),
                                        ALU.mult).then_inc(v_h, 1)

            take_x(0, 0)
            in_turns(dve, slot, NE // R, R)

        @block.tensor
        def _(pe):
            head_start(pe, pe_x, pe_g, pe_u, pe_o)

            def turn_x(i, n):
                pe.wait_ge(x_in[n], landed(i))
                for c in range(C):
                    last = nc.tensor.transpose(pX[n % 2][:, CAP * c:CAP * c + CAP], xe[:, n, P * c:P * c + P], ident[0:CAP, 0:CAP])
                last.then_inc(pe_x, 1)

            def up(ps, w, n, sem):
                for f in range(FC):
                    for c in range(C):
                        last = nc.tensor.matmul(ps[n % 2][:, CAP * f:CAP * f + CAP], w[:, n, c, P * f:P * f + P],
                                                xT[:, n % 2, c, :], start=c == 0, stop=c == C - 1)
                last.then_inc(sem, 1)

            def down(i, n):
                e = R * i + n
                pe.wait_ge(v_h, done(e))
                pe.wait_ge(act_y, done(e - 2))
                for f in range(FC):
                    last = nc.tensor.matmul(pO[n % 2][0:CAP, :], h[:, n % 2, f, :], wd[:, n, f, :], start=f == 0, stop=f == FC - 1)
                last.then_inc(pe_o, 1)

            def slot(i, n, back=True, ahead=True):
                e = R * i + n
                if ahead:
                    turn_x(*following(i, n, R))
                pe.wait_ge(w_in[n], 48 * (i + 1))
                pe.wait_ge(v_x, done(e))
                pe.wait_ge(act_g, done(e - 2))
                up(pG, wg, n, pe_g)
                pe.wait_ge(v_h, done(e - 2))
                up(pU, wu, n, pe_u)
                if back:
                    down(*preceding(i, n, R))

            turn_x(0, 0)
            in_turns(pe, slot, NE // R, R)
            down(NE // R - 1, R - 1)


def routed_experts(nc, psum, ident, packed, result, expert, w_dram, NP):
    NE, F, R = 8, 352, 4
    FC = 3
    NT = 2 * NP
    rows = [P, P, F - 2 * P]
    with ExitStack() as ctx:
        st = Stage(nc, ctx, "n")
        pX, pH, pG, pU, pO = psum[0], psum[1], psum[2:4], psum[4:6], psum[6:8]
        xe = st.sbuf("xe", [P, R, D])
        shape = {"g": [P, 2, C, F], "u": [P, 2, C, F], "d": [P, 2, FC, D]}
        raw = {k: st.sbuf(f"w{k}", shape[k]) for k in "gud"}
        hi = {k: st.sbuf(f"w{k}_hi", shape[k], F32R) for k in "gud"}
        lo = {k: st.sbuf(f"w{k}_lo", shape[k], F32R) for k in "gud"}
        x_hi, x_lo = (st.sbuf(n, [P, 2, C, P], F32R) for n in ("x_hi", "x_lo"))
        gate = st.sbuf("gate", [P, 2, F])
        h = st.sbuf("h", [P, 2, F])
        h_hi, h_lo = (st.sbuf(n, [P, 2, FC, P], F32R) for n in ("h_hi", "h_lo"))
        ye = st.sbuf("ye", [P, R, D])
        x_in, y_out = ([st.sem(f"{s}{n}") for n in range(R)] for s in ("x_in", "y_out"))
        gate_in, up_in, d_in = ([st.sem(f"{s}{w}") for w in range(2)] for s in ("gate_in", "up_in", "d_in"))
        act_gate, act_d, v_gate, v_up, g_u, g_d = st.sems("act_gate", "act_d", "v_gate", "v_up", "g_u", "g_d")
        pe_x, pe_g, pe_u, pe_h, pe_o, act_x, act_g, act_h, v_x, v_y, v_h, v_hl = st.sems(
            "pe_x", "pe_g", "pe_u", "pe_h", "pe_o", "act_x", "act_g", "act_h", "v_x", "v_y", "v_h", "v_hl")
        block = ctx.enter_context(nc.Block())

        def each_down(t, w):
            return t[:, w, 0:2], t[0:rows[2], w, 2]

        @block.sync
        def _(sp):
            def load_x(i, n):
                sp.dma_start(xe[:, n, :], packed[R * i + n]).then_inc(x_in[n], 16)

            def load(i, w):
                e = sp.value_load(expert[0:1, bass.ds(2 * i + w, 1)], min_val=0, max_val=NE - 1)
                sp.dma_start(raw["g"][:, w], w_dram["wg"][e]).then_inc(gate_in[w], 16)
                sp.dma_start(raw["u"][:, w], w_dram["wu"][e]).then_inc(up_in[w], 16)
                for part, name in zip(each_down(raw["d"], w), ("wd01", "wd2")):
                    sp.dma_start(part, w_dram[name][e]).then_inc(d_in[w], 16)

            def store(i, n):
                sp.wait_ge(v_y, done(R * i + n))
                sp.dma_start(result.rearrange("(t r) d -> t r d", r=P)[R * i + n], ye[:, n, :]).then_inc(y_out[n], 16)

            for n in range(R):
                sp.sem_inc(y_out[n], 16)
            load_x(0, 0)
            load(0, 0)
            for n in range(1, R):
                load_x(0, n)
            load(0, 1)
            with sp.Fori(0, NT // R - 1) as i:
                for w in range(2):
                    for n in (2 * w, 2 * w + 1):
                        sp.wait_ge(pe_x, done(R * i + n))
                        load_x(i + 1, n)
                    sp.wait_ge(v_gate, done(2 * i + w))
                    sp.wait_ge(g_u, done(2 * i + w))
                    sp.wait_ge(g_d, done(2 * i + w))
                    load(i + 1, w)
                    for n in (2 * w, 2 * w + 1):
                        store(i, n)
            for n in range(R):
                store(NT // R - 1, n)
            for n in range(R):
                sp.wait_ge(y_out[n], landed(NT // R))

        @block.scalar
        def _(act):
            head_start(act, act_x, act_g, act_h, act_gate, act_d)

            def take_x(i, n):
                act.wait_ge(pe_x, done(R * i + n))
                act.wait_ge(pe_u, done(R * i + n - 2))
                nc.scalar.copy(x_hi[:, n % 2], pX[:, :]).then_inc(act_x, 1)

            def take_h(i, n):
                act.wait_ge(pe_h, done(R * i + n))
                act.wait_ge(pe_o, done(R * i + n - 2))
                nc.scalar.copy(h_hi[:, n % 2, 0:2], pH[:, 0:2 * P])
                nc.scalar.copy(h_hi[0:rows[2], n % 2, 2], pH[0:rows[2], 2 * P:3 * P]).then_inc(act_h, 1)

            def split_gate(i, w):
                act.wait_ge(gate_in[w], landed(i))
                act.wait_ge(pe_g, done(R * i + 2 * w - 3))
                nc.scalar.copy(hi["g"][:, w], raw["g"][:, w]).then_inc(act_gate, 1)

            def split_d(i, w):
                act.wait_ge(d_in[w], 32 * (i + 1))
                act.wait_ge(pe_o, done(R * i + 2 * w - 3))
                first, second = zip(each_down(hi["d"], w), each_down(raw["d"], w))
                nc.scalar.copy(*first)
                nc.scalar.copy(*second).then_inc(act_d, 1)

            def slot(i, n, back=True, ahead=True):
                t = R * i + n
                if ahead:
                    take_x(*following(i, n, R))
                act.wait_ge(pe_g, done(t))
                act.wait_ge(v_h, done(t - 2))
                nc.scalar.activation(gate[:, n % 2], pG[n % 2][:, 0:F], ACT.Silu).then_inc(act_g, 1)
                if back:
                    take_h(*preceding(i, n, R))
                next_pair = (i, 1) if n < 2 else (i + 1, 0)
                if n < 2 or not (isinstance(i, int) and i == NT // R - 1):
                    (split_gate if n % 2 == 0 else split_d)(*next_pair)

            take_x(0, 0)
            split_gate(0, 0)
            split_d(0, 0)
            in_turns(act, slot, NT // R, R)
            take_h(NT // R - 1, R - 1)

        @block.gpsimd
        def _(pool):
            head_start(pool, g_u, g_d)

            def split_up(i, w):
                pool.wait_ge(v_up, done(2 * i + w))
                nc.gpsimd.tensor_tensor(lo["u"][:, w], raw["u"][:, w], hi["u"][:, w].bitcast(F32), ALU.subtract).then_inc(g_u, 1)

            def split_d(i, w):
                pool.wait_ge(act_d, done(2 * i + w))
                for n, (o, x, y) in enumerate(zip(*(each_down(t["d"], w) for t in (lo, raw, hi)))):
                    sub = nc.gpsimd.tensor_tensor(o, x, y.bitcast(F32), ALU.subtract)
                sub.then_inc(g_d, 1)

            with pool.Fori(0, NT // R) as i:
                for w in range(2):
                    split_up(i, w)
                    split_d(i, w)

        @block.vector
        def _(dve):
            head_start(dve, v_x, v_y, v_h, v_hl, v_gate, v_up)

            def take_x(i, n):
                dve.wait_ge(act_x, done(R * i + n))
                nc.vector.tensor_tensor(x_lo[:, n % 2], pX[:, :].rearrange("p (c t) -> p c t", c=C), x_hi[:, n % 2].bitcast(F32),
                                        ALU.subtract).then_inc(v_x, 1)

            def take_h(i, n):
                dve.wait_ge(act_h, done(R * i + n))
                nc.vector.tensor_tensor(h_lo[:, n % 2, 0:2], pH[:, 0:2 * P].rearrange("p (c t) -> p c t", c=2),
                                        h_hi[:, n % 2, 0:2].bitcast(F32), ALU.subtract)
                nc.vector.tensor_tensor(h_lo[0:rows[2], n % 2, 2], pH[0:rows[2], 2 * P:3 * P],
                                        h_hi[0:rows[2], n % 2, 2].bitcast(F32), ALU.subtract).then_inc(v_hl, 1)

            def take_y(i, n):
                dve.wait_ge(pe_o, done(R * i + n))
                dve.wait_ge(y_out[n], landed(i))
                nc.vector.tensor_copy(ye[:, n, :], pO[n % 2][:, :]).then_inc(v_y, 1)

            def split_gate(i, w):
                dve.wait_ge(act_gate, done(2 * i + w))
                nc.vector.tensor_tensor(lo["g"][:, w], raw["g"][:, w], hi["g"][:, w].bitcast(F32), ALU.subtract).then_inc(v_gate, 1)

            def split_up(i, w):
                dve.wait_ge(up_in[w], landed(i))
                dve.wait_ge(pe_u, done(R * i + 2 * w - 3))
                nc.vector.tensor_copy(hi["u"][:, w], raw["u"][:, w]).then_inc(v_up, 1)

            def slot(i, n, back=True, ahead=True):
                t = R * i + n
                if ahead:
                    take_x(*following(i, n, R))
                if n == 1 or n == 3 and not (isinstance(i, int) and i == NT // R - 1):
                    split_gate(*((i, 1) if n == 1 else (i + 1, 0)))
                if back:
                    take_h(*preceding(i, n, R))
                dve.wait_ge(act_g, done(t))
                dve.wait_ge(pe_u, done(t))
                nc.vector.tensor_tensor(h[:, n % 2], gate[:, n % 2], pU[n % 2][:, 0:F], ALU.mult).then_inc(v_h, 1)
                if n == 0 or n == 2 and not (isinstance(i, int) and i == NT // R - 1):
                    split_up(*((i, 1) if n == 0 else (i + 1, 0)))
                if back:
                    take_y(*preceding(i, n, R))

            take_x(0, 0)
            split_gate(0, 0)
            split_up(0, 0)
            in_turns(dve, slot, NT // R, R)
            take_h(NT // R - 1, R - 1)
            take_y(NT // R - 1, R - 1)

        @block.tensor
        def _(pe):
            head_start(pe, pe_x, pe_g, pe_u, pe_h, pe_o)

            def turn_x(i, n):
                pe.wait_ge(x_in[n], landed(i))
                pe.wait_ge(v_x, done(R * i + n - 1))
                for c in range(C):
                    last = nc.tensor.transpose(pX[:, P * c:P * c + P], xe[:, n, P * c:P * c + P], ident[:])
                last.then_inc(pe_x, 1)

            def turn_h(i, n):
                pe.wait_ge(v_h, done(R * i + n))
                pe.wait_ge(v_hl, done(R * i + n - 1))
                for f in range(FC):
                    last = nc.tensor.transpose(pH[0:rows[f], P * f:P * f + P], h[:, n % 2, P * f:P * f + rows[f]], ident[:])
                last.then_inc(pe_h, 1)

            def up(ps, k, n, sem):
                for c in range(C):
                    last = split_product(nc, ps[n % 2][:, 0:F], x_hi[:, n % 2, c, :], x_lo[:, n % 2, c, :],
                                         hi[k][:, n // 2, c, :], lo[k][:, n // 2, c, :], start=c == 0, stop=c == C - 1)
                last.then_inc(sem, 1)

            def down(i, n):
                t = R * i + n
                pe.wait_ge(v_hl, done(t))
                if n % 2 == 0:
                    pe.wait_ge(g_d, done(2 * i + n // 2))
                pe.wait_ge(v_y, done(t - 2))
                for f in range(FC):
                    r = rows[f]
                    last = split_product(nc, pO[n % 2][:, :], h_hi[0:r, n % 2, f, :], h_lo[0:r, n % 2, f, :],
                                         hi["d"][0:r, n // 2, f, :], lo["d"][0:r, n // 2, f, :], start=f == 0, stop=f == FC - 1)
                last.then_inc(pe_o, 1)

            def slot(i, n, back=True, ahead=True):
                t = R * i + n
                if ahead:
                    turn_x(*following(i, n, R))
                pe.wait_ge(v_x, done(t))
                if n % 2 == 0:
                    pe.wait_ge(v_gate, done(2 * i + n // 2))
                pe.wait_ge(act_g, done(t - 2))
                up(pG, "g", n, pe_g)
                if back:
                    turn_h(*preceding(i, n, R))
                pe.wait_ge(v_h, done(t - 2))
                if n % 2 == 0:
                    pe.wait_ge(g_u, done(2 * i + n // 2))
                up(pU, "u", n, pe_u)
                if back:
                    down(*preceding(i, n, R))

            turn_x(0, 0)
            in_turns(pe, slot, NT // R, R)
            turn_h(NT // R - 1, R - 1)
            down(NT // R - 1, R - 1)


def combine(nc, name, base, result, rows, weight, x_dst, K, shared=None):
    R = 4
    with ExitStack() as ctx:
        st = Stage(nc, ctx, name)
        got = st.sbuf("got", [P, R, K, D])
        acc = st.sbuf("acc", [P, R, D])
        yn = st.sbuf("yn", [P, R, D])
        stats = st.sbuf("stats", [P, R, 6])
        mv = st.sbuf("mv", [P, R, 2])
        rstd = st.sbuf("rstd", [P, R])
        mhalf = st.sbuf("mhalf", [P, 1])
        eps = st.sbuf("eps", [P, 1])
        still = st.sbuf("still", [P, 1])
        g_in, y_out = ([st.sem(f"{s}{n}") for n in range(R)] for s in ("g_in", "y_out"))
        g_c, g_ve, g_rs, v_k, v_acc, v_st, v_mv, v_yn = st.sems("g_c", "g_ve", "g_rs", "v_k", "v_acc", "v_st", "v_mv", "v_yn")
        if shared:
            part = shared(st)
        block = ctx.enter_context(nc.Block())

        if shared:
            @block.scalar
            def _(act):
                part.scalar(act)

            @block.tensor
            def _(pe):
                part.tensor(pe)

        @block.sync
        def _(sp):
            if shared:
                part.load(sp)
            for n in range(R):
                sp.sem_inc(y_out[n], 16)

            def store(i, n):
                sp.wait_ge(v_yn, done(R * i + n))
                sp.dma_start(x_dst[R * i + n], yn[:, n, :]).then_inc(y_out[n], 16)

            with sp.Fori(0, B // R - 1) as i:
                for n in range(R):
                    store(i, n)
            for n in range(R):
                store(B // R - 1, n)
            for n in range(R):
                sp.wait_ge(y_out[n], landed(B // R))

        @block.gpsimd
        def _(pool):
            head_start(pool, g_ve, g_rs)
            nc.gpsimd.memset(mhalf[:], -0.5).then_inc(g_c, 1)
            nc.gpsimd.memset(eps[:], EPS).then_inc(g_c, 1)
            pool.wait_ge(g_c, 2)

            def gather(b):
                n = b % R
                pool.wait_ge(v_acc, done(b - R))
                for k in range(K):
                    nc.gpsimd.indirect_dma_start(got[:, n, k, :], None, result,
                                                 bass.IndirectOffsetOnAxis(ap=rows[:, b, k:k + 1], axis=0)).then_inc(g_in[n], 16)

            def norm(b):
                n = b % R
                pool.wait_ge(v_mv, done(b))
                nc.gpsimd.tensor_tensor(rstd[:, n:n + 1], mv[:, n, 1:2], eps[:], ALU.add).then_inc(g_ve, 1)
                pool.wait_ge(g_ve, done(b))
                nc.gpsimd.tensor_tensor(rstd[:, n:n + 1], rstd[:, n:n + 1], mhalf[:], ALU.pow).then_inc(g_rs, 1)

            for b in range(R):
                gather(b)
            for b in range(B):
                norm(b)
                if b + R < B:
                    gather(b + R)

        @block.vector
        def _(dve):
            head_start(dve, v_k, v_acc, v_st, v_mv, v_yn)

            def tile(i, n):
                b = R * i + n
                dve.wait_ge(g_in[n], 16 * K * (i + 1))
                dve.wait_ge(v_yn, done(b - R))
                for k in range(K):
                    if k:
                        dve.wait_ge(v_k, done((K - 1) * b + k - 1))
                    prev = acc[:, n] if k else base[:, b]
                    ins = nc.vector.scalar_tensor_tensor(out=acc[:, n], in0=got[:, n, k, :], scalar=weight[:, b, k:k + 1], in1=prev,
                                                         op0=ALU.mult, op1=ALU.add)
                    ins.then_inc(v_k if k < K - 1 else v_acc, 1)
                dve.wait_ge(v_acc, done(b))
                nc.vector.bn_stats(stats[:, n], acc[:, n]).then_inc(v_st, 1)
                dve.wait_ge(v_st, done(b))
                carry_wait(nc.vector, still)
                nc.vector.bn_aggr(mv[:, n], stats[:, n]).then_inc(v_mv, 1)

            def normed(i, n):
                dve.wait_ge(g_rs, done(R * i + n))
                dve.wait_ge(y_out[n], landed(i))
                nc.vector.tensor_scalar(yn[:, n], acc[:, n], mv[:, n, 0:1], rstd[:, n:n + 1], ALU.subtract, ALU.mult).then_inc(v_yn, 1)

            if shared:
                head_start(dve, part.v_h, part.v_b)
                for b in range(B):
                    k = b // 2
                    if b % 2 == 0:
                        part.hidden(dve, k)
                        if k:
                            part.add(dve, k - 1)
                    if b == B - 1:
                        part.add(dve, k)
                    if b >= part.first:
                        dve.wait_ge(part.v_b, done(b - part.first))
                    tile(b // R, b % R)
                    if b:
                        normed((b - 1) // R, (b - 1) % R)
                normed(B // R - 1, R - 1)
                return

            tile(0, 0)
            with dve.Fori(0, B // R - 1) as i:
                for n in range(1, R):
                    tile(i, n)
                    normed(i, n - 1)
                tile(i + 1, 0)
                normed(i, R - 1)
            for n in range(1, R):
                tile(B // R - 1, n)
                normed(B // R - 1, n - 1)
            normed(B // R - 1, R - 1)


def logits_only(nc, name, psum, ident, xall, w_dram, logits, NE, prefetch=None):
    R = 4
    with ExitStack() as ctx:
        st = Stage(nc, ctx, name)
        pX, pT, pL = psum[0:2], psum[2:4], psum[4:6]
        xT = st.sbuf("xT", [P, 2, C, R * P])
        turned = st.sbuf("turned", [NE, 2, R * P])
        rw = st.sbuf("rw", [P, C, NE])
        w_in, pe_x, pe_t, pe_l, act_x, v_t, v_l = st.sems("w_in", "pe_x", "pe_t", "pe_l", "act_x", "v_t", "v_l")
        block = ctx.enter_context(nc.Block())

        @block.sync
        def _(sp):
            sp.dma_start(rw[:], w_dram["rw"]).then_inc(w_in, 16)
            if prefetch:
                prefetch(sp)

        @block.scalar
        def _(act):
            head_start(act, act_x)
            for b in range(B):
                act.wait_ge(pe_x, done(b))
                act.wait_ge(pe_t, done(b // R - 2))
                nc.scalar.copy(xT[:, b // R % 2, :, P * (b % R):P * (b % R) + P],
                               pX[b % 2][:, :].rearrange("p (c t) -> p c t", c=C)).then_inc(act_x, 1)

        @block.vector
        def _(dve):
            head_start(dve, v_t, v_l)

            def take_turned(q):
                dve.wait_ge(pe_t, done(q))
                dve.wait_ge(pe_l, done(q - 2))
                nc.vector.tensor_copy(turned[:, q % 2], pT[q % 2][0:NE, :]).then_inc(v_t, 1)

            def take_logits(q):
                dve.wait_ge(pe_l, done(q))
                nc.vector.tensor_copy(logits[:, R * q:R * q + R].rearrange("p b e -> p (b e)"), pL[q % 2][:, 0:R * NE]).then_inc(v_l, 1)

            for q in range(B // R):
                take_turned(q)
                if q:
                    take_logits(q - 1)
            take_logits(B // R - 1)

        @block.tensor
        def _(pe):
            head_start(pe, pe_x, pe_t, pe_l)

            def turn_x(q):
                for b in range(R * q, R * q + R):
                    pe.wait_ge(act_x, done(b - 2))
                    for c in range(C):
                        last = nc.tensor.transpose(pX[b % 2][:, P * c:P * c + P], xall[:, b, P * c:P * c + P], ident[:])
                    last.then_inc(pe_x, 1)

            def turn_back(q):
                pe.wait_ge(v_t, done(q))
                pe.wait_ge(v_l, done(q - 2))
                for n in range(R):
                    last = nc.tensor.transpose(pL[q % 2][:, NE * n:NE * n + NE], turned[:, q % 2, P * n:P * n + P], ident[0:NE, 0:NE])
                last.then_inc(pe_l, 1)

            turn_x(0)
            pe.wait_ge(w_in, 16)
            for q in range(B // R):
                if q < B // R - 1:
                    turn_x(q + 1)
                pe.wait_ge(act_x, done(R * q + R - 1))
                pe.wait_ge(v_t, done(q - 2))
                for c in range(C):
                    last = nc.tensor.matmul(pT[q % 2][0:NE, :], rw[:, c, :], xT[:, q % 2, c, :], start=c == 0, stop=c == C - 1)
                last.then_inc(pe_t, 1)
                if q:
                    turn_back(q - 1)
            turn_back(B // R - 1)


NP2 = (2 * B * P + 8 * (2 * P - 1)) // (2 * P)
NP2 += NP2 % 2


def decoder(nc, x, ctxT, c, out):
    def scratch(name, rows):
        return nc.dram_tensor(name, [rows, D], F32, kind="Internal").ap()

    x1, x2, x3 = (scratch(f"x{n}", B * P).rearrange("(b p) d -> b p d", p=P) for n in range(1, 4))
    packed1, result1 = scratch("packed1", 32 * 80), scratch("result1", 32 * 80 + 1)
    packed2, result2 = scratch("packed2", NP2 * 2 * P), scratch("result2", NP2 * 2 * P)

    def of(prefix):
        return {n[2:]: a for n, a in c.items() if n.startswith(prefix)}

    with ExitStack() as ctx:
        st = Stage(nc, ctx, "all")
        psum = [ctx.enter_context(nc.psum_tensor(f"bank{n}", [P, 512], F32)) for n in range(8)]
        ident, tri, ones = (st.sbuf(n, [P, P]) for n in ("ident", "tri", "ones"))
        zero = st.sbuf("zero", [P, D])
        c_in, packed_out, g_z = st.sems("c_in", "packed_out", "g_z")
        with nc.Block() as block:
            @block.sync
            def _(sp):
                sp.dma_start(ident[:], c["ident"]).then_inc(c_in, 16)
                sp.dma_start(tri[:], c["tri"]).then_inc(c_in, 16)
                sp.dma_start(ones[:], c["ones"]).then_inc(c_in, 16)
                sp.wait_ge(g_z, 1)
                sp.wait_ge(c_in, 48)

            @block.gpsimd
            def _(pool):
                nc.gpsimd.memset(zero[:], 0.0).then_inc(g_z, 1)

        def zero_rows(sp, v):
            for packed in (packed1, packed2):
                n = -(-packed.shape[0] // (2 * B * P))
                part = packed.rearrange("(v p n) d -> v p n d", v=2 * B, n=n)[v]
                r = part.shape[0]
                sp.dma_start(part, zero[0:r].unsqueeze(1).to_broadcast([r, n, D])).then_inc(packed_out, 16)

        zeroed_rows = [(packed_out, 2 * 2 * B * 16)]
        wide_attention(nc, "a", psum, ident, x, x1, of("a_"), rope=True, background=zero_rows)
        with ExitStack() as moe:
            sc = Stage(nc, moe, "moe1")
            xall = sc.sbuf("xall", [P, B, D])
            narrow_attention(nc, "b", psum, ident, lambda b: x1[b], None, {**of("b_"), "ctxT": ctxT}, 32,
                             EVENTS_8, rope=True, keep=xall)
            base, logits = sc.sbuf("base", [P, B, D]), sc.sbuf("logits", [P, B, 32])
            weight, rows = sc.sbuf("weight", [P, B, 4]), sc.sbuf("rows", [P, B, 4], U32)
            w = of("c_")

            def half(first):
                return lambda st: SharedExpert(nc, st, psum, ident, xall, w, base, first)

            with ExitStack() as routed:
                weights = CappedWeights(Stage(nc, routed, "cw"), w)
                logits_only(nc, "c", psum, ident, xall, w, logits, 32, weights.load_first)
                route(nc, "cr", psum, tri, ones, logits, w, 32, 4, weight, rows, None, True)
                dispatch(nc, "cd", xall, rows, packed1, 4, 32 * 80 - 1, zeroed_rows, half(0))
                capped_experts(nc, psum, ident, packed1.rearrange("(e r) d -> e r d", r=80), result1, zero, weights)
            combine(nc, "cc", base, result1, rows, weight, x2, 4, half(8))
        steps = [t.rearrange("l (j n) d -> j l n d", n=8) for t in (x2, x3)]
        narrow_attention(nc, "d", psum, ident, lambda b: steps[0][b], lambda b: steps[1][b], of("d_"), 16, EVENTS_4, causal=True)
        with ExitStack() as moe:
            sc = Stage(nc, moe, "moe2")
            xall = sc.sbuf("xall", [P, B, D])
            wide_attention(nc, "e", psum, ident, x3, None, {**of("e_"), "ctxT": ctxT}, rms=True, keep=xall)
            logits = sc.sbuf("logits", [P, B, 8])
            weight, rows = sc.sbuf("weight", [P, B, 2]), sc.sbuf("rows", [P, B, 2], U32)
            expert = sc.sbuf("expert", [P, NP2], I32)
            w = of("f_")
            logits_only(nc, "r", psum, ident, xall, w, logits, 8)
            route(nc, "fr", psum, tri, ones, logits, w, 8, 2, weight, rows, {"pairs": NP2, "expert": expert}, False)
            dispatch(nc, "fd", xall, rows, packed2, 2, NP2 * 2 * P - 1, [])
            routed_experts(nc, psum, ident, packed2.rearrange("(t r) d -> t r d", r=P), result2, expert, w, NP2)
            combine(nc, "fc", xall, result2, rows, weight, out, 2)


def rope_tables():
    inv = (np.float32(1.0) / np.power(np.float32(10000.0), np.arange(0, 128, 2, dtype=np.float32) / np.float32(128))).astype(np.float32)
    ang = np.outer(np.arange(P, dtype=np.float32), inv).astype(np.float32)
    c, s = np.cos(ang), np.sin(ang)
    cos, sin = np.concatenate([c, c], 1), np.concatenate([-s, s], 1)
    scale = np.float32(1.0 / np.sqrt(128.0))
    return {"cosq": cos * scale, "sinq": sin * scale, "cosk": cos, "sink": sin}


def causal_mask():
    i = np.arange(P)
    return np.where(i[None, :] <= i[:, None], 0.0, NEG).astype(np.float32)


def by_chunk(w):
    return np.ascontiguousarray(w.reshape(-1, P, w.shape[1]).transpose(1, 0, 2))


def pairs_apart(w, groups):
    r, c = w.shape
    return w.reshape(r, groups, -1, 2).transpose(0, 1, 3, 2).reshape(r, c)


def layout_l0_attn(i):
    flat = {n: i[f"L0_attn_W_{n}"].transpose(1, 0, 2).reshape(D, -1) for n in "QKV"}
    out = {
        "a_wq": by_chunk(pairs_apart(flat["Q"], 16)), "a_wk": by_chunk(pairs_apart(flat["K"], 16)),
        "a_wv": by_chunk(flat["V"]), "a_wo": np.ascontiguousarray(i["L0_attn_W_O"].transpose(1, 0, 2)),
        "a_bq": pairs_apart(i["L0_attn_b_Q"].reshape(1, -1), 16)[0], "a_bk": pairs_apart(i["L0_attn_b_K"].reshape(1, -1), 16)[0],
        "a_bv": i["L0_attn_b_V"].reshape(-1), "a_bo": i["L0_attn_b_O"], "a_mask": causal_mask(),
    }
    out.update({"a_" + n: t.astype(np.float32) for n, t in rope_tables().items()})
    return out


def layout_l1_xattn(i):
    return {
        "e_wq": by_chunk(i["L1_xattn_Wq"]), "e_wk": by_chunk(i["L1_xattn_Wk"]), "e_wv": by_chunk(i["L1_xattn_Wv"]),
        "e_wo": by_chunk(i["L1_xattn_Wo"]), "e_gq": i["L1_xattn_gq"], "e_gk": i["L1_xattn_gk"],
    }


def layout_shared(i):
    return {"x": i["x"], "ctxT": np.ascontiguousarray(i["ctx_1024"].reshape(B, P, 2, P).transpose(3, 0, 2, 1)),
            "ident": np.eye(P, dtype=np.float32)}


def layout_l0_xattn(i):
    wk, wv = i["L0_xattn_Wkv"][:, :D], i["L0_xattn_Wkv"][:, D:]
    freq = np.power(np.float32(10000.0), -np.arange(4, dtype=np.float32) / np.float32(4)).astype(np.float32)
    return {
        "b_wq": by_chunk(pairs_apart(i["L0_xattn_Wq"], 32)), "b_wk": by_chunk(pairs_apart(wk, 32)), "b_wv": by_chunk(wv),
        "b_wo": by_chunk(i["L0_xattn_Wout"]), "b_bo": i["L0_xattn_bout"],
        "b_pos": np.ascontiguousarray(i["fside_BxSx2_0"].transpose(1, 0, 2).reshape(P, 2 * B)),
        "b_freq": np.ascontiguousarray(np.broadcast_to(freq, (P, 4))),
    }


def layout_l1_attn(i):
    w = i["L1_attn_weight_qkv"]
    r = np.arange(P)
    seen = (r[None, :] % 8 == r[:, None] % 8) & (r[None, :] // 8 <= r[:, None] // 8)
    return {
        "d_wq": by_chunk(w[:D].T), "d_wk": by_chunk(w[D:2 * D].T), "d_wv": by_chunk(w[2 * D:].T),
        "d_wo": by_chunk(i["L1_attn_weight_out"].T), "d_mask": np.where(seen, 0.0, NEG).astype(np.float32),
    }


def layout_moe(i):
    def by_expert(w):
        return np.ascontiguousarray(w.reshape(w.shape[0], -1, P, w.shape[2]).transpose(0, 2, 1, 3))

    down = i["L1_ffn_down_proj"].transpose(0, 2, 1)
    iota = np.ascontiguousarray(np.broadcast_to(np.arange(P, dtype=np.float32), (P, P)))
    return {
        "c_rw": by_chunk(i["L0_ffn_router_w"].T), "c_sg": by_chunk(i["L0_ffn_shared_gate"].T),
        "c_su": by_chunk(i["L0_ffn_shared_up"].T), "c_sd": by_chunk(i["L0_ffn_shared_down"].T),
        "c_bias": i["L0_ffn_e_bias"], "c_iota": iota, "c_wg": by_expert(i["L0_ffn_W_gate"]), "c_wu": by_expert(i["L0_ffn_W_up"]),
        "c_wd": by_expert(i["L0_ffn_W_down"]),
        "f_rw": by_chunk(i["L1_ffn_gate_w"].T), "f_iota": iota, "f_wg": by_expert(i["L1_ffn_gate_proj"].transpose(0, 2, 1)),
        "f_wu": by_expert(i["L1_ffn_up_proj"].transpose(0, 2, 1)), "f_wd01": by_expert(down[:, :2 * P]),
        "f_wd2": np.ascontiguousarray(down[:, 2 * P:]),
        "tri": np.triu(np.ones((P, P), np.float32), 1), "ones": np.ones((P, P), np.float32),
    }


def kernel(**inputs):
    import concourse.bacc as bacc
    from concourse.bass_utils import run_bass_kernel_spmd

    i = {n: np.asarray(a) for n, a in inputs.items()}
    arrays = layout_shared(i)
    for part in (layout_l0_attn, layout_l0_xattn, layout_moe, layout_l1_attn, layout_l1_xattn):
        arrays.update(part(i))
    nc = bacc.Bacc("TRN2", target_bir_lowering=False, num_devices=1)
    arrays = {"in_" + n: np.ascontiguousarray(a) for n, a in arrays.items()}
    aps = {n[3:]: nc.dram_tensor(n, a.shape, mybir.dt.from_np(a.dtype), kind="ExternalInput").ap() for n, a in arrays.items()}
    out = nc.dram_tensor("out", (B, P, D), F32, kind="ExternalOutput").ap()
    decoder(nc, aps["x"], aps["ctxT"], aps, out)
    return run_bass_kernel_spmd(nc, [arrays], core_ids=[0]).results[0]["out"]
```
